# Optimizing a Trainium2 kernel written in Bass

```python
import numpy as np
import jax
import jax.numpy as jnp

def _softmax(x, axis=-1):
    return jax.nn.softmax(x, axis=axis)

def _gelu(x):
    return jax.nn.gelu(x, approximate=True)

def _silu(x):
    return jax.nn.silu(x)

def _sigmoid(x):
    return jax.nn.sigmoid(x)

def _layernorm(x, axis=-1, eps=1e-05):
    m = jnp.mean(x, axis=axis, keepdims=True)
    v = jnp.var(x, axis=axis, keepdims=True)
    return (x - m) / jnp.sqrt(v + eps)

def _scatter_add(tgt, idx, src, axis=0):
    return tgt.at[idx].add(src)

def _segment_sum(src, seg, n):
    return jax.ops.segment_sum(src, seg, n)
kernel_name = 'mk_xattn_ffn_d2_seqx_r2_98ad44'

def setup_inputs(seed: int=0):
    np.random.seed(seed)
    _w = jnp.asarray

    def _rec_inputs():
        import jax
        import jax.numpy as jnp
        _rk = jax.random.key(seed)
        x = -0.000125 + 0.9999 * jax.random.normal(jax.random.fold_in(_rk, 1), (4, 1024, 512), jnp.float32)
        _lenS = 1024 - jax.random.randint(jax.random.fold_in(_rk, 7), (4,), 0, max(1, 1024 // 4) + 1, jnp.int32)
        _lenS2 = 64 - jax.random.randint(jax.random.fold_in(_rk, 8), (4,), 0, max(1, 64 // 4) + 1, jnp.int32)
        _ctx_1024P = jax.random.normal(jax.random.fold_in(_rk, 11), (4, 16, 512), jnp.float32)
        _ctx_1024c = jax.random.dirichlet(jax.random.fold_in(_rk, 511), 0.3 * jnp.ones((16,), jnp.float32), (4, 64))
        _ctx_1024t = jnp.einsum('bsk,bkd->bsd', _ctx_1024c, _ctx_1024P)
        _ctx_1024t = _ctx_1024t * jax.lax.rsqrt(jnp.mean(jnp.square(_ctx_1024t)) + 1e-12) * 0.953939
        ctx_1024 = 4.13588e-05 + 0.999923 * (_ctx_1024t + 0.3 * jax.random.normal(jax.random.fold_in(_rk, 611), (4, 64, 512), jnp.float32))
        _validS = jnp.arange(1024)[None, :] < _lenS[:, None]
        _validS2 = jnp.arange(64)[None, :] < _lenS2[:, None]
        _causal = jnp.tril(jnp.ones((1024, 1024), dtype=bool))
        mask_BxS2_bf1 = jnp.ones((4, 64), dtype=bool)
        return (x, ctx_1024, mask_BxS2_bf1)
    x, ctx_1024, mask_BxS2_bf1 = _rec_inputs()

    def _L0_xattn_setup():
        import jax, jax.numpy as jnp
        import numpy as np
        key = jax.random.key(seed)
        k1, k2 = jax.random.split(key)
        hidden_states = jax.random.normal(k1, (8, 2048, 512), dtype=jnp.float32)
        visual_hidden_state = jax.random.normal(k2, (8, 512, 512), dtype=jnp.float32)
        return {'hidden_states': hidden_states, 'visual_hidden_state': visual_hidden_state}
    _L0_xattn_all = _L0_xattn_setup()
    _L0_xattn_in = {k: v for k, v in _L0_xattn_all.items() if k in ()}
    del _L0_xattn_all

    def _L0_ffn_setup():
        import jax, jax.numpy as jnp
        import numpy as np
        INT8_MAX = 127.0

        def _absmax_scale(x, axes):
            amax = jnp.max(jnp.abs(x), axis=axes, keepdims=True)
            return jnp.maximum(amax, 1e-12) / INT8_MAX
        key = jax.random.key(seed)
        k1, k2 = jax.random.split(key)
        lhs = jax.random.normal(k1, (4, 4096, 512), dtype=jnp.float32)
        rhs = jax.random.normal(k2, (512, 512), dtype=jnp.float32)
        return {'lhs': lhs, 'rhs': rhs}
    _L0_ffn_all = _L0_ffn_setup()
    _L0_ffn_in = {k: v for k, v in _L0_ffn_all.items() if k in ('rhs',)}
    del _L0_ffn_all

    def _L1_xattn_setup():
        import jax, jax.numpy as jnp
        import numpy as np
        B, T, S, DM, H, D, TOPK = (4, 256, 1024, 512, 16, 64, 32)
        INNER = H * D
        key = jax.random.key(seed)
        ks = jax.random.split(key, 7)
        x = jax.random.normal(ks[0], (B, T, DM), dtype=jnp.float32)
        mem_keys = jax.random.normal(ks[1], (B, S, DM), dtype=jnp.float32)
        mem_values = jax.random.normal(ks[2], (B, S, DM), dtype=jnp.float32)
        mem_mask = jnp.ones((B, S), dtype=bool)
        sc = 0.02
        Wq = sc * jax.random.normal(ks[3], (DM, INNER), dtype=jnp.float32)
        Wk = sc * jax.random.normal(ks[4], (DM, INNER), dtype=jnp.float32)
        Wv = sc * jax.random.normal(ks[5], (DM, INNER), dtype=jnp.float32)
        Wo = sc * jax.random.normal(ks[6], (INNER, DM), dtype=jnp.float32)
        inv_temp = jnp.ones((H,), dtype=jnp.float32)
        return {'x': x, 'mem_keys': mem_keys, 'mem_values': mem_values, 'mem_mask': mem_mask, 'Wq': Wq, 'Wk': Wk, 'Wv': Wv, 'Wo': Wo, 'inv_temp': inv_temp}
    _L1_xattn_all = _L1_xattn_setup()
    _L1_xattn_in = {k: v for k, v in _L1_xattn_all.items() if k in ('Wq', 'Wk', 'Wv', 'Wo', 'inv_temp')}
    del _L1_xattn_all

    def _L1_ffn_setup():
        import jax, jax.numpy as jnp
        import numpy as np

        def _moe_layer(x, rw, rb, ew, eb):
            logits = jnp.einsum('bsh,eh->bse', x, rw) + rb
            probs = jax.nn.softmax(logits, axis=-1)
            _, topk_idx = jax.lax.top_k(probs, 2)
            out = jnp.zeros_like(x)
            num_experts = rw.shape[0]
            for e in range(num_experts):
                mask = (topk_idx == e).any(axis=-1)
                expert_out = jnp.einsum('bsh,dh->bsd', x, ew[e]) + eb[e]
                out = out + jnp.where(mask[..., None], expert_out, 0.0)
            return out
        key = jax.random.key(seed)
        ks = jax.random.split(key, 4)
        L, E, H = (2, 8, 512)
        B, S = (4, 2048)
        return {'hidden_states': jax.random.normal(ks[0], (B, S, H), dtype=jnp.float32), 'router_w': jax.random.normal(ks[1], (L, E, H), dtype=jnp.float32) * (1.0 / np.sqrt(H)), 'router_b': jnp.zeros((L, E), dtype=jnp.float32), 'expert_w': jax.random.normal(ks[2], (L, E, H, H), dtype=jnp.float32) * (1.0 / np.sqrt(H)), 'expert_b': jnp.zeros((L, E, H), dtype=jnp.float32)}
    _L1_ffn_all = _L1_ffn_setup()
    _L1_ffn_in = {k: v for k, v in _L1_ffn_all.items() if k in ('router_w', 'router_b', 'expert_w', 'expert_b')}
    del _L1_ffn_all
    return {'x': x, 'ctx_1024': ctx_1024, 'mask_BxS2_bf1': mask_BxS2_bf1, 'L0_ffn_rhs': _L0_ffn_in['rhs'], 'L1_xattn_Wq': _L1_xattn_in['Wq'], 'L1_xattn_Wk': _L1_xattn_in['Wk'], 'L1_xattn_Wv': _L1_xattn_in['Wv'], 'L1_xattn_Wo': _L1_xattn_in['Wo'], 'L1_xattn_inv_temp': _L1_xattn_in['inv_temp'], 'L1_ffn_router_w': _L1_ffn_in['router_w'], 'L1_ffn_router_b': _L1_ffn_in['router_b'], 'L1_ffn_expert_w': _L1_ffn_in['expert_w'], 'L1_ffn_expert_b': _L1_ffn_in['expert_b']}

def reference(x, ctx_1024, mask_BxS2_bf1, L0_ffn_rhs, L1_xattn_Wq, L1_xattn_Wk, L1_xattn_Wv, L1_xattn_Wo, L1_xattn_inv_temp, L1_ffn_router_w, L1_ffn_router_b, L1_ffn_expert_w, L1_ffn_expert_b):
    import jax
    import jax.numpy as jnp

    def _L0_xattn_ref(hidden_states, visual_hidden_state):
        import jax, jax.numpy as jnp
        import numpy as np
        fusion_scores = jnp.einsum('bsd,bvd->bsv', hidden_states, visual_hidden_state)
        fusion_probs = jax.nn.softmax(fusion_scores, axis=-1)
        fusion_output = jnp.einsum('bsv,bvd->bsd', fusion_probs, visual_hidden_state)
        return fusion_output

    def _L0_ffn_ref(lhs, rhs):
        import jax, jax.numpy as jnp
        import numpy as np
        INT8_MAX = 127.0

        def _absmax_scale(x, axes):
            amax = jnp.max(jnp.abs(x), axis=axes, keepdims=True)
            return jnp.maximum(amax, 1e-12) / INT8_MAX
        lhs_scale = _absmax_scale(lhs, (2,))
        rhs_scale = _absmax_scale(rhs, (0,))
        q_lhs = jnp.clip(jnp.round(lhs / lhs_scale), -INT8_MAX, INT8_MAX).astype(jnp.int8)
        q_rhs = jnp.clip(jnp.round(rhs / rhs_scale), -INT8_MAX, INT8_MAX).astype(jnp.int8)
        acc = jax.lax.dot_general(q_lhs, q_rhs, (((2,), (0,)), ((), ())), preferred_element_type=jnp.int32)
        return acc.astype(jnp.float32) * lhs_scale * rhs_scale

    def _L1_xattn_ref(x, mem_keys, mem_values, mem_mask, Wq, Wk, Wv, Wo, inv_temp):
        import jax, jax.numpy as jnp
        import numpy as np
        B, T, S, DM, H, D, TOPK = (4, 256, 1024, 512, 16, 64, 32)
        INNER = H * D
        b, t, _ = x.shape
        s = mem_keys.shape[1]
        q = (x @ Wq).reshape(b, t, H, D).transpose(0, 2, 1, 3)
        k = (mem_keys @ Wk).reshape(b, s, H, D).transpose(0, 2, 1, 3)
        v = (mem_values @ Wv).reshape(b, s, H, D).transpose(0, 2, 1, 3)
        q = q * inv_temp.reshape(1, H, 1, 1)
        scores = jnp.einsum('bhtd,bhsd->bhts', q, k) / jnp.asarray(np.sqrt(D), x.dtype)
        scores = jnp.where(mem_mask[:, None, None, :], scores, -jnp.inf)
        full_attn = jax.nn.softmax(scores, axis=-1)
        topk_vals = jax.lax.top_k(scores, TOPK)[0]
        threshold = topk_vals[..., -1:]
        topk_mask = (scores >= threshold).astype(scores.dtype)
        sparse_attn = full_attn * topk_mask
        sparse_attn = sparse_attn / (jnp.sum(sparse_attn, axis=-1, keepdims=True) + 1e-08)
        attn = full_attn + jax.lax.stop_gradient(sparse_attn - full_attn)
        out = jnp.einsum('bhts,bhsd->bhtd', attn, v)
        out = out.transpose(0, 2, 1, 3).reshape(b, t, INNER)
        return out @ Wo

    def _L1_ffn_ref(hidden_states, router_w, router_b, expert_w, expert_b):
        import jax, jax.numpy as jnp
        import numpy as np

        def _moe_layer(x, rw, rb, ew, eb):
            logits = jnp.einsum('bsh,eh->bse', x, rw) + rb
            probs = jax.nn.softmax(logits, axis=-1)
            _, topk_idx = jax.lax.top_k(probs, 2)
            out = jnp.zeros_like(x)
            num_experts = rw.shape[0]
            for e in range(num_experts):
                mask = (topk_idx == e).any(axis=-1)
                expert_out = jnp.einsum('bsh,dh->bsd', x, ew[e]) + eb[e]
                out = out + jnp.where(mask[..., None], expert_out, 0.0)
            return out
        x = hidden_states
        num_layers = router_w.shape[0]
        for l in range(num_layers):
            x = _moe_layer(x, router_w[l], router_b[l], expert_w[l], expert_b[l])
        return x
    x = x + _L0_xattn_ref(_layernorm(x, axis=-1), ctx_1024)
    x = x + _L0_ffn_ref(_layernorm(x, axis=-1), L0_ffn_rhs)
    x = x + _L1_xattn_ref(_layernorm(x, axis=-1), ctx_1024, ctx_1024, mask_BxS2_bf1, L1_xattn_Wq, L1_xattn_Wk, L1_xattn_Wv, L1_xattn_Wo, L1_xattn_inv_temp)
    x = x + _L1_ffn_ref(_layernorm(x, axis=-1), L1_ffn_router_w, L1_ffn_router_b, L1_ffn_expert_w, L1_ffn_expert_b)
    return x

_drawn_inputs = setup_inputs


def setup_inputs(seed=0):
    import zlib

    import numpy as np

    out = dict(_drawn_inputs(seed))
    spreads = {'L1_xattn_inv_temp': (1.0, 0.6),
     'L1_ffn_router_b': (0.0, 0.1),
     'L1_ffn_expert_b': (0.0, 0.1)}
    factors = {'L1_xattn_Wq': 8.0, 'L1_xattn_Wk': 7.014, 'L1_xattn_Wv': 4.108, 'L1_xattn_Wo': 4.275}
    for name, (base, spread) in spreads.items():
        noise = np.random.default_rng([zlib.crc32(name.encode()), seed]).standard_normal(out[name].shape)
        drawn = base * np.exp(spread * noise) if base else spread * noise
        out[name] = jnp.asarray(drawn.astype(out[name].dtype))
    for name, factor in factors.items():
        out[name] = (out[name] * factor).astype(out[name].dtype)
    return out
```

```python
import concourse.bass as bass
from concourse import mybir
from contextlib import ExitStack

P = 128
BATCH, SEQ, D = 4, 1024, 512
KV = 64
HEADS, DH = 16, 64
TOPK = 32
EXPERTS, LAYERS, CHOICES = 8, 2, 2
TOKENS = BATCH * SEQ
TILES = TOKENS // P
TPB = SEQ // P
DC = D // P
PAIRS = HEADS // 2
G = 2
GROUPS = TILES // G
GPB = GROUPS // BATCH
SPARE = EXPERTS * TILES
SLOTS = (CHOICES * TOKENS + EXPERTS * (P - 1)) // P
SPARES = SLOTS - CHOICES * TILES
LN_EPS = 1e-5
NORM_EPS = 1e-8
INT8_MAX = 127.0
ROUND = 1.5 * 2.0 ** 23
MASKED = -3.0e38
TAKEN = -3.4e38

fp32 = mybir.dt.float32
bf16 = mybir.dt.bfloat16
u8 = mybir.dt.uint8
i32 = mybir.dt.int32
u32 = mybir.dt.uint32
ALU = mybir.AluOpType
ACT = mybir.ActivationFunctionType
AX = mybir.AxisListType


HELD = {}


def wait_for(eng, sem, count):
    eng.wait_ge(sem, count)
    if not isinstance(count, int):
        eng.sem_inc(HELD["waited"], 1)


def free_slot(eng, released, t, depth, per=1):
    if not isinstance(t, int) or t >= depth:
        wait_for(eng, released, (t - depth + 1) * per)


def pipeline(eng, count, stages, slots=2):
    first = min(lag for lag, _ in stages)
    last = max(lag for lag, _ in stages) + count
    cuts = {first, last}
    for lag, _ in stages:
        cuts |= {lag, lag + slots, lag + count}
    cuts = sorted(cuts)

    def window(w, place, live):
        for lag, stage in live:
            stage(w - lag, (place - lag) % slots)

    for a, b in zip(cuts, cuts[1:]):
        live = [(lag, stage) for lag, stage in stages if lag <= a < lag + count]
        looped = (b - a) // slots * slots if all(a - lag >= slots for lag, _ in live) else 0
        if looped >= 2 * slots:
            with eng.Fori(0, looped // slots) as body:
                for n in range(slots):
                    window(body * slots + (a + n), a + n, live)
            a += looped
        for w in range(a, b):
            window(w, w, live)


def build(nc, x, ctxT, ctx, mask, rhs, WqT, Wk, Wv, Wo, inv_temp, rwT, rb, ewT, eb, out):
    top = ExitStack()
    with top:
        def scope(recycle=False):
            stack = ExitStack()
            used = []

            def clear():
                nc.clear_and_free_semaphores(used)
                nc.all_engine_barrier()

            if recycle:
                stack.callback(clear)

            def sb(name, shape, dt=fp32):
                return stack.enter_context(nc.sbuf_tensor(name, shape, dt))

            def ps(name, shape, dt=fp32):
                return stack.enter_context(nc.psum_tensor(name, shape, dt))

            def sem(name):
                if not recycle:
                    return stack.enter_context(nc.semaphore(name))
                used.append(nc.alloc_semaphore(name))
                return used[-1]
            return stack, sb, ps, sem

        keep, sb, ps, sem = scope()
        top.enter_context(keep)
        X = sb("X", [P, TILES, D])
        ident = sb("ident", [P, P])
        identb = sb("identb", [P, P], bf16)
        KT = sb("KT", [P, PAIRS, BATCH * KV])
        VT = sb("VT", [P, PAIRS, BATCH * KV])
        mhalf = sb("mhalf", [P, G])
        maskrow = sb("maskrow", [1, BATCH, HEADS // 2, KV], bf16)
        onesrow = sb("onesrow", [1, P], bf16)

        HELD["waited"] = sem("waited")
        hidden = nc.dram_tensor("hidden", (TOKENS, D), fp32, kind="Internal").ap()
        listed = nc.dram_tensor("listed", (SPARE * P, 1), fp32, kind="Internal").ap()
        made = nc.dram_tensor("made", (SLOTS * P, D), fp32, kind="Internal").ap()
        constants(nc, scope, ident, identb, mhalf, onesrow, maskrow, mask)
        kv_prep(nc, scope, KT, VT, ctxT, Wk, Wv, inv_temp)
        phase_a(nc, scope, X, x, ctxT, ctx, ident, mhalf)
        phase_b(nc, scope, X, rhs, identb, mhalf)
        phase_c(nc, scope, X, KT, VT, WqT, Wo, ident, mhalf, maskrow, onesrow)
        routing, rsb, _, _ = scope()
        with routing:
            R = Routing(rsb)
            W = rsb("expert_W", [P, EXPERTS, DC, D])
            for layer in range(LAYERS):
                route(nc, scope, R, layer, X, W, ident, mhalf, rwT, rb, ewT, hidden, listed, made)
                experts(nc, scope, R, layer, W, ident, eb, hidden, listed, made)
            combine(nc, scope, R, X, made, out)


def constants(nc, scope, ident, identb, mhalf, onesrow, maskrow, mask):
    stack, sb, ps, sem = scope()
    with stack:
        m8 = sb("m8", [1, BATCH, KV], u8)
        zeroed = sem("const_zeroed")
        made = sem("const_made")
        mask_in = sem("mask_in")
        block = stack.enter_context(nc.Block())

        @block.sync
        def _(sp):
            sp.dma_start(m8[0:1, :, :], mask.rearrange("(o b) s -> o b s", o=1)).then_inc(mask_in, 16)
            sp.wait_ge(mask_in, 16)

        @block.gpsimd
        def _(pool):
            pool.memset(ident[:, :], 0.0).then_inc(zeroed, 1)
            pool.memset(identb[:, :], 0.0).then_inc(zeroed, 1)
            pool.memset(mhalf[:, :], -0.5)
            pool.memset(onesrow[:, :], 1.0)
            pool.wait_ge(zeroed, 2)
            for m in (ident, identb):
                pool.affine_select(out=m[:, :], in_=m[:, :], compare_op=ALU.not_equal, fill=1.0, base=0,
                                   pattern=[[-1, P]], channel_multiplier=1).then_inc(made, 1)

        @block.vector
        def _(dve):
            dve.wait_ge(mask_in, 16)
            for n in range(HEADS // 2):
                dve.tensor_scalar(maskrow[0:1, :, n, :], m8[0:1, :, :], 1.0, -MASKED, ALU.subtract, ALU.mult)


def kv_prep(nc, scope, KT, VT, ctxT, Wk, Wv, inv_temp):
    stack, sb, ps, sem = scope()
    with stack:
        cT = sb("cT", [P, DC, BATCH * KV])
        wk = sb("wk", [P, DC, HEADS * DH])
        wv = sb("wv", [P, DC, HEADS * DH])
        it = sb("it", [P, PAIRS])
        it8 = sb("it8", [P, PAIRS])
        pk = ps("pk", [P, 2, 512])
        pv = ps("pv", [P, 2, 512])
        c_in = sem("c_in")
        wk_in = sem("wk_in")
        wv_in = sem("wv_in")
        it_in = sem("it_in")
        it_done = sem("it_done")
        k_mm = sem("k_mm")
        v_mm = sem("v_mm")
        k_out = sem("k_out")
        v_out = sem("v_out")
        block = stack.enter_context(nc.Block())

        @block.sync
        def _(sp):
            sp.dma_start(cT[:, :, :], ctxT.rearrange("(k p) n -> p k n", p=P)).then_inc(c_in, 16)
            sp.dma_start(wk[:, :, :], Wk.rearrange("(k p) n -> p k n", p=P)).then_inc(wk_in, 16)
            sp.dma_start(wv[:, :, :], Wv.rearrange("(k p) n -> p k n", p=P)).then_inc(wv_in, 16)
            sp.dma_start(it[:, :], inv_temp).then_inc(it_in, 16)

        @block.tensor
        def _(pe):
            pe.wait_ge(c_in, 16)
            pe.wait_ge(wk_in, 16)
            pe.wait_ge(wv_in, 16)
            for p in range(PAIRS):
                for w, acc, done, released in ((wk, pk, k_mm, k_out), (wv, pv, v_mm, v_out)):
                    free_slot(pe, released, p, 2)
                    for k in range(DC):
                        mm = pe.matmul(acc[:, p % 2, 0:BATCH * KV], w[:, k, p * P:(p + 1) * P], cT[:, k, :],
                                       start=(k == 0), stop=(k == DC - 1))
                    mm.then_inc(done, 1)

        @block.scalar
        def _(act):
            act.wait_ge(it_done, 1)
            for p in range(PAIRS):
                act.wait_ge(k_mm, p + 1)
                act.activation(KT[:, p, :], pk[:, p % 2, 0:BATCH * KV], ACT.Identity,
                               scale=it8[:, p:p + 1]).then_inc(k_out, 1)

        @block.vector
        def _(dve):
            dve.wait_ge(it_in, 16)
            dve.tensor_scalar(it8[:, :], it[:, :], DH ** -0.5, None, ALU.mult).then_inc(it_done, 1)
            for p in range(PAIRS):
                dve.wait_ge(v_mm, p + 1)
                dve.tensor_copy(VT[:, p, :], pv[:, p % 2, 0:BATCH * KV]).then_inc(v_out, 1)


def rstd_steps(pool, rstd, nmr, mv, mhalf, chain, base, done):
    pool.tensor_scalar(rstd, mv[:, :, 1], LN_EPS, None, ALU.add).then_inc(chain, 1)
    pool.tensor_scalar(nmr, mv[:, :, 0], -1.0, None, ALU.mult).then_inc(chain, 1)
    wait_for(pool, chain, base + 2)
    pool.tensor_tensor(rstd, rstd, mhalf, ALU.pow).then_inc(chain, 1)
    wait_for(pool, chain, base + 3)
    pool.tensor_tensor(nmr, nmr, rstd, ALU.mult).then_inc(done, 1)


def phase_a(nc, scope, X, x, ctxT, ctx, ident, mhalf):
    stack, sb, ps, sem = scope()
    with stack:
        cT = sb("a_cT", [P, DC, BATCH * KV])
        cn = sb("a_cn", [KV, BATCH, D])
        bn = sb("a_bn", [P, 2, G, 6])
        mv = sb("a_mv", [P, 2, G, 2])
        rstd = sb("a_rstd", [P, 2, G])
        nmr = sb("a_nmr", [P, 2, G])
        y = sb("a_y", [P, 2, G, D])
        yT = sb("a_yT", [P, 2, G, DC, P])
        nmax = sb("a_nmax", [P, 2, G])
        probs = sb("a_probs", [P, 2, G, KV])
        Z = sb("a_Z", [P, 2, G])
        rZ = sb("a_rZ", [P, 2, G])
        pT = sb("a_pT", [KV, 2, G, P])
        psT = ps("a_psT", [P, G, DC, P])
        psS = ps("a_psS", [P, 512])
        psP = ps("a_psP", [P, 512])
        psO = ps("a_psO", [P, G, D])
        c_in = sem("a_c_in")
        x_in = sem("a_x_in")
        bn_done = sem("a_bn_done")
        mv_done = sem("a_mv_done")
        chain = sem("a_chain")
        rstd_done = sem("a_rstd_done")
        y_done = sem("a_y_done")
        yT_mm = sem("a_yT_mm")
        yT_done = sem("a_yT_done")
        s_mm = sem("a_s_mm")
        nmax_done = sem("a_nmax_done")
        p_done = sem("a_p_done")
        pT_mm = sem("a_pT_mm")
        pT_done = sem("a_pT_done")
        rZ_done = sem("a_rZ_done")
        o_mm = sem("a_o_mm")
        x_done = sem("a_x_done")
        block = stack.enter_context(nc.Block())
        xv = x.rearrange("(t p) d -> p t d", p=P)
        S = psS[:, 0:G * KV].rearrange("p (g s) -> p g s", g=G)
        PT = psP[0:KV, 0:G * P].rearrange("p (g s) -> p g s", g=G)

        @block.sync
        def _(sp):
            sp.dma_start(cT[:, :, :], ctxT.rearrange("(k p) n -> p k n", p=P)).then_inc(c_in, 16)
            sp.dma_start(cn[:, :, :], ctx.rearrange("(b s) d -> s b d", b=BATCH)).then_inc(c_in, 16)
            with sp.Fori(0, GROUPS) as i:
                sp.dma_start(X[:, bass.ds(i * G, G), :], xv[:, bass.ds(i * G, G), :]).then_inc(x_in, 16)
                wait_for(sp, x_in, (i + 1) * 16)

        @block.vector
        def _(dve):
            def stats(i, s):
                wait_for(dve, x_in, (i + 1) * 16)
                free_slot(dve, rstd_done, i, 2)
                for g in range(G):
                    last = dve.bn_stats(bn[:, s, g, :], X[:, i * G + g, :])
                last.then_inc(bn_done, 1)
                wait_for(dve, bn_done, i + 1)
                for g in range(G):
                    last = dve.bn_aggr(mv[:, s, g, :], bn[:, s, g, :])
                last.then_inc(mv_done, 1)

            def row_max(i, s):
                wait_for(dve, s_mm, i + 1)
                free_slot(dve, p_done, i, 2)
                dve.tensor_reduce(nmax[:, s, :], S, AX.X, ALU.max, negate=True).then_inc(nmax_done, 1)

            def inverse(i, s):
                wait_for(dve, p_done, i + 1)
                free_slot(dve, x_done, i, 2)
                dve.reciprocal(rZ[:, s, :], Z[:, s, :]).then_inc(rZ_done, 1)

            def residual(i, s):
                wait_for(dve, o_mm, i + 1)
                wait_for(dve, rZ_done, i + 1)
                for g in range(G):
                    xt = X[:, i * G + g, :]
                    last = dve.scalar_tensor_tensor(xt, psO[:, g, :], rZ[:, s, g:g + 1], xt, ALU.mult, ALU.add)
                last.then_inc(x_done, 1)

            pipeline(dve, GROUPS, [(0, stats), (2, row_max), (2, inverse), (3, residual)])

        @block.gpsimd
        def _(pool):
            def rstds(i, s):
                wait_for(pool, mv_done, i + 1)
                free_slot(pool, y_done, i, 2)
                rstd_steps(pool, rstd[:, s, :], nmr[:, s, :], mv[:, s, :, :], mhalf[:, 0:G],
                           chain, i * 3, rstd_done)

            pipeline(pool, GROUPS, [(0, rstds)])

        @block.scalar
        def _(act):
            def norm(i, s):
                wait_for(act, rstd_done, i + 1)
                free_slot(act, yT_mm, i, 2)
                for g in range(G):
                    last = act.activation(y[:, s, g, :], X[:, i * G + g, :], ACT.Identity,
                                          bias=nmr[:, s, g:g + 1], scale=rstd[:, s, g:g + 1])
                last.then_inc(y_done, 1)

            def copy_yT(i, s):
                wait_for(act, yT_mm, i + 1)
                free_slot(act, s_mm, i, 2)
                act.activation(yT[:, s, :, :, :], psT[:, :, :, :], ACT.Copy).then_inc(yT_done, 1)

            def exps(i, s):
                wait_for(act, nmax_done, i + 1)
                free_slot(act, pT_mm, i, 2)
                free_slot(act, rZ_done, i, 2)
                for g in range(G):
                    last = act.activation(probs[:, s, g, :], S[:, g, :], ACT.Exp, bias=nmax[:, s, g:g + 1],
                                          accum_out=Z[:, s, g:g + 1])
                last.then_inc(p_done, 1)

            def copy_pT(i, s):
                wait_for(act, pT_mm, i + 1)
                free_slot(act, o_mm, i, 2)
                act.activation(pT[:, s, :, :], PT, ACT.Copy).then_inc(pT_done, 1)

            pipeline(act, GROUPS, [(0, norm), (1, copy_yT), (2, exps), (2, copy_pT)])

        @block.tensor
        def _(pe):
            pe.wait_ge(c_in, 32)

            def transpose_y(i, s):
                wait_for(pe, y_done, i + 1)
                free_slot(pe, yT_done, i, 1)
                for g in range(G):
                    for k in range(DC):
                        mm = pe.transpose(psT[:, g, k, :], y[:, s, g, k * P:(k + 1) * P], ident[:, :])
                mm.then_inc(yT_mm, 1)

            def scores(i, s):
                wait_for(pe, yT_done, i + 1)
                free_slot(pe, p_done, i, 1)
                for g in range(G):
                    for k in range(DC):
                        mm = pe.matmul(S[:, g, :], yT[:, s, g, k, :],
                                       cT[:, k, bass.ds((i // GPB) * KV, KV)], start=(k == 0), stop=(k == DC - 1))
                mm.then_inc(s_mm, 1)

            def transpose_p(i, s):
                wait_for(pe, p_done, i + 1)
                free_slot(pe, pT_done, i, 1)
                for g in range(G):
                    mm = pe.transpose(PT[:, g, :], probs[:, s, g, :], ident[:, :])
                mm.then_inc(pT_mm, 1)

            def values(i, s):
                wait_for(pe, pT_done, i + 1)
                free_slot(pe, x_done, i, 1)
                for g in range(G):
                    mm = pe.matmul(psO[:, g, :], pT[:, s, g, :], cn[:, i // GPB, :], start=True, stop=True)
                mm.then_inc(o_mm, 1)

            pipeline(pe, GROUPS, [(0, transpose_y), (1, scores), (2, transpose_p), (2, values)])


def phase_b(nc, scope, X, rhs, identb, mhalf):
    stack, sb, ps, sem = scope()
    with stack:
        w = sb("b_w", [P, DC, D])
        wabs = sb("b_wabs", [P, DC, D])
        wmax = sb("b_wmax", [P, D])
        wscale = sb("b_wscale", [P, D])
        winv = sb("b_winv", [P, D])
        wq = sb("b_wq", [P, DC, D], bf16)
        bn = sb("b_bn", [P, 2, G, 6])
        mv = sb("b_mv", [P, 2, G, 2])
        rstd = sb("b_rstd", [P, 2, G])
        nmr = sb("b_nmr", [P, 2, G])
        y = sb("b_y", [P, 2, G, D])
        amax = sb("b_amax", [P, 2, G])
        scale = sb("b_scale", [P, 4, G])
        inv = sb("b_inv", [P, 2, G])
        q = sb("b_q", [P, 2, G, D], bf16)
        qT = sb("b_qT", [P, 2, G, DC, P], bf16)
        delta = sb("b_delta", [P, 2, G, D])
        minus_round = sb("b_minus_round", [P, 1])
        psT = ps("b_psT", [P, 2, G, DC, P], bf16)
        psO = ps("b_psO", [P, 2, G, D])
        w_in = sem("b_w_in")
        w_chain = sem("b_w_chain")
        wmax_done = sem("b_wmax_done")
        wq_done = sem("b_wq_done")
        bn_done = sem("b_bn_done")
        mv_done = sem("b_mv_done")
        chain = sem("b_chain")
        rstd_done = sem("b_rstd_done")
        y_done = sem("b_y_done")
        amax_done = sem("b_amax_done")
        sc_chain = sem("b_sc_chain")
        v_done = sem("b_v_done")
        q_done = sem("b_q_done")
        qT_mm = sem("b_qT_mm")
        qT_done = sem("b_qT_done")
        o_mm = sem("b_o_mm")
        d_done = sem("b_d_done")
        x_done = sem("b_x_done")
        block = stack.enter_context(nc.Block())

        @block.sync
        def _(sp):
            sp.dma_start(w[:, :, :], rhs.rearrange("(k p) n -> p k n", p=P)).then_inc(w_in, 16)

        @block.vector
        def _(dve):
            dve.memset(minus_round[:, :], -ROUND).then_inc(w_chain, 1)
            dve.wait_ge(w_in, 16)
            dve.tensor_reduce(wabs[:, 0, :], w[:, :, :].rearrange("p k n -> p n k"), AX.X, ALU.max,
                              apply_absolute_value=True).then_inc(w_chain, 1)
            dve.wait_ge(wmax_done, 1)
            dve.tensor_scalar(wscale[:, :], wmax[:, :], 1e-12, 1.0 / INT8_MAX, ALU.max, ALU.mult).then_inc(w_chain, 1)
            dve.wait_ge(w_chain, 3)
            dve.reciprocal(winv[:, :], wscale[:, :]).then_inc(w_chain, 1)
            dve.wait_ge(w_chain, 4)
            for k in range(DC):
                dve.tensor_tensor(w[:, k, :], w[:, k, :], winv[:, :], ALU.mult).then_inc(w_chain, 1)
            dve.wait_ge(w_chain, 4 + DC)
            dve.tensor_scalar(w[:, :, :], w[:, :, :], INT8_MAX, -INT8_MAX, ALU.min, ALU.max).then_inc(w_chain, 1)
            dve.wait_ge(w_chain, 5 + DC)
            dve.tensor_scalar(w[:, :, :], w[:, :, :], ROUND, None, ALU.add).then_inc(w_chain, 1)
            dve.wait_ge(w_chain, 6 + DC)
            dve.tensor_scalar(wq[:, :, :], w[:, :, :], -ROUND, None, ALU.add).then_inc(wq_done, 1)

            def stats(i, s):
                free_slot(dve, rstd_done, i, 2)
                for g in range(G):
                    last = dve.bn_stats(bn[:, s, g, :], X[:, i * G + g, :])
                last.then_inc(bn_done, 1)
                wait_for(dve, bn_done, i + 1)
                for g in range(G):
                    last = dve.bn_aggr(mv[:, s, g, :], bn[:, s, g, :])
                last.then_inc(mv_done, 1)

            def quantize(i, s):
                wait_for(dve, y_done, i + 1)
                dve.tensor_reduce(amax[:, s, :], y[:, s, :, :], AX.X, ALU.max,
                                  apply_absolute_value=True).then_inc(sc_chain, 1)
                wait_for(dve, sc_chain, i * 4 + 1)
                dve.tensor_scalar(scale[:, i % 4, :], amax[:, s, :], 1e-12, 1.0 / INT8_MAX, ALU.max,
                                  ALU.mult).then_inc(sc_chain, 1)
                wait_for(dve, sc_chain, i * 4 + 2)
                dve.reciprocal(inv[:, s, :], scale[:, i % 4, :]).then_inc(sc_chain, 1)
                wait_for(dve, sc_chain, i * 4 + 3)
                for g in range(G):
                    yt = y[:, s, g, :]
                    last = dve.tensor_scalar(yt, yt, inv[:, s, g:g + 1], INT8_MAX, ALU.mult, ALU.min)
                last.then_inc(sc_chain, 1)
                wait_for(dve, sc_chain, i * 4 + 4)
                dve.tensor_scalar(y[:, s, :, :], y[:, s, :, :], -INT8_MAX, ROUND, ALU.max,
                                  ALU.add).then_inc(v_done, 1)

            def rescale(i, s):
                wait_for(dve, o_mm, i + 1)
                free_slot(dve, x_done, i, 2)
                for g in range(G):
                    last = dve.scalar_tensor_tensor(delta[:, s, g, :], psO[:, s, g, :],
                                                    scale[:, i % 4, g:g + 1], wscale[:, :], ALU.mult, ALU.mult)
                last.then_inc(d_done, 1)

            pipeline(dve, GROUPS, [(0, stats), (1, quantize), (3, rescale)])

        @block.gpsimd
        def _(pool):
            pool.wait_ge(w_chain, 2)
            pool.partition_all_reduce(wmax[:, :], wabs[:, 0, :], P, bass.bass_isa.ReduceOp.max).then_inc(wmax_done, 1)

            def rstds(i, s):
                wait_for(pool, mv_done, i + 1)
                free_slot(pool, y_done, i, 2)
                rstd_steps(pool, rstd[:, s, :], nmr[:, s, :], mv[:, s, :, :], mhalf[:, 0:G],
                           chain, i * 3, rstd_done)

            def residual(i, s):
                wait_for(pool, d_done, i + 1)
                xt = X[:, bass.ds(i * G, G), :]
                pool.tensor_tensor(xt, delta[:, s, :, :], xt, ALU.add).then_inc(x_done, 1)

            pipeline(pool, GROUPS, [(0, rstds), (4, residual)])

        @block.scalar
        def _(act):
            def norm(i, s):
                wait_for(act, rstd_done, i + 1)
                free_slot(act, q_done, i, 2)
                for g in range(G):
                    last = act.activation(y[:, s, g, :], X[:, i * G + g, :], ACT.Identity,
                                          bias=nmr[:, s, g:g + 1], scale=rstd[:, s, g:g + 1])
                last.then_inc(y_done, 1)

            def unround(i, s):
                wait_for(act, v_done, i + 1)
                free_slot(act, qT_mm, i, 2)
                act.activation(q[:, s, :, :], y[:, s, :, :], ACT.Identity,
                               bias=minus_round[:, :]).then_inc(q_done, 1)

            def copy_qT(i, s):
                wait_for(act, qT_mm, i + 1)
                free_slot(act, o_mm, i, 2)
                act.activation(qT[:, s, :, :, :], psT[:, s, :, :, :], ACT.Copy).then_inc(qT_done, 1)

            act.wait_ge(w_chain, 1)
            pipeline(act, GROUPS, [(0, norm), (2, copy_qT), (1, unround)])

        @block.tensor
        def _(pe):
            pe.wait_ge(wq_done, 1)

            def transpose_q(i, s):
                wait_for(pe, q_done, i + 1)
                free_slot(pe, qT_done, i, 2)
                for g in range(G):
                    for k in range(DC):
                        mm = pe.transpose(psT[:, s, g, k, :], q[:, s, g, k * P:(k + 1) * P], identb[:, :])
                mm.then_inc(qT_mm, 1)

            def product(i, s):
                wait_for(pe, qT_done, i + 1)
                free_slot(pe, d_done, i, 2)
                for g in range(G):
                    for k in range(DC):
                        mm = pe.matmul(psO[:, s, g, :], qT[:, s, g, k, :], wq[:, k, :],
                                       start=(k == 0), stop=(k == DC - 1))
                mm.then_inc(o_mm, 1)

            pipeline(pe, GROUPS, [(1, transpose_q), (2, product)])


def phase_c(nc, scope, X, KT, VT, WqT, Wo, ident, mhalf, maskrow, onesrow):
    stack, sb, ps, sem = scope()
    with stack:
        M = sb("c_M", [P, 2, DC, HEADS * KV])
        U = sb("c_U", [P, 2, PAIRS, D])
        wq = sb("c_wq", [P, 2, D])
        KB = sb("c_KB", [P, 2, P])
        VB = sb("c_VB", [P, 2, P])
        wo = sb("c_wo", [P, 2, D])
        bn = sb("c_bn", [P, 2, 1, 6])
        mv = sb("c_mv", [P, 2, 1, 2])
        rstd = sb("c_rstd", [P, 2, 1])
        nmr = sb("c_nmr", [P, 2, 1])
        y = sb("c_y", [P, D])
        yT = sb("c_yT", [P, 2, DC, P])
        S = sb("c_S", [P, 2, HEADS, KV])
        W = sb("c_W", [P, HEADS, KV])
        top8 = sb("c_top8", [P, 4, HEADS, 8])
        nmax = sb("c_nmax", [P, HEADS])
        E = sb("c_E", [P, 2, HEADS, KV])
        Z = sb("c_Z", [P, HEADS])
        kept = sb("c_kept", [P, HEADS])
        den = sb("c_den", [P, HEADS])
        rden = sb("c_rden", [P, HEADS])
        aT = sb("c_aT", [P, PAIRS, P])
        psY = ps("c_psY", [P, DC, P])
        psS = ps("c_psS", [P, HEADS, KV])
        psA = ps("c_psA", [P, PAIRS, P])
        psO = ps("c_psO", [P, D])
        psM = ps("c_psM", [P, DC, P])
        psU = ps("c_psU", [P, D])
        wq_in = sem("c_wq_in")
        wo_in = sem("c_wo_in")
        blocks_zero = sem("c_blocks_zero")
        kb_done = sem("c_kb_done")
        vb_done = sem("c_vb_done")
        m_mm = sem("c_m_mm")
        m_done = sem("c_m_done")
        u_mm = sem("c_u_mm")
        u_done = sem("c_u_done")
        bn_done = sem("c_bn_done")
        mv_done = sem("c_mv_done")
        chain = sem("c_chain")
        rstd_done = sem("c_rstd_done")
        y_done = sem("c_y_done")
        yT_mm = sem("c_yT_mm")
        yT_done = sem("c_yT_done")
        s_mm = sem("c_s_mm")
        s_done = sem("c_s_done")
        topk = sem("c_topk")
        nmax_done = sem("c_nmax_done")
        e_done = sem("c_e_done")
        kept_done = sem("c_kept_done")
        den_chain = sem("c_den_chain")
        den_done = sem("c_den_done")
        rden_done = sem("c_rden_done")
        a_done = sem("c_a_done")
        aT_mm = sem("c_aT_mm")
        aT_done = sem("c_aT_done")
        o_mm = sem("c_o_mm")
        x_done = sem("c_x_done")
        block = stack.enter_context(nc.Block())
        HALF = HEADS // 2
        ROUNDS = TOPK // 8
        STEPS = 2 * (2 * ROUNDS - 1)
        PREPS = BATCH * PAIRS

        @block.sync
        def _(sp):
            def load_wq(u, s):
                free_slot(sp, m_mm, u, 2)
                sp.dma_start(wq[:, s, :], WqT[bass.ds((u % PAIRS) * P, P), :]).then_inc(wq_in, 16)
                wait_for(sp, wq_in, (u + 1) * 16)

            def load_wo(u, s):
                free_slot(sp, u_mm, u, 2)
                sp.dma_start(wo[:, s, :], Wo[bass.ds((u % PAIRS) * P, P), :]).then_inc(wo_in, 16)
                wait_for(sp, wo_in, (u + 1) * 16)

            pipeline(sp, PREPS, [(-8, load_wq), (-6, load_wo)])

        @block.vector
        def _(dve):
            def stats(t, s):
                free_slot(dve, rstd_done, t, 2)
                dve.bn_stats(bn[:, s, 0, :], X[:, t, :]).then_inc(bn_done, 1)
                wait_for(dve, bn_done, t + 1)
                dve.bn_aggr(mv[:, s, 0, :], bn[:, s, 0, :]).then_inc(mv_done, 1)

            def residual(t, s):
                wait_for(dve, o_mm, t + 1)
                dve.tensor_tensor(X[:, t, :], psO[:, :], X[:, t, :], ALU.add).then_inc(x_done, 1)

            def select(t, s):
                wait_for(dve, s_done, t + 1)
                free_slot(dve, nmax_done, t, 1)
                for r in range(ROUNDS):
                    if r:
                        for h in range(HEADS):
                            if h % HALF == 0:
                                wait_for(dve, topk, t * STEPS + 4 * r - 3 + h // HALF)
                            last = dve.match_replace(W[:, h, :], top8[:, r - 1, h, :],
                                                     (S[:, s, h, :] if r == 1 else W[:, h, :]), TAKEN)
                            if h % HALF == HALF - 1:
                                last.then_inc(topk, 1)
                    for h in range(HEADS):
                        if r and h % HALF == 0:
                            wait_for(dve, topk, t * STEPS + 4 * r - 1 + h // HALF)
                        last = dve.max(top8[:, r, h, :], (W[:, h, :] if r else S[:, s, h, :]))
                        if h % HALF == HALF - 1:
                            last.then_inc(topk, 1)

            def keep_top(t, s):
                wait_for(dve, e_done, t + 1)
                free_slot(dve, den_done, t, 1)
                for h in range(HEADS):
                    if h % HALF == 0:
                        wait_for(dve, topk, t * STEPS + STEPS - 1 + h // HALF)
                    e = E[:, s, h, :]
                    last = dve.scalar_tensor_tensor(e, S[:, s, h, :], top8[:, ROUNDS - 1, h, 7:8], e,
                                                    ALU.is_ge, ALU.mult, accum_out=kept[:, h:h + 1])
                last.then_inc(kept_done, 1)

            def inverse(t, s):
                wait_for(dve, den_done, t + 1)
                free_slot(dve, a_done, t, 1)
                dve.reciprocal(rden[:, :], den[:, :]).then_inc(rden_done, 1)

            pipeline(dve, TILES, [(0, stats), (3, inverse), (4, residual), (2, select), (2, keep_top)])

        @block.gpsimd
        def _(pool):
            def rstds(t, s):
                wait_for(pool, mv_done, t + 1)
                free_slot(pool, y_done, t, 2)
                rstd_steps(pool, rstd[:, s, :], nmr[:, s, :], mv[:, s, :, :], mhalf[:, 0:1],
                           chain, t * 3, rstd_done)

            def negate_max(t, s):
                wait_for(pool, topk, t * STEPS + 2)
                free_slot(pool, e_done, t, 1)
                pool.tensor_scalar(nmax[:, :], top8[:, 0, :, 0], -1.0, None, ALU.mult).then_inc(nmax_done, 1)

            def denominator(t, s):
                wait_for(pool, kept_done, t + 1)
                free_slot(pool, rden_done, t, 1)
                pool.tensor_scalar(den[:, :], Z[:, :], NORM_EPS, None, ALU.mult).then_inc(den_chain, 1)
                wait_for(pool, den_chain, t + 1)
                pool.tensor_tensor(den[:, :], den[:, :], kept[:, :], ALU.add).then_inc(den_done, 1)

            def normalize(t, s):
                wait_for(pool, rden_done, t + 1)
                e = E[:, s, :, :]
                pool.tensor_tensor(e, e, rden[:, :].unsqueeze(2).to_broadcast([P, HEADS, KV]), ALU.mult).then_inc(a_done, 1)

            pool.memset(KB[:, :, :], 0.0).then_inc(blocks_zero, 1)
            pool.memset(VB[:, :, :], 0.0).then_inc(blocks_zero, 1)
            pipeline(pool, TILES, [(0, rstds), (3, normalize), (2, negate_max), (2, denominator)])

        @block.scalar
        def _(act):
            def norm(t, s):
                wait_for(act, rstd_done, t + 1)
                free_slot(act, yT_mm, t, 1)
                act.activation(y[:, :], X[:, t, :], ACT.Identity, bias=nmr[:, s, :],
                               scale=rstd[:, s, :]).then_inc(y_done, 1)

            def copy_yT(t, s):
                wait_for(act, yT_mm, t + 1)
                free_slot(act, s_mm, t, 2)
                act.activation(yT[:, s, :, :], psY[:, :, :], ACT.Copy).then_inc(yT_done, 1)

            def copy_M(u, s):
                wait_for(act, m_mm, u + 1)
                act.activation(M[:, (u // PAIRS) % 2, :, bass.ds((u % PAIRS) * P, P)], psM[:, :, :],
                               ACT.Copy).then_inc(m_done, 1)

            def copy_U(u, s):
                wait_for(act, u_mm, u + 1)
                act.activation(U[:, (u // PAIRS) % 2, u % PAIRS, :], psU[:, :], ACT.Copy).then_inc(u_done, 1)

            def exps(t, s):
                wait_for(act, nmax_done, t + 1)
                free_slot(act, den_done, t, 1)
                free_slot(act, aT_mm, t, 2)
                for h in range(HEADS):
                    last = act.activation(E[:, s, h, :], S[:, s, h, :], ACT.Exp, bias=nmax[:, h:h + 1],
                                          accum_out=Z[:, h:h + 1])
                last.then_inc(e_done, 1)

            def copy_aT(t, s):
                wait_for(act, aT_mm, t + 1)
                free_slot(act, o_mm, t, 1)
                act.activation(aT[:, :, :], psA[:, :, :], ACT.Copy).then_inc(aT_done, 1)

            def copy_S(t, s):
                wait_for(act, s_mm, t + 1)
                free_slot(act, kept_done, t, 2)
                act.activation(S[:, s, :, :], psS[:, :, :], ACT.Copy).then_inc(s_done, 1)

            def spread(u, s, T, B, used, done):
                free_slot(act, used, u, 2)
                for h in range(2):
                    at = slice(h * DH, (h + 1) * DH)
                    last = act.activation(B[at, s, at], T[at, u % PAIRS, bass.ds((u // PAIRS) * KV, KV)],
                                          ACT.Copy)
                last.then_inc(done, 1)

            def spread_K(u, s):
                spread(u, s, KT, KB, m_mm, kb_done)

            def spread_V(u, s):
                spread(u, s, VT, VB, u_mm, vb_done)

            act.wait_ge(blocks_zero, 2)
            pipeline(act, TILES, [(-8, spread_K), (-6, spread_V), (0, norm), (0, copy_yT), (-7, copy_M), (2, exps), (3, copy_aT), (1, copy_S),
                                  (-5, copy_U)])

        @block.tensor
        def _(pe):
            def scores(t, s):
                wait_for(pe, yT_done, t + 1)
                wait_for(pe, m_done, (t // TPB) * PAIRS + PAIRS)
                free_slot(pe, s_done, t, 1)
                for n in range(2):
                    half = psS[:, n * HALF:(n + 1) * HALF, :]
                    pe.matmul(half, onesrow[:, :], maskrow[:, t // TPB, :, :], start=True, stop=False)
                    for k in range(DC):
                        mm = pe.matmul(half, yT[:, s, k, :], M[:, (t // TPB) % 2, k, n * 512:(n + 1) * 512],
                                       start=False, stop=(k == DC - 1))
                mm.then_inc(s_mm, 1)

            def make_M(u, s):
                wait_for(pe, wq_in, (u + 1) * 16)
                free_slot(pe, m_done, u, 1)
                wait_for(pe, kb_done, u + 1)
                for k in range(DC):
                    mm = pe.matmul(psM[:, k, :], wq[:, s, k * P:(k + 1) * P], KB[:, s, :], start=True, stop=True)
                mm.then_inc(m_mm, 1)

            def make_U(u, s):
                wait_for(pe, wo_in, (u + 1) * 16)
                free_slot(pe, u_done, u, 1)
                wait_for(pe, vb_done, u + 1)
                pe.matmul(psU[:, :], VB[:, s, :], wo[:, s, :],
                          start=True, stop=True).then_inc(u_mm, 1)

            def transpose_y(t, s):
                wait_for(pe, y_done, t + 1)
                free_slot(pe, yT_done, t, 1)
                for k in range(DC):
                    mm = pe.transpose(psY[:, k, :], y[:, k * P:(k + 1) * P], ident[:, :])
                mm.then_inc(yT_mm, 1)

            def transpose_a(t, s):
                wait_for(pe, a_done, t + 1)
                free_slot(pe, aT_done, t, 1)
                a = E[:, s, :, :].rearrange("p h s -> p (h s)")
                for n in range(PAIRS):
                    mm = pe.transpose(psA[:, n, :], a[:, n * P:(n + 1) * P], ident[:, :])
                mm.then_inc(aT_mm, 1)

            def values(t, s):
                wait_for(pe, aT_done, t + 1)
                wait_for(pe, u_done, (t // TPB) * PAIRS + PAIRS)
                free_slot(pe, x_done, t, 1)
                for n in range(PAIRS):
                    mm = pe.matmul(psO[:, :], aT[:, n, :], U[:, (t // TPB) % 2, n, :],
                                   start=(n == 0), stop=(n == PAIRS - 1))
                mm.then_inc(o_mm, 1)

            pipeline(pe, TILES, [(1, scores), (-7, make_M), (0, transpose_y), (3, transpose_a), (-5, make_U),
                                 (3, values)])


class Routing:

    def __init__(self, sb):
        self.tri = sb("r_tri", [P, P], bf16)
        self.ones = sb("r_ones", [P, P], bf16)
        self.ones1 = sb("r_ones1", [1, P])
        self.eid = sb("r_eid", [P, EXPERTS])
        self.ebase = sb("r_ebase", [P, EXPERTS])
        self.token = sb("r_token", [P, TILES])
        self.jrow = sb("r_jrow", [1, SLOTS])
        self.which = sb("r_which", [P, TILES, CHOICES])
        self.row = sb("r_row", [P, TILES, CHOICES])
        self.pos = sb("r_pos", [P, TILES, CHOICES], u32)
        self.load = sb("r_load", [P, 2, EXPERTS], bf16)


def gather_rows(pool, done, R, t, s, idx, picked, rows, made):
    pool.tensor_copy(idx[:, s, :, :], R.pos[:, bass.ds(t * G, G), :]).then_inc(picked, 1)
    wait_for(pool, picked, t + 1)
    for g in range(G):
        for c in range(CHOICES):
            pool.indirect_dma_start(rows[:, s, g, c, :], None, made,
                                    bass.IndirectOffsetOnAxis(ap=idx[:, s, g, c:c + 1], axis=0)).then_inc(done[s], 16)


def route(nc, scope, R, layer, X, W, ident, mhalf, rwT, rb, ewT, hidden, listed, made):
    stack, sb, ps, sem = scope(recycle=True)
    with stack:
        L = f"r{layer}_"
        rw = sb(L + "rw", [P, DC, EXPERTS])
        rbr = sb(L + "rbr", [1, EXPERTS])
        h = sb(L + "h", [P, 2, G, D])
        hT = sb(L + "hT", [P, 2, G, DC, P])
        logits = sb(L + "logits", [P, 2, G, EXPERTS])
        best = sb(L + "best", [P, 2, G, 8])
        which = sb(L + "which", [P, 2, G, 8], u32)
        whichf = sb(L + "whichf", [P, G, CHOICES])
        hot = sb(L + "hot", [P, 2, G, CHOICES, EXPERTS])
        chosen = sb(L + "chosen", [P, 2, G, EXPERTS], bf16)
        row = sb(L + "row", [P, G, EXPERTS])
        rowhot = sb(L + "rowhot", [P, G, CHOICES, EXPERTS])
        rowf = sb(L + "rowf", [P, G, CHOICES])
        rowi = sb(L + "rowi", [P, 2, G, CHOICES], u32)
        tok = sb(L + "tok", [P, 2, G])
        psT = ps(L + "psT", [P, G, DC, P])
        psL = ps(L + "psL", [P, 512])
        psR = ps(L + "psR", [P, 512])
        made_const = sem(L + "const")
        w_in = sem(L + "w_in")
        W_in = [sem(L + f"W_in{e}") for e in range(EXPERTS)]
        h_done = sem(L + "h_done")
        h_out = [sem(L + f"h_out{n}") for n in range(2)]
        hT_mm = sem(L + "hT_mm")
        hT_done = sem(L + "hT_done")
        l_mm = sem(L + "l_mm")
        top = sem(L + "top")
        chosen_done = sem(L + "chosen_done")
        load_done = sem(L + "load_done")
        r_mm = sem(L + "r_mm")
        row_chain = sem(L + "row_chain")
        row_done = sem(L + "row_done")
        tok_done = sem(L + "tok_done")
        listing = [sem(L + f"listing{n}") for n in range(2)]
        LG = psL[:, 0:G * EXPERTS].rearrange("p (g e) -> p g e", g=G)
        RW = psR[:, 0:G * EXPERTS].rearrange("p (g e) -> p g e", g=G)
        if layer == 0:
            bn = sb(L + "bn", [P, 2, G, 6])
            mv = sb(L + "mv", [P, 2, G, 2])
            rstd = sb(L + "rstd", [P, 2, G])
            nmr = sb(L + "nmr", [P, 2, G])
            zero = sb(L + "zero", [P, SPARE])
            bn_done = sem(L + "bn_done")
            mv_done = sem(L + "mv_done")
            chain = sem(L + "chain")
            rstd_done = sem(L + "rstd_done")
            zero_made = sem(L + "zero_made")
            zeroed = sem(L + "zeroed")
        else:
            idx = sb(L + "idx", [P, 2, G, CHOICES], u32)
            rows = sb(L + "rows", [P, 2, G, CHOICES, D])
            picked = sem(L + "picked")
            rows_in = [sem(L + f"rows_in{n}") for n in range(2)]
        block = stack.enter_context(nc.Block())
        hv = hidden.rearrange("(t p) d -> p t d", p=P)

        @block.sync
        def _(sp):
            sp.dma_start(rw[:, :, :], rwT[layer].rearrange("(k p) e -> p k e", p=P)).then_inc(w_in, 16)
            sp.dma_start(rbr[:, :], rb[layer:layer + 1, :]).then_inc(w_in, 16)
            for e in range(EXPERTS):
                sp.dma_start(W[:, e, :, :], ewT[layer, e].rearrange("(k p) n -> p k n", p=P)).then_inc(W_in[e], 16)
            if layer == 0:
                sp.wait_ge(zero_made, 1)
                sp.dma_start(listed.rearrange("(p n) o -> p (n o)", p=P), zero[:, :]).then_inc(zeroed, 16)

            def store_h(i, s):
                wait_for(sp, h_done, i + 1)
                sp.dma_start(hv[:, bass.ds(i * G, G), :], h[:, s, :, :]).then_inc(h_out[s], 16)

            pipeline(sp, GROUPS, [(0, store_h)])
            for n in range(2):
                sp.wait_ge(h_out[n], GROUPS // 2 * 16)
            for e in range(EXPERTS):
                sp.wait_ge(W_in[e], 16)

        @block.vector
        def _(dve):
            def stats(i, s):
                free_slot(dve, rstd_done, i, 2)
                for g in range(G):
                    last = dve.bn_stats(bn[:, s, g, :], X[:, i * G + g, :])
                last.then_inc(bn_done, 1)
                wait_for(dve, bn_done, i + 1)
                for g in range(G):
                    last = dve.bn_aggr(mv[:, s, g, :], bn[:, s, g, :])
                last.then_inc(mv_done, 1)

            def add_outputs(i, s):
                wait_for(dve, rows_in[s], (i // 2 + 1) * (G * CHOICES * 16))
                free_slot(dve, hT_mm, i, 2)
                if not isinstance(i, int) or i >= 2:
                    wait_for(dve, h_out[s], (i // 2) * 16)
                dve.tensor_tensor(h[:, s, :, :], rows[:, s, :, 0, :], rows[:, s, :, 1, :], ALU.add).then_inc(h_done, 1)

            def choose(i, s):
                wait_for(dve, l_mm, i + 1)
                dve.tensor_copy(logits[:, s, :, :], LG).then_inc(top, 1)
                wait_for(dve, top, i * 5 + 1)
                for g in range(G):
                    last = dve.max(best[:, s, g, :], logits[:, s, g, :])
                last.then_inc(top, 1)
                wait_for(dve, top, i * 5 + 2)
                for g in range(G):
                    last = dve.max_index(which[:, s, g, :], best[:, s, g, :], logits[:, s, g, :])
                last.then_inc(top, 1)
                wait_for(dve, top, i * 5 + 3)
                dve.tensor_copy(whichf[:, :, :], which[:, s, :, 0:CHOICES]).then_inc(top, 1)
                wait_for(dve, top, i * 5 + 4)
                shape = [P, G * CHOICES, EXPERTS]
                dve.tensor_tensor(hot[:, s, :, :, :].rearrange("p g c e -> p (g c) e"),
                                  R.eid[:, :].unsqueeze(1).to_broadcast(shape),
                                  whichf[:, :, :].rearrange("p g c -> p (g c)").unsqueeze(2).to_broadcast(shape),
                                  ALU.is_equal).then_inc(top, 1)
                wait_for(dve, top, i * 5 + 5)
                dve.tensor_copy(R.which[:, bass.ds(i * G, G), :], whichf[:, :, :])
                free_slot(dve, r_mm, i, 2)
                dve.tensor_tensor(chosen[:, s, :, :], hot[:, s, :, 0, :], hot[:, s, :, 1, :],
                                  ALU.add).then_inc(chosen_done, 1)

            def count(i, s):
                wait_for(dve, chosen_done, i + 1)
                free_slot(dve, r_mm, i, 1)
                dve.tensor_tensor(R.load[:, 1 - s, :], R.load[:, s, :], chosen[:, s, 0, :], ALU.add).then_inc(load_done, 1)
                wait_for(dve, load_done, i * 2 + 2)
                dve.tensor_tensor(R.load[:, 1 - s, :], R.load[:, 1 - s, :], chosen[:, s, 1, :],
                                  ALU.add).then_inc(load_done, 1)

            def place(i, s):
                wait_for(dve, r_mm, i + 1)
                dve.tensor_tensor(row[:, :, :], RW, R.ebase[:, :].unsqueeze(1).to_broadcast([P, G, EXPERTS]),
                                  ALU.add).then_inc(row_chain, 1)
                wait_for(dve, row_chain, i * 4 + 1)
                for g in range(G):
                    last = dve.tensor_tensor(rowhot[:, g, :, :], hot[:, s, g, :, :],
                                             row[:, g, :].unsqueeze(1).to_broadcast([P, CHOICES, EXPERTS]), ALU.mult)
                last.then_inc(row_chain, 1)
                wait_for(dve, row_chain, i * 4 + 2)
                dve.tensor_reduce(rowf[:, :, :], rowhot[:, :, :, :], AX.X, ALU.add).then_inc(row_chain, 1)
                wait_for(dve, row_chain, i * 4 + 3)
                dve.tensor_copy(R.row[:, bass.ds(i * G, G), :], rowf[:, :, :]).then_inc(row_chain, 1)
                if not isinstance(i, int) or i >= 2:
                    wait_for(dve, listing[s], (i // 2) * (G * CHOICES * 16))
                dve.tensor_copy(rowi[:, s, :, :], rowf[:, :, :]).then_inc(row_done, 1)

            dve.memset(R.load[:, :, :], 0.0).then_inc(load_done, 1)
            dve.memset(tok[:, :, :], 0.0)
            if layer == 0:
                dve.memset(zero[:, :], 0.0).then_inc(zero_made, 1)
            dve.wait_ge(load_done, 1)
            if layer == 0:
                pipeline(dve, GROUPS, [(0, stats), (3, choose), (3, count), (4, place)])
            else:
                pipeline(dve, GROUPS, [(0, add_outputs), (3, choose), (3, count), (4, place)])

        @block.gpsimd
        def _(pool):
            if layer == 0:
                pool.memset(R.ones[:, :], 1.0).then_inc(made_const, 1)
                pool.memset(R.ones1[:, :], 1.0)
                pool.iota(R.eid[:, :], [[1, EXPERTS]], base=0, channel_multiplier=0,
                          allow_small_or_imprecise_dtypes=True).then_inc(made_const, 1)
                pool.iota(R.ebase[:, :], [[TILES * P, EXPERTS]], base=0, channel_multiplier=0,
                          allow_small_or_imprecise_dtypes=True).then_inc(made_const, 1)
                pool.iota(R.token[:, :], [[P, TILES]], base=0, channel_multiplier=1,
                          allow_small_or_imprecise_dtypes=True).then_inc(made_const, 1)
                pool.iota(R.jrow[:, :], [[1, SLOTS]], base=0, channel_multiplier=0,
                          allow_small_or_imprecise_dtypes=True).then_inc(made_const, 1)
                pool.wait_ge(made_const, 5)
                pool.affine_select(out=R.tri[:, :], in_=R.ones[:, :], compare_op=ALU.is_gt, fill=0.0, base=0,
                                   pattern=[[1, P]], channel_multiplier=-1).then_inc(made_const, 1)
                pool.wait_ge(zeroed, 16)

            def rstds(i, s):
                wait_for(pool, mv_done, i + 1)
                free_slot(pool, h_done, i, 2)
                rstd_steps(pool, rstd[:, s, :], nmr[:, s, :], mv[:, s, :, :], mhalf[:, 0:G], chain, i * 3, rstd_done)

            def fetch(i, s):
                free_slot(pool, h_done, i, 2)
                gather_rows(pool, rows_in, R, i, s, idx, picked, rows, made)

            def list_tokens(i, s):
                if not isinstance(i, int) or i >= 2:
                    wait_for(pool, listing[s], (i // 2) * (G * CHOICES * 16))
                pool.tensor_copy(tok[:, s, :], R.token[:, bass.ds(i * G, G)]).then_inc(tok_done, 1)
                wait_for(pool, tok_done, i + 1)
                wait_for(pool, row_done, i + 1)
                for g in range(G):
                    for c in range(CHOICES):
                        pool.indirect_dma_start(listed, bass.IndirectOffsetOnAxis(ap=rowi[:, s, g, c:c + 1], axis=0),
                                                tok[:, s, g:g + 1], None).then_inc(listing[s], 16)

            pipeline(pool, GROUPS, [(0, rstds if layer == 0 else fetch), (4, list_tokens)])
            for n in range(2):
                pool.wait_ge(listing[n], GROUPS // 2 * G * CHOICES * 16)

        @block.scalar
        def _(act):
            def norm(i, s):
                wait_for(act, rstd_done, i + 1)
                free_slot(act, hT_mm, i, 2)
                if not isinstance(i, int) or i >= 2:
                    wait_for(act, h_out[s], (i // 2) * 16)
                for g in range(G):
                    last = act.activation(h[:, s, g, :], X[:, i * G + g, :], ACT.Identity,
                                          bias=nmr[:, s, g:g + 1], scale=rstd[:, s, g:g + 1])
                last.then_inc(h_done, 1)

            def copy_hT(i, s):
                wait_for(act, hT_mm, i + 1)
                free_slot(act, l_mm, i, 2)
                act.activation(hT[:, s, :, :, :], psT[:, :, :, :], ACT.Copy).then_inc(hT_done, 1)

            pipeline(act, GROUPS, ([(0, norm)] if layer == 0 else []) + [(1, copy_hT)])

        @block.tensor
        def _(pe):
            pe.wait_ge(w_in, 32)
            if layer == 0:
                pe.wait_ge(made_const, 6)

            def transpose_h(i, s):
                wait_for(pe, h_done, i + 1)
                free_slot(pe, hT_done, i, 1)
                for g in range(G):
                    for k in range(DC):
                        mm = pe.transpose(psT[:, g, k, :], h[:, s, g, k * P:(k + 1) * P], ident[:, :])
                mm.then_inc(hT_mm, 1)

            def logit(i, s):
                wait_for(pe, hT_done, i + 1)
                if not isinstance(i, int) or i >= 1:
                    wait_for(pe, top, i * 5 - 4)
                for g in range(G):
                    pe.matmul(LG[:, g, :], R.ones1[:, :], rbr[:, :], start=True, stop=False)
                    for k in range(DC):
                        mm = pe.matmul(LG[:, g, :], hT[:, s, g, k, :], rw[:, k, :], start=False, stop=(k == DC - 1))
                mm.then_inc(l_mm, 1)

            def rank(i, s):
                wait_for(pe, chosen_done, i + 1)
                wait_for(pe, load_done, i * 2 + 1)
                if not isinstance(i, int) or i >= 1:
                    wait_for(pe, row_chain, i * 4 - 3)
                for g in range(G):
                    pe.matmul(RW[:, g, :], R.ones[:, :], R.load[:, s, :], start=True, stop=False)
                    if g:
                        pe.matmul(RW[:, g, :], R.ones[:, :], chosen[:, s, 0, :], start=False, stop=False)
                    mm = pe.matmul(RW[:, g, :], R.tri[:, :], chosen[:, s, g, :], start=False, stop=True)
                mm.then_inc(r_mm, 1)

            pipeline(pe, GROUPS, [(0, transpose_h), (1, logit), (3, rank)])


def experts(nc, scope, R, layer, W, ident, eb, hidden, listed, made):
    stack, sb, ps, sem = scope(recycle=True)
    with stack:
        L = f"e{layer}_"
        DEEP = 4
        bias = sb(L + "bias", [P, EXPERTS, D])
        lists = sb(L + "lists", [P, EXPERTS * TILES // P, P])
        tokens = sb(L + "tokens", [P, SPARE + SPARES], u32)
        n_pad = sb(L + "n_pad", [P, EXPERTS], i32)
        n_cut = sb(L + "n_cut", [P, EXPERTS], i32)
        tiles = sb(L + "tiles", [P, EXPERTS])
        one = sb(L + "one", [P, EXPERTS])
        ends = sb(L + "ends", [P, EXPERTS])
        skip = sb(L + "skip", [P, EXPERTS])
        skipped = sb(L + "skipped", [P, EXPERTS])
        before = sb(L + "before", [P, EXPERTS])
        isin = sb(L + "isin", [P, TILES * CHOICES, EXPERTS])
        shift = sb(L + "shift", [P, TILES * CHOICES])
        past = sb(L + "past", [1, SLOTS, EXPERTS])
        pastskip = sb(L + "pastskip", [1, SLOTS, EXPERTS])
        sumf = sb(L + "sumf", [1, 2, SLOTS])
        expert_of = sb(L + "expert_of", [1, SLOTS], i32)
        tile_of = sb(L + "tile_of", [1, SLOTS], i32)
        idx = sb(L + "idx", [P, DEEP], u32)
        rows = sb(L + "rows", [P, DEEP, D])
        rT = sb(L + "rT", [P, 2, DC, P])
        y = sb(L + "y", [P, DEEP, D])
        psN = ps(L + "psN", [P, 512])
        psI = ps(L + "psI", [P, 512])
        psT = ps(L + "psT", [P, 2, DC, P])
        psO = ps(L + "psO", [P, 2, D])
        bias_in = sem(L + "bias_in")
        lists_in = sem(L + "lists_in")
        n_mm = sem(L + "n_mm")
        i_mm = sem(L + "i_mm")
        c = sem(L + "chain")
        maps_done = sem(L + "maps_done")
        tokens_done = sem(L + "tokens_done")
        picked = sem(L + "picked")
        rows_in = [sem(L + f"rows_in{n}") for n in range(DEEP)]
        rT_mm = sem(L + "rT_mm")
        rT_done = sem(L + "rT_done")
        o_mm = sem(L + "o_mm")
        y_done = sem(L + "y_done")
        y_out = [sem(L + f"y_out{n}") for n in range(DEEP)]
        block = stack.enter_context(nc.Block())
        A = EXPERTS * TILES // P

        @block.sync
        def _(sp):
            sp.dma_start(lists[:, :, :], listed[0:SPARE * P, :].rearrange("(a r q) o -> r a (q o)", a=A, q=P)).then_inc(lists_in, 16)
            sp.dma_start(bias[:, :, :], eb[layer:layer + 1, :, :].to_broadcast([P, EXPERTS, D])).then_inc(bias_in, 16)
            slot = made.rearrange("(t p) d -> t p d", p=P)

            def store(t, s):
                wait_for(sp, y_done, t + 1)
                sp.dma_start(slot[bass.ds(t, 1), :, :].rearrange("o p d -> (o p) d"), y[:, s, :]).then_inc(y_out[s], 16)

            pipeline(sp, SLOTS, [(0, store)], DEEP)
            for n in range(DEEP):
                sp.wait_ge(y_out[n], (SLOTS - n + DEEP - 1) // DEEP * 16)

        @block.vector
        def _(dve):
            dve.memset(tokens[:, SPARE:], 0).then_inc(c, 1)
            dve.memset(one[:, :], 1.0).then_inc(c, 1)
            dve.wait_ge(n_mm, 1)
            dve.tensor_scalar(n_pad[:, :], psN[:, 0:EXPERTS], float(P - 1), None, ALU.add).then_inc(c, 1)
            dve.wait_ge(c, 3)
            dve.tensor_scalar(n_cut[:, :], n_pad[:, :], -P, None, ALU.bitwise_and).then_inc(c, 1)
            dve.wait_ge(c, 4)
            dve.tensor_scalar(tiles[:, :], n_cut[:, :], 1.0 / P, None, ALU.mult).then_inc(c, 1)
            dve.wait_ge(c, 5)
            dve.tensor_tensor_scan(ends[:, :], one[:, :], tiles[:, :], 0.0, ALU.mult, ALU.add).then_inc(c, 1)
            dve.tensor_scalar(skip[:, :], tiles[:, :], -1.0, float(TILES), ALU.mult, ALU.add).then_inc(c, 1)
            dve.wait_ge(c, 7)
            shape = [1, SLOTS, EXPERTS]
            dve.tensor_tensor(past[:, :, :], ends[0:1, :].unsqueeze(1).to_broadcast(shape),
                              R.jrow[:, :].unsqueeze(2).to_broadcast(shape), ALU.is_le).then_inc(c, 1)
            dve.wait_ge(c, 8)
            dve.tensor_tensor(pastskip[:, :, :], past[:, :, :], skip[0:1, :].unsqueeze(1).to_broadcast(shape),
                              ALU.mult).then_inc(c, 1)
            dve.tensor_reduce(sumf[:, 0, :], past[:, :, :], AX.X, ALU.add).then_inc(c, 1)
            dve.wait_ge(c, 10)
            dve.tensor_reduce(sumf[:, 1, :], pastskip[:, :, :], AX.X, ALU.add).then_inc(c, 1)
            dve.tensor_scalar(expert_of[:, :], sumf[:, 0, :], float(EXPERTS - 1), None, ALU.min).then_inc(c, 1)
            dve.wait_ge(c, 12)
            dve.tensor_tensor(tile_of[:, :], sumf[:, 1, :], R.jrow[:, :], ALU.add).then_inc(maps_done, 1)
            dve.wait_ge(i_mm, 1)
            dve.tensor_copy(tokens[:, 0:SPARE], psI[:, 0:SPARE]).then_inc(tokens_done, 1)
            dve.tensor_tensor_scan(skipped[:, :], one[:, :], skip[:, :], 0.0, ALU.mult, ALU.add).then_inc(c, 1)
            shape = [P, TILES * CHOICES, EXPERTS]
            dve.tensor_tensor(isin[:, :, :], R.which[:, :, :].rearrange("p t c -> p (t c)").unsqueeze(2).to_broadcast(shape),
                              R.eid[:, :].unsqueeze(1).to_broadcast(shape), ALU.is_equal).then_inc(c, 1)
            dve.wait_ge(c, 14)
            dve.tensor_tensor(before[:, :], skipped[:, :], skip[:, :], ALU.subtract).then_inc(c, 1)
            dve.wait_ge(c, 15)
            dve.tensor_tensor(isin[:, :, :], isin[:, :, :], before[:, :].unsqueeze(1).to_broadcast(shape),
                              ALU.mult).then_inc(c, 1)
            dve.wait_ge(c, 16)
            dve.tensor_reduce(shift[:, :], isin[:, :, :], AX.X, ALU.add).then_inc(c, 1)
            dve.wait_ge(c, 17)
            dve.scalar_tensor_tensor(R.pos[:, :, :].rearrange("p t c -> p (t c)"), shift[:, :], float(-P),
                                     R.row[:, :, :].rearrange("p t c -> p (t c)"), ALU.mult, ALU.add).then_inc(c, 1)
            dve.wait_ge(maps_done, 1)
            dve.wait_ge(bias_in, 16)

            def add_bias(t, s):
                e = dve.value_load(expert_of[0:1, bass.ds(t, 1)], min_val=0, max_val=EXPERTS - 1)
                wait_for(dve, o_mm, t + 1)
                if not isinstance(t, int) or t >= DEEP:
                    wait_for(dve, y_out[s], (t // DEEP) * 16)
                dve.tensor_tensor(y[:, s, :], psO[:, s % 2, :], bias[:, bass.ds(e, 1), :].rearrange("p o d -> p (o d)"),
                                  ALU.add).then_inc(y_done, 1)

            pipeline(dve, SLOTS, [(0, add_bias)], DEEP)

        @block.gpsimd
        def _(pool):
            pool.wait_ge(tokens_done, 1)
            pool.wait_ge(maps_done, 1)

            def fetch(t, s):
                tile = pool.value_load(tile_of[0:1, bass.ds(t, 1)], min_val=0, max_val=SPARE + SPARES - 1)
                free_slot(pool, rT_mm, t, DEEP)
                pool.tensor_copy(idx[:, s:s + 1], tokens[:, bass.ds(tile, 1)]).then_inc(picked, 1)
                wait_for(pool, picked, t + 1)
                pool.indirect_dma_start(rows[:, s, :], None, hidden,
                                        bass.IndirectOffsetOnAxis(ap=idx[:, s:s + 1], axis=0)).then_inc(rows_in[s], 16)

            pipeline(pool, SLOTS, [(0, fetch)], DEEP)

        @block.scalar
        def _(act):
            def copy_rT(t, s):
                wait_for(act, rT_mm, t + 1)
                free_slot(act, o_mm, t, 2)
                act.activation(rT[:, s % 2, :, :], psT[:, s % 2, :, :], ACT.Copy).then_inc(rT_done, 1)

            pipeline(act, SLOTS, [(0, copy_rT)], DEEP)

        @block.tensor
        def _(pe):
            pe.matmul(psN[:, 0:EXPERTS], R.ones[:, :], R.load[:, GROUPS % 2, :], start=True, stop=True).then_inc(n_mm, 1)
            pe.wait_ge(lists_in, 16)
            for a in range(A):
                mm = pe.transpose(psI[:, a * P:(a + 1) * P], lists[:, a, :], ident[:, :])
            mm.then_inc(i_mm, 1)
            pe.wait_ge(maps_done, 1)

            def transpose_rows(t, s):
                wait_for(pe, rows_in[s], (t // DEEP + 1) * 16)
                free_slot(pe, rT_done, t, 2)
                for k in range(DC):
                    mm = pe.transpose(psT[:, s % 2, k, :], rows[:, s, k * P:(k + 1) * P], ident[:, :])
                mm.then_inc(rT_mm, 1)

            def product(t, s):
                e = pe.value_load(expert_of[0:1, bass.ds(t, 1)], min_val=0, max_val=EXPERTS - 1)
                wait_for(pe, rT_done, t + 1)
                free_slot(pe, y_done, t, 2)
                for k in range(DC):
                    mm = pe.matmul(psO[:, s % 2, :], rT[:, s % 2, k, :],
                                   W[:, bass.ds(e, 1), k, :].rearrange("p o d -> p (o d)"),
                                   start=(k == 0), stop=(k == DC - 1))
                mm.then_inc(o_mm, 1)

            pipeline(pe, SLOTS, [(0, transpose_rows), (1, product)], DEEP)


def combine(nc, scope, R, X, made, out):
    stack, sb, ps, sem = scope()
    with stack:
        idx = sb("o_idx", [P, 2, G, CHOICES], u32)
        rows = sb("o_rows", [P, 2, G, CHOICES, D])
        y = sb("o_y", [P, 2, G, D])
        picked = sem("o_picked")
        rows_in = [sem(f"o_rows_in{n}") for n in range(2)]
        sum_done = sem("o_sum_done")
        y_done = sem("o_y_done")
        y_out = [sem(f"o_y_out{n}") for n in range(2)]
        block = stack.enter_context(nc.Block())
        ov = out.rearrange("(t p) d -> p t d", p=P)

        @block.gpsimd
        def _(pool):
            def fetch(i, s):
                free_slot(pool, sum_done, i, 2)
                gather_rows(pool, rows_in, R, i, s, idx, picked, rows, made)

            pipeline(pool, GROUPS, [(0, fetch)])

        @block.vector
        def _(dve):
            def add(i, s):
                wait_for(dve, rows_in[s], (i // 2 + 1) * (G * CHOICES * 16))
                if not isinstance(i, int) or i >= 2:
                    wait_for(dve, y_out[s], (i // 2) * 16)
                dve.tensor_tensor(y[:, s, :, :], rows[:, s, :, 0, :], rows[:, s, :, 1, :], ALU.add).then_inc(sum_done, 1)
                wait_for(dve, sum_done, i + 1)
                dve.tensor_tensor(y[:, s, :, :], y[:, s, :, :], X[:, bass.ds(i * G, G), :], ALU.add).then_inc(y_done, 1)

            pipeline(dve, GROUPS, [(0, add)])

        @block.sync
        def _(sp):
            def store(i, s):
                wait_for(sp, y_done, i + 1)
                sp.dma_start(ov[:, bass.ds(i * G, G), :], y[:, s, :, :]).then_inc(y_out[s], 16)

            pipeline(sp, GROUPS, [(0, store)])
            for n in range(2):
                sp.wait_ge(y_out[n], GROUPS // 2 * 16)


def kernel(x, ctx_1024, mask_BxS2_bf1, L0_ffn_rhs, L1_xattn_Wq, L1_xattn_Wk, L1_xattn_Wv, L1_xattn_Wo,
           L1_xattn_inv_temp, L1_ffn_router_w, L1_ffn_router_b, L1_ffn_expert_w, L1_ffn_expert_b):
    import numpy as np
    import concourse.bacc as bacc
    from concourse.bass_utils import run_bass_kernel_spmd

    ctx = np.asarray(ctx_1024).reshape(BATCH * KV, D)
    laid = {
        "x": np.asarray(x).reshape(TOKENS, D),
        "ctxT": ctx.T,
        "ctx": ctx,
        "mask": np.asarray(mask_BxS2_bf1).view(np.uint8),
        "rhs": np.asarray(L0_ffn_rhs),
        "WqT": np.asarray(L1_xattn_Wq).T,
        "Wk": np.asarray(L1_xattn_Wk),
        "Wv": np.asarray(L1_xattn_Wv),
        "Wo": np.asarray(L1_xattn_Wo),
        "inv_temp": np.repeat(np.asarray(L1_xattn_inv_temp), DH).reshape(PAIRS, P).T,
        "rwT": np.asarray(L1_ffn_router_w).transpose(0, 2, 1),
        "rb": np.asarray(L1_ffn_router_b),
        "ewT": np.asarray(L1_ffn_expert_w).transpose(0, 1, 3, 2),
        "eb": np.asarray(L1_ffn_expert_b),
    }
    nc = bacc.Bacc("TRN2", target_bir_lowering=False, num_devices=1)
    arrays, args = {}, []
    for name, a in laid.items():
        a = np.ascontiguousarray(a)
        arrays["in_" + name] = a
        args.append(nc.dram_tensor("in_" + name, a.shape, mybir.dt.from_np(a.dtype), kind="ExternalInput").ap())
    out = nc.dram_tensor("out_x", (TOKENS, D), fp32, kind="ExternalOutput").ap()
    build(nc, *args, out)
    r = run_bass_kernel_spmd(nc, [arrays], core_ids=[0])
    return r.results[0]["out_x"].reshape(BATCH, SEQ, D)
```

```python
import concourse.bass as bass
from concourse import mybir
from contextlib import ExitStack

P = 128
BATCH, SEQ, D = 4, 1024, 512
KV = 64
HEADS, DH = 16, 64
TOPK = 32
EXPERTS, LAYERS, CHOICES = 8, 2, 2
TOKENS = BATCH * SEQ
TILES = TOKENS // P
TPB = SEQ // P
DC = D // P
PAIRS = HEADS // 2
G = 2
GROUPS = TILES // G
GPB = GROUPS // BATCH
SLOTS = (CHOICES * TOKENS + EXPERTS * (P - 1)) // P
TOKEN_ZERO = TOKENS // 2
LN_EPS = 1e-5
NORM_EPS = 1e-8
INT8_MAX = 127.0
ROUND = 1.5 * 2.0 ** 23
MASKED = -3.0e38
TAKEN = -3.4e38

fp32 = mybir.dt.float32
bf16 = mybir.dt.bfloat16
fp16 = mybir.dt.float16
u8 = mybir.dt.uint8
i32 = mybir.dt.int32
u32 = mybir.dt.uint32
ALU = mybir.AluOpType
ACT = mybir.ActivationFunctionType
AX = mybir.AxisListType


HELD = {}


def wait_for(eng, sem, count):
    eng.wait_ge(sem, count)
    if not isinstance(count, int):
        eng.sem_inc(HELD["waited"], 1)


def free_slot(eng, released, t, depth, per=1):
    if not isinstance(t, int) or t >= depth:
        wait_for(eng, released, (t - depth + 1) * per)


def pipeline(eng, count, stages, slots=2):
    first = min(lag for lag, _ in stages)
    last = max(lag for lag, _ in stages) + count
    cuts = {first, last}
    for lag, _ in stages:
        cuts |= {lag, lag + slots, lag + count}
    cuts = sorted(cuts)

    def window(w, place, live):
        for lag, stage in live:
            stage(w - lag, (place - lag) % slots)

    for a, b in zip(cuts, cuts[1:]):
        live = [(lag, stage) for lag, stage in stages if lag <= a < lag + count]
        looped = (b - a) // slots * slots if all(a - lag >= slots for lag, _ in live) else 0
        if looped >= 2 * slots:
            with eng.Fori(0, looped // slots) as body:
                for n in range(slots):
                    window(body * slots + (a + n), a + n, live)
            a += looped
        for w in range(a, b):
            window(w, w, live)


def build(nc, x, ctxT, ctx, mask, rhs, WqT, Wk, Wv, Wo, inv_temp, rwT, rb, ewT, eb, out):
    top = ExitStack()
    with top:
        def scope(recycle=False):
            stack = ExitStack()
            used = []

            def clear():
                nc.clear_and_free_semaphores(used)
                nc.all_engine_barrier()

            if recycle:
                stack.callback(clear)

            def sb(name, shape, dt=fp32):
                return stack.enter_context(nc.sbuf_tensor(name, shape, dt))

            def ps(name, shape, dt=fp32):
                return stack.enter_context(nc.psum_tensor(name, shape, dt))

            def sem(name):
                if not recycle:
                    return stack.enter_context(nc.semaphore(name))
                used.append(nc.alloc_semaphore(name))
                return used[-1]
            return stack, sb, ps, sem

        keep, sb, ps, sem = scope()
        top.enter_context(keep)
        X = sb("X", [P, TILES, D])
        ident = sb("ident", [P, P])
        identb = sb("identb", [P, P], bf16)
        mhalf = sb("mhalf", [P, G])
        maskrow = sb("maskrow", [1, BATCH, HEADS // 2, KV], bf16)
        onesrow = sb("onesrow", [1, P], bf16)

        HELD["waited"] = sem("waited")
        hidden = nc.dram_tensor("hidden", (TOKENS, D), fp32, kind="Internal").ap()
        made = nc.dram_tensor("made", (SLOTS * P, D), fp32, kind="Internal").ap()
        constants(nc, scope, ident, identb, mhalf, onesrow, maskrow, mask)
        attention, asb, _, _ = scope()
        with attention:
            KT = asb("KT", [P, PAIRS, BATCH * KV])
            VT = asb("VT", [P, PAIRS, BATCH * KV])
            kv_prep(nc, scope, KT, VT, ctxT, Wk, Wv, inv_temp)
            phase_a(nc, scope, X, x, ctxT, ctx, ident, mhalf)
            phase_b(nc, scope, X, rhs, identb, mhalf)
            phase_c(nc, scope, X, KT, VT, WqT, Wo, ident, mhalf, maskrow, onesrow)
        routing, rsb, _, _ = scope()
        with routing:
            R = Routing(rsb)
            W = rsb("expert_W", [P, EXPERTS, DC, D])
            for layer in range(LAYERS):
                route(nc, scope, R, layer, X, W, ident, mhalf, rwT, rb, ewT, hidden, made)
                experts(nc, scope, R, layer, W, ident, eb, hidden, made)
            combine(nc, scope, R, X, made, out)


def constants(nc, scope, ident, identb, mhalf, onesrow, maskrow, mask):
    stack, sb, ps, sem = scope()
    with stack:
        m8 = sb("m8", [1, BATCH, KV], u8)
        zeroed = sem("const_zeroed")
        made = sem("const_made")
        mask_in = sem("mask_in")
        block = stack.enter_context(nc.Block())

        @block.sync
        def _(sp):
            sp.dma_start(m8[0:1, :, :], mask.rearrange("(o b) s -> o b s", o=1)).then_inc(mask_in, 16)
            sp.wait_ge(mask_in, 16)

        @block.gpsimd
        def _(pool):
            pool.memset(ident[:, :], 0.0).then_inc(zeroed, 1)
            pool.memset(identb[:, :], 0.0).then_inc(zeroed, 1)
            pool.memset(mhalf[:, :], -0.5)
            pool.memset(onesrow[:, :], 1.0)
            pool.wait_ge(zeroed, 2)
            for m in (ident, identb):
                pool.affine_select(out=m[:, :], in_=m[:, :], compare_op=ALU.not_equal, fill=1.0, base=0,
                                   pattern=[[-1, P]], channel_multiplier=1).then_inc(made, 1)

        @block.vector
        def _(dve):
            dve.wait_ge(mask_in, 16)
            for n in range(HEADS // 2):
                dve.tensor_scalar(maskrow[0:1, :, n, :], m8[0:1, :, :], 1.0, -MASKED, ALU.subtract, ALU.mult)


def kv_prep(nc, scope, KT, VT, ctxT, Wk, Wv, inv_temp):
    stack, sb, ps, sem = scope()
    with stack:
        cT = sb("cT", [P, DC, BATCH * KV])
        wk = sb("wk", [P, DC, HEADS * DH])
        wv = sb("wv", [P, DC, HEADS * DH])
        it = sb("it", [P, PAIRS])
        it8 = sb("it8", [P, PAIRS])
        pk = ps("pk", [P, 2, 512])
        pv = ps("pv", [P, 2, 512])
        c_in = sem("c_in")
        wk_in = sem("wk_in")
        wv_in = sem("wv_in")
        it_in = sem("it_in")
        it_done = sem("it_done")
        k_mm = sem("k_mm")
        v_mm = sem("v_mm")
        k_out = sem("k_out")
        v_out = sem("v_out")
        block = stack.enter_context(nc.Block())

        @block.sync
        def _(sp):
            sp.dma_start(cT[:, :, :], ctxT.rearrange("(k p) n -> p k n", p=P)).then_inc(c_in, 16)
            sp.dma_start(wk[:, :, :], Wk.rearrange("(k p) n -> p k n", p=P)).then_inc(wk_in, 16)
            sp.dma_start(wv[:, :, :], Wv.rearrange("(k p) n -> p k n", p=P)).then_inc(wv_in, 16)
            sp.dma_start(it[:, :], inv_temp).then_inc(it_in, 16)

        @block.tensor
        def _(pe):
            pe.wait_ge(c_in, 16)
            pe.wait_ge(wk_in, 16)
            pe.wait_ge(wv_in, 16)
            for p in range(PAIRS):
                for w, acc, done, released in ((wk, pk, k_mm, k_out), (wv, pv, v_mm, v_out)):
                    free_slot(pe, released, p, 2)
                    for k in range(DC):
                        mm = pe.matmul(acc[:, p % 2, 0:BATCH * KV], w[:, k, p * P:(p + 1) * P], cT[:, k, :],
                                       start=(k == 0), stop=(k == DC - 1))
                    mm.then_inc(done, 1)

        @block.scalar
        def _(act):
            act.wait_ge(it_done, 1)
            for p in range(PAIRS):
                act.wait_ge(k_mm, p + 1)
                act.activation(KT[:, p, :], pk[:, p % 2, 0:BATCH * KV], ACT.Identity,
                               scale=it8[:, p:p + 1]).then_inc(k_out, 1)

        @block.vector
        def _(dve):
            dve.wait_ge(it_in, 16)
            dve.tensor_scalar(it8[:, :], it[:, :], DH ** -0.5, None, ALU.mult).then_inc(it_done, 1)
            for p in range(PAIRS):
                dve.wait_ge(v_mm, p + 1)
                dve.tensor_copy(VT[:, p, :], pv[:, p % 2, 0:BATCH * KV]).then_inc(v_out, 1)


def rstd_steps(pool, rstd, nmr, mv, mhalf, chain, base, done):
    pool.tensor_scalar(rstd, mv[:, :, 1], LN_EPS, None, ALU.add).then_inc(chain, 1)
    pool.tensor_scalar(nmr, mv[:, :, 0], -1.0, None, ALU.mult).then_inc(chain, 1)
    wait_for(pool, chain, base + 2)
    pool.tensor_tensor(rstd, rstd, mhalf, ALU.pow).then_inc(chain, 1)
    wait_for(pool, chain, base + 3)
    pool.tensor_tensor(nmr, nmr, rstd, ALU.mult).then_inc(done, 1)


def phase_a(nc, scope, X, x, ctxT, ctx, ident, mhalf):
    stack, sb, ps, sem = scope()
    with stack:
        DEEP = 4
        cT = sb("a_cT", [P, DC, BATCH * KV])
        cn = sb("a_cn", [KV, BATCH, D])
        bn = sb("a_bn", [P, DEEP, G, 6])
        mv = sb("a_mv", [P, DEEP, G, 2])
        rstd = sb("a_rstd", [P, DEEP, G])
        nmr = sb("a_nmr", [P, DEEP, G])
        y = sb("a_y", [P, 2, G, D])
        yT = sb("a_yT", [P, 2, G, DC, P])
        nmax = sb("a_nmax", [P, DEEP, G])
        probs = sb("a_probs", [P, DEEP, G, KV])
        Z = sb("a_Z", [P, DEEP, G])
        rZ = sb("a_rZ", [P, DEEP, G])
        pT = sb("a_pT", [KV, DEEP, G, P])
        psT = ps("a_psT", [P, G, DC, P])
        psS = ps("a_psS", [P, 2, 512])
        psP = ps("a_psP", [P, 2, 512])
        psO = ps("a_psO", [P, G, D])
        c_in = sem("a_c_in")
        x_in = [sem(f"a_x_in{n}") for n in range(DEEP)]
        bn_done = sem("a_bn_done")
        mv_done = sem("a_mv_done")
        chain = sem("a_chain")
        rstd_done = sem("a_rstd_done")
        y_done = sem("a_y_done")
        yT_mm = sem("a_yT_mm")
        yT_done = sem("a_yT_done")
        s_mm = sem("a_s_mm")
        nmax_done = sem("a_nmax_done")
        p_done = sem("a_p_done")
        pT_mm = sem("a_pT_mm")
        pT_done = sem("a_pT_done")
        rZ_done = sem("a_rZ_done")
        o_mm = sem("a_o_mm")
        x_done = sem("a_x_done")
        block = stack.enter_context(nc.Block())
        xv = x.rearrange("(t p) d -> p t d", p=P)
        S = psS[:, :, 0:G * KV].rearrange("p n (g s) -> p n g s", g=G)
        PT = psP[0:KV, :, 0:G * P].rearrange("p n (g s) -> p n g s", g=G)

        @block.sync
        def _(sp):
            sp.dma_start(cT[:, :, :], ctxT.rearrange("(k p) n -> p k n", p=P)).then_inc(c_in, 16)
            sp.dma_start(cn[:, :, :], ctx.rearrange("(b s) d -> s b d", b=BATCH)).then_inc(c_in, 16)

            def load(i, s):
                if not isinstance(i, int) or i >= DEEP:
                    wait_for(sp, x_in[s], (i // DEEP) * 16)
                sp.dma_start(X[:, bass.ds(i * G, G), :], xv[:, bass.ds(i * G, G), :]).then_inc(x_in[s], 16)

            pipeline(sp, GROUPS, [(0, load)], DEEP)

        @block.vector
        def _(dve):
            def stats(i, s):
                wait_for(dve, x_in[s], (i // DEEP + 1) * 16)
                free_slot(dve, rstd_done, i, DEEP)
                for g in range(G):
                    last = dve.bn_stats(bn[:, s, g, :], X[:, i * G + g, :])
                last.then_inc(bn_done, 1)
                wait_for(dve, bn_done, i + 1)
                for g in range(G):
                    last = dve.bn_aggr(mv[:, s, g, :], bn[:, s, g, :])
                last.then_inc(mv_done, 1)

            def row_max(i, s):
                wait_for(dve, s_mm, i + 1)
                free_slot(dve, p_done, i, DEEP)
                dve.tensor_reduce(nmax[:, s, :], S[:, s % 2, :, :], AX.X, ALU.max, negate=True).then_inc(nmax_done, 1)

            def inverse(i, s):
                wait_for(dve, p_done, i + 1)
                free_slot(dve, x_done, i, DEEP)
                dve.reciprocal(rZ[:, s, :], Z[:, s, :]).then_inc(rZ_done, 1)

            def residual(i, s):
                wait_for(dve, o_mm, i + 1)
                wait_for(dve, rZ_done, i + 1)
                for g in range(G):
                    xt = X[:, i * G + g, :]
                    last = dve.scalar_tensor_tensor(xt, psO[:, g, :], rZ[:, s, g:g + 1], xt, ALU.mult, ALU.add)
                last.then_inc(x_done, 1)

            pipeline(dve, GROUPS, [(4, row_max), (0, stats), (5, inverse), (6, residual)], DEEP)

        @block.gpsimd
        def _(pool):
            def rstds(i, s):
                wait_for(pool, mv_done, i + 1)
                free_slot(pool, y_done, i, DEEP)
                rstd_steps(pool, rstd[:, s, :], nmr[:, s, :], mv[:, s, :, :], mhalf[:, 0:G],
                           chain, i * 3, rstd_done)

            pipeline(pool, GROUPS, [(0, rstds)], DEEP)

        @block.scalar
        def _(act):
            def norm(i, s):
                wait_for(act, rstd_done, i + 1)
                free_slot(act, yT_mm, i, 2)
                for g in range(G):
                    last = act.activation(y[:, s % 2, g, :], X[:, i * G + g, :], ACT.Identity,
                                          bias=nmr[:, s, g:g + 1], scale=rstd[:, s, g:g + 1])
                last.then_inc(y_done, 1)

            def copy_yT(i, s):
                wait_for(act, yT_mm, i + 1)
                free_slot(act, s_mm, i, 2)
                act.activation(yT[:, s % 2, :, :, :], psT[:, :, :, :], ACT.Copy).then_inc(yT_done, 1)

            def exps(i, s):
                wait_for(act, nmax_done, i + 1)
                free_slot(act, pT_mm, i, DEEP)
                free_slot(act, rZ_done, i, DEEP)
                for g in range(G):
                    last = act.activation(probs[:, s, g, :], S[:, s % 2, g, :], ACT.Exp, bias=nmax[:, s, g:g + 1],
                                          accum_out=Z[:, s, g:g + 1])
                last.then_inc(p_done, 1)

            def copy_pT(i, s):
                wait_for(act, pT_mm, i + 1)
                free_slot(act, o_mm, i, DEEP)
                act.activation(pT[:, s, :, :], PT[:, s % 2, :, :], ACT.Copy).then_inc(pT_done, 1)

            pipeline(act, GROUPS, [(1, norm), (2, copy_yT), (4, exps), (5, copy_pT)], DEEP)

        @block.tensor
        def _(pe):
            pe.wait_ge(c_in, 32)

            def transpose_y(i, s):
                wait_for(pe, y_done, i + 1)
                free_slot(pe, yT_done, i, 1)
                for g in range(G):
                    for k in range(DC):
                        mm = pe.transpose(psT[:, g, k, :], y[:, s % 2, g, k * P:(k + 1) * P], ident[:, :])
                mm.then_inc(yT_mm, 1)

            def scores(i, s):
                wait_for(pe, yT_done, i + 1)
                free_slot(pe, p_done, i, 2)
                for g in range(G):
                    for k in range(DC):
                        mm = pe.matmul(S[:, s % 2, g, :], yT[:, s % 2, g, k, :],
                                       cT[:, k, bass.ds((i // GPB) * KV, KV)], start=(k == 0), stop=(k == DC - 1))
                mm.then_inc(s_mm, 1)

            def transpose_p(i, s):
                wait_for(pe, p_done, i + 1)
                free_slot(pe, pT_done, i, 2)
                for g in range(G):
                    mm = pe.transpose(PT[:, s % 2, g, :], probs[:, s, g, :], ident[:, :])
                mm.then_inc(pT_mm, 1)

            def values(i, s):
                wait_for(pe, pT_done, i + 1)
                free_slot(pe, x_done, i, 1)
                for g in range(G):
                    mm = pe.matmul(psO[:, g, :], pT[:, s, g, :], cn[:, i // GPB, :], start=True, stop=True)
                mm.then_inc(o_mm, 1)

            pipeline(pe, GROUPS, [(2, transpose_y), (5, transpose_p), (6, values), (3, scores)], DEEP)


def phase_b(nc, scope, X, rhs, identb, mhalf):
    stack, sb, ps, sem = scope()
    with stack:
        DEEP = 4
        w = sb("b_w", [P, DC, D])
        wabs = sb("b_wabs", [P, DC, D])
        wmax = sb("b_wmax", [P, D])
        wscale = sb("b_wscale", [P, D])
        winv = sb("b_winv", [P, D])
        wq = sb("b_wq", [P, DC, D], bf16)
        bn = sb("b_bn", [P, DEEP, G, 6])
        mv = sb("b_mv", [P, DEEP, G, 2])
        rstd = sb("b_rstd", [P, DEEP, G])
        nmr = sb("b_nmr", [P, DEEP, G])
        y = sb("b_y", [P, DEEP, G, D])
        amax = sb("b_amax", [P, DEEP, G])
        scale = sb("b_scale", [P, 2 * DEEP, G])
        inv = sb("b_inv", [P, DEEP, G])
        q = sb("b_q", [P, 2, G, D], bf16)
        qT = sb("b_qT", [P, 2, G, DC, P], bf16)
        delta = sb("b_delta", [P, 2, G, D])
        minus_round = sb("b_minus_round", [P, 1])
        psT = ps("b_psT", [P, 2, G, DC, P], bf16)
        psO = ps("b_psO", [P, 2, G, D])
        w_in = sem("b_w_in")
        w_chain = sem("b_w_chain")
        wmax_done = sem("b_wmax_done")
        wq_done = sem("b_wq_done")
        bn_done = sem("b_bn_done")
        mv_done = sem("b_mv_done")
        chain = sem("b_chain")
        rstd_done = sem("b_rstd_done")
        y_done = sem("b_y_done")
        amax_done = sem("b_amax_done")
        sc_chain = sem("b_sc_chain")
        v_done = sem("b_v_done")
        q_done = sem("b_q_done")
        qT_mm = sem("b_qT_mm")
        qT_done = sem("b_qT_done")
        o_mm = sem("b_o_mm")
        d_done = sem("b_d_done")
        x_done = sem("b_x_done")
        block = stack.enter_context(nc.Block())

        @block.sync
        def _(sp):
            sp.dma_start(w[:, :, :], rhs.rearrange("(k p) n -> p k n", p=P)).then_inc(w_in, 16)

        @block.vector
        def _(dve):
            dve.memset(minus_round[:, :], -ROUND).then_inc(w_chain, 1)
            dve.wait_ge(w_in, 16)
            dve.tensor_reduce(wabs[:, 0, :], w[:, :, :].rearrange("p k n -> p n k"), AX.X, ALU.max,
                              apply_absolute_value=True).then_inc(w_chain, 1)
            dve.wait_ge(wmax_done, 1)
            dve.tensor_scalar(wscale[:, :], wmax[:, :], 1e-12, 1.0 / INT8_MAX, ALU.max, ALU.mult).then_inc(w_chain, 1)
            dve.wait_ge(w_chain, 3)
            dve.reciprocal(winv[:, :], wscale[:, :]).then_inc(w_chain, 1)
            dve.wait_ge(w_chain, 4)
            for k in range(DC):
                dve.tensor_tensor(w[:, k, :], w[:, k, :], winv[:, :], ALU.mult).then_inc(w_chain, 1)
            dve.wait_ge(w_chain, 4 + DC)
            dve.tensor_scalar(w[:, :, :], w[:, :, :], INT8_MAX, -INT8_MAX, ALU.min, ALU.max).then_inc(w_chain, 1)
            dve.wait_ge(w_chain, 5 + DC)
            dve.tensor_scalar(w[:, :, :], w[:, :, :], ROUND, None, ALU.add).then_inc(w_chain, 1)
            dve.wait_ge(w_chain, 6 + DC)
            dve.tensor_scalar(wq[:, :, :], w[:, :, :], -ROUND, None, ALU.add).then_inc(wq_done, 1)

            def stats(i, s):
                free_slot(dve, rstd_done, i, DEEP)
                for g in range(G):
                    last = dve.bn_stats(bn[:, s, g, :], X[:, i * G + g, :])
                last.then_inc(bn_done, 1)
                wait_for(dve, bn_done, i + 1)
                for g in range(G):
                    last = dve.bn_aggr(mv[:, s, g, :], bn[:, s, g, :])
                last.then_inc(mv_done, 1)

            def quantize(i, s):
                wait_for(dve, y_done, i + 1)
                dve.tensor_reduce(amax[:, s, :], y[:, s, :, :], AX.X, ALU.max,
                                  apply_absolute_value=True).then_inc(sc_chain, 1)
                wait_for(dve, sc_chain, i * 4 + 1)
                dve.tensor_scalar(scale[:, i % (2 * DEEP), :], amax[:, s, :], 1e-12, 1.0 / INT8_MAX, ALU.max,
                                  ALU.mult).then_inc(sc_chain, 1)
                wait_for(dve, sc_chain, i * 4 + 2)
                dve.reciprocal(inv[:, s, :], scale[:, i % (2 * DEEP), :]).then_inc(sc_chain, 1)
                wait_for(dve, sc_chain, i * 4 + 3)
                for g in range(G):
                    yt = y[:, s, g, :]
                    last = dve.tensor_scalar(yt, yt, inv[:, s, g:g + 1], INT8_MAX, ALU.mult, ALU.min)
                last.then_inc(sc_chain, 1)
                wait_for(dve, sc_chain, i * 4 + 4)
                dve.tensor_scalar(y[:, s, :, :], y[:, s, :, :], -INT8_MAX, ROUND, ALU.max,
                                  ALU.add).then_inc(v_done, 1)

            def rescale(i, s):
                wait_for(dve, o_mm, i + 1)
                free_slot(dve, x_done, i, 2)
                for g in range(G):
                    last = dve.scalar_tensor_tensor(delta[:, s % 2, g, :], psO[:, s % 2, g, :],
                                                    scale[:, i % (2 * DEEP), g:g + 1], wscale[:, :], ALU.mult, ALU.mult)
                last.then_inc(d_done, 1)

            pipeline(dve, GROUPS, [(0, stats), (5, rescale), (2, quantize)], DEEP)

        @block.gpsimd
        def _(pool):
            pool.wait_ge(w_chain, 2)
            pool.partition_all_reduce(wmax[:, :], wabs[:, 0, :], P, bass.bass_isa.ReduceOp.max).then_inc(wmax_done, 1)

            def rstds(i, s):
                wait_for(pool, mv_done, i + 1)
                free_slot(pool, y_done, i, DEEP)
                rstd_steps(pool, rstd[:, s, :], nmr[:, s, :], mv[:, s, :, :], mhalf[:, 0:G],
                           chain, i * 3, rstd_done)

            def residual(i, s):
                wait_for(pool, d_done, i + 1)
                xt = X[:, bass.ds(i * G, G), :]
                pool.tensor_tensor(xt, delta[:, s % 2, :, :], xt, ALU.add).then_inc(x_done, 1)

            pipeline(pool, GROUPS, [(6, residual), (0, rstds)], DEEP)

        @block.scalar
        def _(act):
            def norm(i, s):
                wait_for(act, rstd_done, i + 1)
                free_slot(act, q_done, i, DEEP)
                for g in range(G):
                    last = act.activation(y[:, s, g, :], X[:, i * G + g, :], ACT.Identity,
                                          bias=nmr[:, s, g:g + 1], scale=rstd[:, s, g:g + 1])
                last.then_inc(y_done, 1)

            def unround(i, s):
                wait_for(act, v_done, i + 1)
                free_slot(act, qT_mm, i, 2)
                act.activation(q[:, s % 2, :, :], y[:, s, :, :], ACT.Identity,
                               bias=minus_round[:, :]).then_inc(q_done, 1)

            def copy_qT(i, s):
                wait_for(act, qT_mm, i + 1)
                free_slot(act, o_mm, i, 2)
                act.activation(qT[:, s % 2, :, :, :], psT[:, s % 2, :, :, :], ACT.Copy).then_inc(qT_done, 1)

            act.wait_ge(w_chain, 1)
            pipeline(act, GROUPS, [(1, norm), (4, copy_qT), (3, unround)], DEEP)

        @block.tensor
        def _(pe):
            pe.wait_ge(wq_done, 1)

            def transpose_q(i, s):
                wait_for(pe, q_done, i + 1)
                free_slot(pe, qT_done, i, 2)
                for g in range(G):
                    for k in range(DC):
                        mm = pe.transpose(psT[:, s % 2, g, k, :], q[:, s % 2, g, k * P:(k + 1) * P], identb[:, :])
                mm.then_inc(qT_mm, 1)

            def product(i, s):
                wait_for(pe, qT_done, i + 1)
                free_slot(pe, d_done, i, 2)
                for g in range(G):
                    for k in range(DC):
                        mm = pe.matmul(psO[:, s % 2, g, :], qT[:, s % 2, g, k, :], wq[:, k, :],
                                       start=(k == 0), stop=(k == DC - 1))
                mm.then_inc(o_mm, 1)

            pipeline(pe, GROUPS, [(4, transpose_q), (4, product)], DEEP)


def phase_c(nc, scope, X, KT, VT, WqT, Wo, ident, mhalf, maskrow, onesrow):
    stack, sb, ps, sem = scope()
    with stack:
        HK = KV // 2
        M = sb("c_M", [P, 2, DC, HEADS * KV])
        U = sb("c_U", [P, 2, PAIRS, D])
        wq = sb("c_wq", [P, 2, D])
        KB = sb("c_KB", [P, 2, P])
        VB = sb("c_VB", [P, 2, P])
        wo = sb("c_wo", [P, 2, D])
        bn = sb("c_bn", [P, 2, 1, 6])
        mv = sb("c_mv", [P, 2, 1, 2])
        rstd = sb("c_rstd", [P, 2, 1])
        nmr = sb("c_nmr", [P, 2, 1])
        y = sb("c_y", [P, D])
        yT = sb("c_yT", [P, 2, DC, P])
        S = sb("c_S", [P, 2, HEADS, KV])
        nmax = sb("c_nmax", [P, HEADS])
        SN = sb("c_SN", [P, HEADS, HK])
        W = sb("c_W", [P, 2, HEADS, HK])
        top = sb("c_top", [P, 2, HEADS, HK // 2 + 1])
        cut = sb("c_cut", [P, HEADS, HK // 2 + 1])
        least = sb("c_least", [P, HEADS])
        E = sb("c_E", [P, 2, HEADS, KV])
        Z = sb("c_Z", [P, HEADS])
        kept = sb("c_kept", [P, HEADS])
        den = sb("c_den", [P, HEADS])
        rden = sb("c_rden", [P, HEADS])
        aT = sb("c_aT", [P, PAIRS, P])
        psY = ps("c_psY", [P, DC, P])
        psS = ps("c_psS", [P, HEADS, KV])
        psA = ps("c_psA", [P, PAIRS, P])
        psO = ps("c_psO", [P, D])
        psM = ps("c_psM", [P, DC, P])
        psU = ps("c_psU", [P, D])
        wq_in = [sem(f"c_wq_in{n}") for n in range(2)]
        wo_in = [sem(f"c_wo_in{n}") for n in range(2)]
        blocks_zero = sem("c_blocks_zero")
        kb_done = sem("c_kb_done")
        vb_done = sem("c_vb_done")
        m_mm = sem("c_m_mm")
        m_done = sem("c_m_done")
        u_mm = sem("c_u_mm")
        u_done = sem("c_u_done")
        bn_done = sem("c_bn_done")
        mv_done = sem("c_mv_done")
        chain = sem("c_chain")
        rstd_done = sem("c_rstd_done")
        y_done = sem("c_y_done")
        yT_mm = sem("c_yT_mm")
        yT_done = sem("c_yT_done")
        s_mm = sem("c_s_mm")
        s_done = sem("c_s_done")
        pads_done = sem("c_pads_done")
        topk = sem("c_topk")
        e_done = sem("c_e_done")
        kept_done = sem("c_kept_done")
        den_chain = sem("c_den_chain")
        den_done = sem("c_den_done")
        rden_done = sem("c_rden_done")
        a_done = sem("c_a_done")
        aT_mm = sem("c_aT_mm")
        aT_done = sem("c_aT_done")
        o_mm = sem("c_o_mm")
        x_done = sem("c_x_done")
        block = stack.enter_context(nc.Block())
        HALF = HEADS // 2
        STEPS = 11
        PREPS = BATCH * PAIRS

        @block.sync
        def _(sp):
            def load_wq(u, s):
                free_slot(sp, m_mm, u, 2)
                sp.dma_start(wq[:, s, :], WqT[bass.ds((u % PAIRS) * P, P), :]).then_inc(wq_in[s], 16)

            def load_wo(u, s):
                free_slot(sp, u_mm, u, 2)
                sp.dma_start(wo[:, s, :], Wo[bass.ds((u % PAIRS) * P, P), :]).then_inc(wo_in[s], 16)

            pipeline(sp, PREPS, [(-8, load_wq), (-5, load_wo)])

        @block.vector
        def _(dve):
            def stats(t, s):
                free_slot(dve, rstd_done, t, 2)
                dve.bn_stats(bn[:, s, 0, :], X[:, t, :]).then_inc(bn_done, 1)
                wait_for(dve, bn_done, t + 1)
                dve.bn_aggr(mv[:, s, 0, :], bn[:, s, 0, :]).then_inc(mv_done, 1)

            def residual(t, s):
                wait_for(dve, o_mm, t + 1)
                dve.tensor_tensor(X[:, t, :], psO[:, :], X[:, t, :], ALU.add).then_inc(x_done, 1)

            def eights(first, step):
                for n in range(2):
                    wait_for(dve, topk, first + 2 * step + n + 2)
                    for h in range(HEADS):
                        at = n + 8 * (step // 2)
                        eight = top[:, n, h, at:at + 8]
                        if step == 1:
                            last = dve.match_replace(W[:, n, h, :], eight, W[:, n, h, :], TAKEN)
                        else:
                            last = dve.max(eight, W[:, n, h, :])
                    last.then_inc(topk, 1)

            def pair(t, s):
                first = t * STEPS
                wait_for(dve, s_done, t + 1)
                free_slot(dve, e_done, t, 1)
                low, neg_high = S[:, s, :, 0:HK], SN[:, :, :]
                dve.scalar_tensor_tensor(W[:, 0, :, :], low, -1.0, neg_high, ALU.mult, ALU.min).then_inc(topk, 1)
                dve.scalar_tensor_tensor(W[:, 1, :, :], neg_high, -1.0, low, ALU.mult, ALU.min).then_inc(topk, 1)
                wait_for(dve, topk, first + 1)
                dve.tensor_reduce(nmax[:, :], W[:, 0, :, :], AX.X, ALU.min).then_inc(topk, 1)
                eights(first, 0)

            def select(t, s):
                first = t * STEPS
                eights(first, 1)
                eights(first, 2)
                wait_for(dve, topk, first + 9)
                dve.scalar_tensor_tensor(cut[:, :, :], top[:, 0, :, :], -1.0, top[:, 1, :, :], ALU.mult,
                                         ALU.min).then_inc(topk, 1)
                wait_for(dve, topk, first + 10)
                dve.tensor_reduce(least[:, :], cut[:, :, :], AX.X, ALU.max).then_inc(topk, 1)

            def keep_top(t, s):
                wait_for(dve, e_done, t + 1)
                wait_for(dve, topk, (t + 1) * STEPS)
                free_slot(dve, den_done, t, 1)
                for h in range(HEADS):
                    e = E[:, s, h, :]
                    last = dve.scalar_tensor_tensor(e, S[:, s, h, :], least[:, h:h + 1], e,
                                                    ALU.is_ge, ALU.mult, accum_out=kept[:, h:h + 1])
                last.then_inc(kept_done, 1)

            def inverse(t, s):
                wait_for(dve, den_done, t + 1)
                free_slot(dve, a_done, t, 1)
                dve.reciprocal(rden[:, :], den[:, :]).then_inc(rden_done, 1)

            dve.memset(top[:, 0, :, HK // 2:], TAKEN).then_inc(pads_done, 1)
            dve.memset(top[:, 1, :, 0:1], -TAKEN).then_inc(pads_done, 1)
            dve.wait_ge(pads_done, 2)
            pipeline(dve, TILES, [(0, stats), (3, pair), (6, residual), (4, inverse), (3, select), (3, keep_top)])

        @block.gpsimd
        def _(pool):
            def rstds(t, s):
                wait_for(pool, mv_done, t + 1)
                free_slot(pool, y_done, t, 2)
                rstd_steps(pool, rstd[:, s, :], nmr[:, s, :], mv[:, s, :, :], mhalf[:, 0:1],
                           chain, t * 3, rstd_done)

            def denominator(t, s):
                wait_for(pool, kept_done, t + 1)
                free_slot(pool, rden_done, t, 1)
                pool.tensor_scalar(den[:, :], Z[:, :], NORM_EPS, None, ALU.mult).then_inc(den_chain, 1)
                wait_for(pool, den_chain, t + 1)
                pool.tensor_tensor(den[:, :], den[:, :], kept[:, :], ALU.add).then_inc(den_done, 1)

            def normalize(t, s):
                wait_for(pool, rden_done, t + 1)
                e = E[:, s, :, :]
                pool.tensor_tensor(e, e, rden[:, :].unsqueeze(2).to_broadcast([P, HEADS, KV]), ALU.mult).then_inc(a_done, 1)

            pool.memset(KB[:, :, :], 0.0).then_inc(blocks_zero, 1)
            pool.memset(VB[:, :, :], 0.0).then_inc(blocks_zero, 1)
            pipeline(pool, TILES, [(0, rstds), (4, normalize), (3, denominator)])

        @block.scalar
        def _(act):
            def norm(t, s):
                wait_for(act, rstd_done, t + 1)
                free_slot(act, yT_mm, t, 1)
                act.activation(y[:, :], X[:, t, :], ACT.Identity, bias=nmr[:, s, :],
                               scale=rstd[:, s, :]).then_inc(y_done, 1)

            def copy_yT(t, s):
                wait_for(act, yT_mm, t + 1)
                free_slot(act, s_mm, t, 2)
                act.activation(yT[:, s, :, :], psY[:, :, :], ACT.Copy).then_inc(yT_done, 1)

            def copy_M(u, s):
                wait_for(act, m_mm, u + 1)
                act.activation(M[:, (u // PAIRS) % 2, :, bass.ds((u % PAIRS) * P, P)], psM[:, :, :],
                               ACT.Copy).then_inc(m_done, 1)

            def copy_U(u, s):
                wait_for(act, u_mm, u + 1)
                act.activation(U[:, (u // PAIRS) % 2, u % PAIRS, :], psU[:, :], ACT.Copy).then_inc(u_done, 1)

            def exps(t, s):
                wait_for(act, topk, t * STEPS + 3)
                free_slot(act, den_done, t, 1)
                free_slot(act, aT_mm, t, 2)
                for h in range(HEADS):
                    last = act.activation(E[:, s, h, :], S[:, s, h, :], ACT.Exp, bias=nmax[:, h:h + 1],
                                          accum_out=Z[:, h:h + 1])
                last.then_inc(e_done, 1)

            def copy_aT(t, s):
                wait_for(act, aT_mm, t + 1)
                free_slot(act, o_mm, t, 1)
                act.activation(aT[:, :, :], psA[:, :, :], ACT.Copy).then_inc(aT_done, 1)

            def copy_S(t, s):
                wait_for(act, s_mm, t + 1)
                free_slot(act, kept_done, t, 2)
                if not isinstance(t, int) or t >= 1:
                    wait_for(act, topk, t * STEPS - 9)
                act.activation(SN[:, :, :], psS[:, :, HK:], ACT.Copy, scale=-1.0)
                act.activation(S[:, s, :, :], psS[:, :, :], ACT.Copy).then_inc(s_done, 1)

            def spread(u, s, T, B, used, done):
                free_slot(act, used, u, 2)
                for h in range(2):
                    at = slice(h * DH, (h + 1) * DH)
                    last = act.activation(B[at, s, at], T[at, u % PAIRS, bass.ds((u // PAIRS) * KV, KV)],
                                          ACT.Copy)
                last.then_inc(done, 1)

            def spread_K(u, s):
                spread(u, s, KT, KB, m_mm, kb_done)

            def spread_V(u, s):
                spread(u, s, VT, VB, u_mm, vb_done)

            act.wait_ge(blocks_zero, 2)
            pipeline(act, TILES, [(5, copy_aT), (-8, spread_K), (-5, spread_V), (1, norm), (3, exps), (2, copy_S),
                                  (1, copy_yT), (-7, copy_M), (-4, copy_U)])

        @block.tensor
        def _(pe):
            def scores(t, s):
                wait_for(pe, yT_done, t + 1)
                wait_for(pe, m_done, (t // TPB) * PAIRS + PAIRS)
                free_slot(pe, s_done, t, 1)
                for n in range(2):
                    half = psS[:, n * HALF:(n + 1) * HALF, :]
                    pe.matmul(half, onesrow[:, :], maskrow[:, t // TPB, :, :], start=True, stop=False)
                    for k in range(DC):
                        mm = pe.matmul(half, yT[:, s, k, :], M[:, (t // TPB) % 2, k, n * 512:(n + 1) * 512],
                                       start=False, stop=(k == DC - 1))
                mm.then_inc(s_mm, 1)

            def make_M(u, s):
                wait_for(pe, wq_in[s], (u // 2 + 1) * 16)
                free_slot(pe, m_done, u, 1)
                wait_for(pe, kb_done, u + 1)
                for k in range(DC):
                    mm = pe.matmul(psM[:, k, :], wq[:, s, k * P:(k + 1) * P], KB[:, s, :], start=True, stop=True)
                mm.then_inc(m_mm, 1)

            def make_U(u, s):
                wait_for(pe, wo_in[s], (u // 2 + 1) * 16)
                free_slot(pe, u_done, u, 1)
                wait_for(pe, vb_done, u + 1)
                pe.matmul(psU[:, :], VB[:, s, :], wo[:, s, :],
                          start=True, stop=True).then_inc(u_mm, 1)

            def transpose_y(t, s):
                wait_for(pe, y_done, t + 1)
                free_slot(pe, yT_done, t, 1)
                for k in range(DC):
                    mm = pe.transpose(psY[:, k, :], y[:, k * P:(k + 1) * P], ident[:, :])
                mm.then_inc(yT_mm, 1)

            def transpose_a(t, s):
                wait_for(pe, a_done, t + 1)
                free_slot(pe, aT_done, t, 1)
                a = E[:, s, :, :].rearrange("p h s -> p (h s)")
                for n in range(PAIRS):
                    mm = pe.transpose(psA[:, n, :], a[:, n * P:(n + 1) * P], ident[:, :])
                mm.then_inc(aT_mm, 1)

            def values(t, s):
                wait_for(pe, aT_done, t + 1)
                wait_for(pe, u_done, (t // TPB) * PAIRS + PAIRS)
                free_slot(pe, x_done, t, 1)
                for n in range(PAIRS):
                    mm = pe.matmul(psO[:, :], aT[:, n, :], U[:, (t // TPB) % 2, n, :],
                                   start=(n == 0), stop=(n == PAIRS - 1))
                mm.then_inc(o_mm, 1)

            pipeline(pe, TILES, [(5, transpose_a), (2, scores), (5, values), (1, transpose_y), (-7, make_M),
                                 (-4, make_U)])


class Routing:

    def __init__(self, sb):
        self.tri = sb("r_tri", [P, P], bf16)
        self.ones = sb("r_ones", [P, P], bf16)
        self.eid = sb("r_eid", [P, EXPERTS])
        self.follows = sb("r_follows", [P, EXPERTS, TILES])
        self.token = sb("r_token", [P, TILES])
        self.lane = sb("r_lane", [P, P], fp16)
        self.first = sb("r_first", [P, SLOTS], fp16)
        self.pos = sb("r_pos", [P, TILES, CHOICES], u32)
        self.tokens = sb("r_tokens", [P, SLOTS], u32)
        self.expert_of = sb("r_expert_of", [1, SLOTS], i32)


def gather_rows(pool, done, R, t, s, idx, picked, rows, made):
    pool.tensor_copy(idx[:, s, :, :], R.pos[:, bass.ds(t * G, G), :]).then_inc(picked, 1)
    wait_for(pool, picked, t + 1)
    for g in range(G):
        for c in range(CHOICES):
            pool.indirect_dma_start(rows[:, s, g, c, :], None, made,
                                    bass.IndirectOffsetOnAxis(ap=idx[:, s, g, c:c + 1], axis=0)).then_inc(done[s], 16)


def route(nc, scope, R, layer, X, W, ident, mhalf, rwT, rb, ewT, hidden, made):
    stack, sb, ps, sem = scope(recycle=True)
    with stack:
        L = f"r{layer}_"
        DEEP = 4
        PICKS = TILES * CHOICES
        CHUNK = 8
        CHUNKS = PICKS // CHUNK
        rw = sb(L + "rw", [P, DC, EXPERTS])
        rbc = sb(L + "rbc", [EXPERTS, 1])
        logT = sb(L + "logT", [EXPERTS, 2, G, P])
        rows = sb(L + "rows", [P, DEEP, G, CHOICES, D])
        h = rows[:, :, :, 0, :]
        hT = sb(L + "hT", [P, 2, G, DC, P])
        logits = sb(L + "logits", [P, TILES, EXPERTS])
        best = sb(L + "best", [P, TILES, 8])
        which = sb(L + "which", [P, TILES, 8], u32)
        whichf = sb(L + "whichf", [P, TILES, CHOICES])
        hot = sb(L + "hot", [P, TILES, CHOICES, EXPERTS])
        chosen = sb(L + "chosen", [P, TILES, EXPERTS], bf16)
        perm = sb(L + "perm", [P, EXPERTS, TILES])
        upto = sb(L + "upto", [P, EXPERTS, TILES])
        row = sb(L + "row", [P, TILES, EXPERTS])
        n_pad = sb(L + "n_pad", [P, EXPERTS], i32)
        n_cut = sb(L + "n_cut", [P, EXPERTS], i32)
        filled = sb(L + "filled", [P, EXPERTS])
        one = sb(L + "one", [P, EXPERTS])
        ends = sb(L + "ends", [P, EXPERTS])
        starts = sb(L + "starts", [P, EXPERTS])
        past = sb(L + "past", [1, SLOTS, EXPERTS])
        npast = sb(L + "npast", [1, SLOTS])
        rowf = sb(L + "rowf", [P, PICKS])
        lane_i = sb(L + "lane_i", [P, PICKS], u32)
        lane_f = sb(L + "lane_f", [P, PICKS])
        tile_f = sb(L + "tile_f", [P, PICKS])
        lane_hot = sb(L + "lane_hot", [P, 2, CHUNK, P], fp16)
        slot_hot = sb(L + "slot_hot", [P, 2, CHUNK, SLOTS], fp16)
        slot_tok = sb(L + "slot_tok", [P, 2, CHUNK, SLOTS], fp16)
        psT = ps(L + "psT", [P, 2, G, DC, P])
        psL = ps(L + "psL", [P, 512])
        psE = ps(L + "psE", [P, 512])
        psR = ps(L + "psR", [P, 2, TILES * EXPERTS])
        psI = ps(L + "psI", [P, 512])
        made_const = sem(L + "const")
        w_in = sem(L + "w_in")
        W_in = sem(L + "W_in")
        h_done = sem(L + "h_done")
        h_out = [sem(L + f"h_out{n}") for n in range(DEEP)]
        hT_mm = sem(L + "hT_mm")
        hT_done = sem(L + "hT_done")
        l_mm = sem(L + "l_mm")
        l_done = sem(L + "l_done")
        turned = sem(L + "turned")
        top = sem(L + "top")
        chosen_done = sem(L + "chosen_done")
        n_mm = sem(L + "n_mm")
        c = sem(L + "chain")
        slot_done = sem(L + "slot_done")
        i_mm = sem(L + "i_mm")
        LG = psL[:, 0:TILES * EXPERTS].rearrange("p (t e) -> p t e", t=TILES)
        LT = psE[0:EXPERTS, 0:G * P].rearrange("e (g p) -> e g p", g=G)
        RW = psR[:, 0, :].rearrange("p (t e) -> p t e", t=TILES)
        NT = psR[:, 1, :].rearrange("p (t e) -> p t e", t=TILES)
        if layer == 0:
            bn = sb(L + "bn", [P, DEEP, G, 6])
            mv = sb(L + "mv", [P, DEEP, G, 2])
            rstd = sb(L + "rstd", [P, DEEP, G])
            nmr = sb(L + "nmr", [P, DEEP, G])
            bn_done = sem(L + "bn_done")
            mv_done = sem(L + "mv_done")
            chain = sem(L + "rstd_chain")
            rstd_done = sem(L + "rstd_done")
        else:
            idx = sb(L + "idx", [P, DEEP, G, CHOICES], u32)
            picked = sem(L + "picked")
            rows_in = [sem(L + f"rows_in{n}") for n in range(DEEP)]
        block = stack.enter_context(nc.Block())
        hv = hidden.rearrange("(t p) d -> p t d", p=P)

        def free_rows(eng, i, s):
            free_slot(eng, hT_mm, i, DEEP)
            if not isinstance(i, int) or i >= DEEP:
                wait_for(eng, h_out[s], (i // DEEP) * 16)

        @block.sync
        def _(sp):
            sp.dma_start(rw[:, :, :], rwT[layer].rearrange("(k p) e -> p k e", p=P)).then_inc(w_in, 16)
            sp.dma_start(rbc[:, :], rb[layer:layer + 1, :].rearrange("o e -> e o")).then_inc(w_in, 16)

            def store_h(i, s):
                wait_for(sp, h_done, i + 1)
                sp.dma_start(hv[:, bass.ds(i * G, G), :], h[:, s, :, :]).then_inc(h_out[s], 16)

            def load_W(i, s):
                if s % 2 == 0:
                    e = i // 2
                    sp.dma_start(W[:, bass.ds(e, 1), :, :],
                                 ewT[layer][bass.ds(e, 1), :, :].rearrange("e (k p) n -> p e k n", p=P)).then_inc(W_in, 16)

            pipeline(sp, GROUPS, [(0, store_h), (0, load_W)], DEEP)
            for n in range(DEEP):
                sp.wait_ge(h_out[n], GROUPS // DEEP * 16)
            sp.wait_ge(W_in, EXPERTS * 16)

        @block.vector
        def _(dve):
            def stats(i, s):
                free_slot(dve, rstd_done, i, DEEP)
                for g in range(G):
                    last = dve.bn_stats(bn[:, s, g, :], X[:, i * G + g, :])
                last.then_inc(bn_done, 1)
                wait_for(dve, bn_done, i + 1)
                for g in range(G):
                    last = dve.bn_aggr(mv[:, s, g, :], bn[:, s, g, :])
                last.then_inc(mv_done, 1)

            def add_outputs(i, s):
                wait_for(dve, rows_in[s], (i // DEEP + 1) * (G * CHOICES * 16))
                dve.tensor_tensor(h[:, s, :, :], rows[:, s, :, 0, :], rows[:, s, :, 1, :], ALU.add).then_inc(h_done, 1)

            def spread(values, shape, axis):
                return values.unsqueeze(axis).to_broadcast(shape)

            dve.memset(one[:, :], 1.0).then_inc(c, 1)
            pipeline(dve, GROUPS, [(0, stats if layer == 0 else add_outputs)], DEEP)

            dve.wait_ge(turned, GROUPS)
            dve.tensor_copy(logits[:, :, :], LG).then_inc(top, 1)
            dve.wait_ge(top, 1)
            for t in range(TILES):
                last = dve.max(best[:, t, :], logits[:, t, :])
            last.then_inc(top, 1)
            dve.wait_ge(top, 2)
            for t in range(TILES):
                last = dve.max_index(which[:, t, :], best[:, t, :], logits[:, t, :])
            last.then_inc(top, 1)
            dve.wait_ge(top, 3)
            dve.tensor_copy(whichf[:, :, :], which[:, :, 0:CHOICES]).then_inc(top, 1)
            dve.wait_ge(top, 4)
            shape = [P, PICKS, EXPERTS]
            dve.tensor_tensor(hot[:, :, :, :].rearrange("p t c e -> p (t c) e"), spread(R.eid[:, :], shape, 1),
                              spread(whichf[:, :, :].rearrange("p t c -> p (t c)"), shape, 2),
                              ALU.is_equal).then_inc(top, 1)
            dve.wait_ge(top, 5)
            dve.tensor_tensor(chosen[:, :, :], hot[:, :, 0, :], hot[:, :, 1, :], ALU.add).then_inc(chosen_done, 1)

            dve.wait_ge(n_mm, 1)
            dve.tensor_copy(perm[:, :, :], NT.rearrange("p t e -> p e t")).then_inc(c, 1)
            dve.wait_ge(c, 2)
            dve.tensor_tensor_scan(upto[:, :, :].rearrange("p e t -> p (e t)"),
                                   R.follows[:, :, :].rearrange("p e t -> p (e t)"),
                                   perm[:, :, :].rearrange("p e t -> p (e t)"), 0.0, ALU.mult, ALU.add).then_inc(c, 1)
            dve.wait_ge(c, 3)
            dve.tensor_scalar(n_pad[:, :], upto[:, :, TILES - 1], float(P - 1), None, ALU.add).then_inc(c, 1)
            dve.tensor_tensor(perm[:, :, :], upto[:, :, :], perm[:, :, :], ALU.subtract).then_inc(c, 1)
            dve.wait_ge(c, 4)
            dve.tensor_scalar(n_cut[:, :], n_pad[:, :], -P, None, ALU.bitwise_and).then_inc(c, 1)
            dve.wait_ge(c, 6)
            dve.tensor_copy(filled[:, :], n_cut[:, :]).then_inc(c, 1)
            dve.wait_ge(c, 7)
            dve.tensor_tensor_scan(ends[:, :], one[:, :], filled[:, :], 0.0, ALU.mult, ALU.add).then_inc(c, 1)
            dve.wait_ge(c, 8)
            dve.tensor_tensor(starts[:, :], ends[:, :], filled[:, :], ALU.subtract).then_inc(c, 1)
            shape = [1, SLOTS, EXPERTS]
            dve.tensor_tensor(past[:, :, :], spread(ends[0:1, :], shape, 1), spread(R.first[0:1, :], shape, 2),
                              ALU.is_le).then_inc(c, 1)
            dve.wait_ge(c, 9)
            dve.tensor_tensor(perm[:, :, :], perm[:, :, :], spread(starts[:, :], [P, EXPERTS, TILES], 2),
                              ALU.add).then_inc(c, 1)
            dve.wait_ge(c, 11)
            dve.tensor_tensor(row[:, :, :], RW, perm[:, :, :].rearrange("p e t -> p t e"), ALU.add).then_inc(c, 1)
            dve.wait_ge(c, 12)
            for n in range(CHOICES):
                dve.tensor_tensor(hot[:, :, n, :], hot[:, :, n, :], row[:, :, :], ALU.mult).then_inc(c, 1)
            dve.wait_ge(c, 12 + CHOICES)
            dve.tensor_reduce(rowf[:, :], hot[:, :, :, :].rearrange("p t c e -> p (t c) e"), AX.X, ALU.add).then_inc(c, 1)
            dve.wait_ge(c, 13 + CHOICES)
            dve.tensor_copy(R.pos[:, :, :].rearrange("p t c -> p (t c)"), rowf[:, :]).then_inc(c, 1)
            dve.wait_ge(c, 14 + CHOICES)
            dve.tensor_scalar(lane_i[:, :], R.pos[:, :, :].rearrange("p t c -> p (t c)"), P - 1, None,
                              ALU.bitwise_and).then_inc(c, 1)
            dve.wait_ge(c, 15 + CHOICES)
            dve.tensor_copy(lane_f[:, :], lane_i[:, :]).then_inc(c, 1)
            dve.wait_ge(c, 16 + CHOICES)
            dve.tensor_tensor(tile_f[:, :], rowf[:, :], lane_f[:, :], ALU.subtract).then_inc(c, 1)
            dve.wait_ge(c, 17 + CHOICES)
            for n in range(CHUNKS):
                free_slot(dve, i_mm, n, 2)
                part = slice(n * CHUNK, (n + 1) * CHUNK)
                shape = [P, CHUNK, SLOTS]
                numbers = R.token[:, n * CHUNK // CHOICES:(n + 1) * CHUNK // CHOICES]
                dve.tensor_tensor(slot_hot[:, n % 2, :, :], spread(R.first[:, :], shape, 1),
                                  spread(tile_f[:, part], shape, 2), ALU.is_equal).then_inc(slot_done, 1)
                dve.tensor_tensor(lane_hot[:, n % 2, :, :], spread(R.lane[:, :], [P, CHUNK, P], 1),
                                  spread(lane_f[:, part], [P, CHUNK, P], 2), ALU.is_equal)
                dve.wait_ge(slot_done, 2 * n + 1)
                each = [P, CHUNK // CHOICES, CHOICES, SLOTS]
                dve.tensor_tensor(slot_tok[:, n % 2, :, :].rearrange("p (t c) s -> p t c s", c=CHOICES),
                                  slot_hot[:, n % 2, :, :].rearrange("p (t c) s -> p t c s", c=CHOICES),
                                  numbers.unsqueeze(2).unsqueeze(3).to_broadcast(each), ALU.mult).then_inc(slot_done, 1)
            dve.tensor_reduce(npast[:, :], past[:, :, :], AX.X, ALU.add).then_inc(c, 1)
            dve.wait_ge(c, 18 + CHOICES)
            dve.tensor_scalar(R.expert_of[:, :], npast[:, :], float(EXPERTS - 1), None, ALU.min)
            dve.wait_ge(i_mm, CHUNKS)
            dve.tensor_scalar(R.tokens[:, :], psI[:, 0:SLOTS], float(TOKEN_ZERO), None, ALU.add)

        @block.gpsimd
        def _(pool):
            if layer == 0:
                pool.memset(R.ones[:, :], 1.0).then_inc(made_const, 1)
                pool.memset(R.follows[:, :, :], 1.0).then_inc(made_const, 1)
                for out, step, size, base, lane in ((R.eid, 1, EXPERTS, 0, 0), (R.token, P, TILES, -TOKEN_ZERO, 1),
                                                    (R.lane, 1, P, 0, 0), (R.first, P, SLOTS, 0, 0)):
                    pool.iota(out[:, :], [[step, size]], base=base, channel_multiplier=lane,
                              allow_small_or_imprecise_dtypes=True).then_inc(made_const, 1)
                pool.wait_ge(made_const, 6)
                pool.affine_select(out=R.tri[:, :], in_=R.ones[:, :], compare_op=ALU.is_gt, fill=0.0, base=0,
                                   pattern=[[1, P]], channel_multiplier=-1).then_inc(made_const, 1)
                pool.memset(R.follows[:, :, 0:1], 0.0).then_inc(made_const, 1)

            def rstds(i, s):
                wait_for(pool, mv_done, i + 1)
                free_slot(pool, h_done, i, DEEP)
                rstd_steps(pool, rstd[:, s, :], nmr[:, s, :], mv[:, s, :, :], mhalf[:, 0:G], chain, i * 3, rstd_done)

            def fetch(i, s):
                free_rows(pool, i, s)
                gather_rows(pool, rows_in, R, i, s, idx, picked, rows, made)

            pipeline(pool, GROUPS, [(0, rstds if layer == 0 else fetch)], DEEP)

        @block.scalar
        def _(act):
            def norm(i, s):
                wait_for(act, rstd_done, i + 1)
                free_rows(act, i, s)
                for g in range(G):
                    last = act.activation(h[:, s, g, :], X[:, i * G + g, :], ACT.Identity,
                                          bias=nmr[:, s, g:g + 1], scale=rstd[:, s, g:g + 1])
                last.then_inc(h_done, 1)

            def copy_hT(i, s):
                wait_for(act, hT_mm, i + 1)
                free_slot(act, l_mm, i, 2)
                act.activation(hT[:, s % 2, :, :, :], psT[:, s % 2, :, :, :], ACT.Copy).then_inc(hT_done, 1)

            def copy_logits(i, s):
                wait_for(act, l_mm, i + 1)
                free_slot(act, turned, i, 2)
                act.activation(logT[:, s % 2, :, :], LT, ACT.Identity, bias=rbc[:, :]).then_inc(l_done, 1)

            act.wait_ge(w_in, 32)
            pipeline(act, GROUPS, [(1, norm), (2, copy_hT), (3, copy_logits)] if layer == 0 else
                     [(0, copy_hT), (1, copy_logits)], DEEP)

        @block.tensor
        def _(pe):
            pe.wait_ge(w_in, 32)
            if layer == 0:
                pe.wait_ge(made_const, 8)

            def transpose_h(i, s):
                wait_for(pe, h_done, i + 1)
                free_slot(pe, hT_done, i, 2)
                for g in range(G):
                    for k in range(DC):
                        mm = pe.transpose(psT[:, s % 2, g, k, :], h[:, s, g, k * P:(k + 1) * P], ident[:, :])
                mm.then_inc(hT_mm, 1)

            def logit(i, s):
                wait_for(pe, hT_done, i + 1)
                free_slot(pe, l_done, i, 1)
                for k in range(DC):
                    mm = pe.matmul(LT, rw[:, k, :], hT[:, s % 2, :, k, :], start=(k == 0), stop=(k == DC - 1))
                mm.then_inc(l_mm, 1)

            def turn(i, s):
                wait_for(pe, l_done, i + 1)
                for g in range(G):
                    mm = pe.matmul(psL[:, bass.ds((i * G + g) * EXPERTS, EXPERTS)], logT[:, s % 2, g, :],
                                   ident[0:EXPERTS, 0:EXPERTS], start=True, stop=True)
                mm.then_inc(turned, 1)

            pipeline(pe, GROUPS, [(0, transpose_h), (1, logit), (2, turn)], DEEP)
            pe.wait_ge(chosen_done, 1)
            marks = chosen[:, :, :].rearrange("p t e -> p (t e)")
            pe.matmul(psR[:, 0, :], R.tri[:, :], marks, start=True, stop=True)
            pe.matmul(psR[:, 1, :], R.ones[:, :], marks, start=True, stop=True).then_inc(n_mm, 1)
            for n in range(CHUNKS):
                pe.wait_ge(slot_done, 2 * n + 2)
                for i in range(CHUNK):
                    mm = pe.matmul(psI[:, 0:SLOTS], lane_hot[:, n % 2, i, :], slot_tok[:, n % 2, i, :],
                                   start=(n == 0 and i == 0), stop=(n == CHUNKS - 1 and i == CHUNK - 1))
                mm.then_inc(i_mm, 1)


def experts(nc, scope, R, layer, W, ident, eb, hidden, made):
    stack, sb, ps, sem = scope(recycle=True)
    with stack:
        L = f"e{layer}_"
        DEEP = 4
        bias = sb(L + "bias", [P, EXPERTS, D])
        idx = sb(L + "idx", [P, DEEP], u32)
        rows = sb(L + "rows", [P, DEEP, D])
        rT = sb(L + "rT", [P, 2, DC, P])
        y = sb(L + "y", [P, DEEP, D])
        psT = ps(L + "psT", [P, 2, DC, P])
        psO = ps(L + "psO", [P, 2, D])
        bias_in = sem(L + "bias_in")
        picked = sem(L + "picked")
        rows_in = [sem(L + f"rows_in{n}") for n in range(DEEP)]
        rT_mm = sem(L + "rT_mm")
        rT_done = sem(L + "rT_done")
        o_mm = sem(L + "o_mm")
        y_done = sem(L + "y_done")
        y_out = [sem(L + f"y_out{n}") for n in range(DEEP)]
        block = stack.enter_context(nc.Block())

        @block.sync
        def _(sp):
            sp.dma_start(bias[:, :, :], eb[layer:layer + 1, :, :].to_broadcast([P, EXPERTS, D])).then_inc(bias_in, 16)
            slot = made.rearrange("(t p) d -> t p d", p=P)

            def store(t, s):
                wait_for(sp, y_done, t + 1)
                sp.dma_start(slot[bass.ds(t, 1), :, :].rearrange("o p d -> (o p) d"), y[:, s, :]).then_inc(y_out[s], 16)

            pipeline(sp, SLOTS, [(0, store)], DEEP)
            for n in range(DEEP):
                sp.wait_ge(y_out[n], (SLOTS - n + DEEP - 1) // DEEP * 16)

        @block.vector
        def _(dve):
            dve.wait_ge(bias_in, 16)

            def add_bias(t, s):
                e = dve.value_load(R.expert_of[0:1, bass.ds(t, 1)], min_val=0, max_val=EXPERTS - 1)
                wait_for(dve, o_mm, t + 1)
                if not isinstance(t, int) or t >= DEEP:
                    wait_for(dve, y_out[s], (t // DEEP) * 16)
                dve.tensor_tensor(y[:, s, :], psO[:, s % 2, :], bias[:, bass.ds(e, 1), :].rearrange("p o d -> p (o d)"),
                                  ALU.add).then_inc(y_done, 1)

            pipeline(dve, SLOTS, [(0, add_bias)], DEEP)

        @block.gpsimd
        def _(pool):
            def fetch(t, s):
                free_slot(pool, rT_mm, t, DEEP)
                pool.tensor_copy(idx[:, s:s + 1], R.tokens[:, bass.ds(t, 1)]).then_inc(picked, 1)
                wait_for(pool, picked, t + 1)
                pool.indirect_dma_start(rows[:, s, :], None, hidden,
                                        bass.IndirectOffsetOnAxis(ap=idx[:, s:s + 1], axis=0)).then_inc(rows_in[s], 16)

            pipeline(pool, SLOTS, [(0, fetch)], DEEP)

        @block.scalar
        def _(act):
            def copy_rT(t, s):
                wait_for(act, rT_mm, t + 1)
                free_slot(act, o_mm, t, 2)
                act.activation(rT[:, s % 2, :, :], psT[:, s % 2, :, :], ACT.Copy).then_inc(rT_done, 1)

            pipeline(act, SLOTS, [(0, copy_rT)], DEEP)

        @block.tensor
        def _(pe):
            def transpose_rows(t, s):
                wait_for(pe, rows_in[s], (t // DEEP + 1) * 16)
                free_slot(pe, rT_done, t, 2)
                for k in range(DC):
                    mm = pe.transpose(psT[:, s % 2, k, :], rows[:, s, k * P:(k + 1) * P], ident[:, :])
                mm.then_inc(rT_mm, 1)

            def product(t, s):
                e = pe.value_load(R.expert_of[0:1, bass.ds(t, 1)], min_val=0, max_val=EXPERTS - 1)
                wait_for(pe, rT_done, t + 1)
                free_slot(pe, y_done, t, 2)
                for k in range(DC):
                    mm = pe.matmul(psO[:, s % 2, :], rT[:, s % 2, k, :],
                                   W[:, bass.ds(e, 1), k, :].rearrange("p o d -> p (o d)"),
                                   start=(k == 0), stop=(k == DC - 1))
                mm.then_inc(o_mm, 1)

            pipeline(pe, SLOTS, [(0, transpose_rows), (1, product)], DEEP)


def combine(nc, scope, R, X, made, out):
    stack, sb, ps, sem = scope()
    with stack:
        DEEP = 4
        idx = sb("o_idx", [P, DEEP, G, CHOICES], u32)
        rows = sb("o_rows", [P, DEEP, G, CHOICES, D])
        picked = sem("o_picked")
        rows_in = [sem(f"o_rows_in{n}") for n in range(DEEP)]
        sum_done = sem("o_sum_done")
        y_done = sem("o_y_done")
        y_out = [sem(f"o_y_out{n}") for n in range(DEEP)]
        block = stack.enter_context(nc.Block())
        ov = out.rearrange("(t p) d -> p t d", p=P)

        @block.gpsimd
        def _(pool):
            def fetch(i, s):
                if not isinstance(i, int) or i >= DEEP:
                    wait_for(pool, y_out[s], (i // DEEP) * 16)
                gather_rows(pool, rows_in, R, i, s, idx, picked, rows, made)

            pipeline(pool, GROUPS, [(0, fetch)], DEEP)

        @block.vector
        def _(dve):
            def add(i, s):
                wait_for(dve, rows_in[s], (i // DEEP + 1) * (G * CHOICES * 16))
                y = rows[:, s, :, 0, :]
                dve.tensor_tensor(y, y, rows[:, s, :, 1, :], ALU.add).then_inc(sum_done, 1)
                wait_for(dve, sum_done, i + 1)
                dve.tensor_tensor(y, y, X[:, bass.ds(i * G, G), :], ALU.add).then_inc(y_done, 1)

            pipeline(dve, GROUPS, [(0, add)], DEEP)

        @block.sync
        def _(sp):
            def store(i, s):
                wait_for(sp, y_done, i + 1)
                sp.dma_start(ov[:, bass.ds(i * G, G), :], rows[:, s, :, 0, :]).then_inc(y_out[s], 16)

            pipeline(sp, GROUPS, [(0, store)], DEEP)
            for n in range(DEEP):
                sp.wait_ge(y_out[n], GROUPS // DEEP * 16)


def kernel(x, ctx_1024, mask_BxS2_bf1, L0_ffn_rhs, L1_xattn_Wq, L1_xattn_Wk, L1_xattn_Wv, L1_xattn_Wo,
           L1_xattn_inv_temp, L1_ffn_router_w, L1_ffn_router_b, L1_ffn_expert_w, L1_ffn_expert_b):
    import numpy as np
    import concourse.bacc as bacc
    from concourse.bass_utils import run_bass_kernel_spmd

    ctx = np.asarray(ctx_1024).reshape(BATCH * KV, D)
    laid = {
        "x": np.asarray(x).reshape(TOKENS, D),
        "ctxT": ctx.T,
        "ctx": ctx,
        "mask": np.asarray(mask_BxS2_bf1).view(np.uint8),
        "rhs": np.asarray(L0_ffn_rhs),
        "WqT": np.asarray(L1_xattn_Wq).T,
        "Wk": np.asarray(L1_xattn_Wk),
        "Wv": np.asarray(L1_xattn_Wv),
        "Wo": np.asarray(L1_xattn_Wo),
        "inv_temp": np.repeat(np.asarray(L1_xattn_inv_temp), DH).reshape(PAIRS, P).T,
        "rwT": np.asarray(L1_ffn_router_w).transpose(0, 2, 1),
        "rb": np.asarray(L1_ffn_router_b),
        "ewT": np.asarray(L1_ffn_expert_w).transpose(0, 1, 3, 2),
        "eb": np.asarray(L1_ffn_expert_b),
    }
    nc = bacc.Bacc("TRN2", target_bir_lowering=False, num_devices=1)
    arrays, args = {}, []
    for name, a in laid.items():
        a = np.ascontiguousarray(a)
        arrays["in_" + name] = a
        args.append(nc.dram_tensor("in_" + name, a.shape, mybir.dt.from_np(a.dtype), kind="ExternalInput").ap())
    out = nc.dram_tensor("out_x", (TOKENS, D), fp32, kind="ExternalOutput").ap()
    build(nc, *args, out)
    r = run_bass_kernel_spmd(nc, [arrays], core_ids=[0])
    return r.results[0]["out_x"].reshape(BATCH, SEQ, D)
```

```python
import concourse.bass as bass
from concourse import mybir
from contextlib import ExitStack

P = 128
BATCH, SEQ, D = 4, 1024, 512
KV = 64
HEADS, DH = 16, 64
TOPK = 32
EXPERTS, LAYERS, CHOICES = 8, 2, 2
TOKENS = BATCH * SEQ
TILES = TOKENS // P
TPB = SEQ // P
DC = D // P
PAIRS = HEADS // 2
G = 2
GROUPS = TILES // G
GPB = GROUPS // BATCH
SLOTS = (CHOICES * TOKENS + EXPERTS * (P - 1)) // P
TOKEN_ZERO = TOKENS // 2
LN_EPS = 1e-5
NORM_EPS = 1e-8
INT8_MAX = 127.0
ROUND = 1.5 * 2.0 ** 23
MASKED = -3.0e38
TAKEN = -3.4e38

fp32 = mybir.dt.float32
bf16 = mybir.dt.bfloat16
fp16 = mybir.dt.float16
fp32r = mybir.dt.float32r
u8 = mybir.dt.uint8
i32 = mybir.dt.int32
u32 = mybir.dt.uint32
ALU = mybir.AluOpType
ACT = mybir.ActivationFunctionType
AX = mybir.AxisListType


class Waited:
    sem = None


def wait_for(eng, sem, count):
    eng.wait_ge(sem, count)
    if not isinstance(count, int):
        eng.sem_inc(Waited.sem, 1)


def free_slot(eng, released, t, depth, per=1):
    if not isinstance(t, int) or t >= depth:
        wait_for(eng, released, (t - depth + 1) * per)


def pipeline(eng, count, stages, slots=2):
    stages = [(stage[0], stage[1], stage[2] if len(stage) > 2 else count) for stage in stages]
    cuts = sorted({cut for lag, _, steps in stages for cut in (lag, min(lag + slots, lag + steps), lag + steps)})
    for a, b in zip(cuts, cuts[1:]):
        live = [(lag, stage) for lag, stage, steps in stages if lag <= a < lag + steps]

        def window(w, place):
            for lag, stage in live:
                stage(w - lag, (place - lag) % slots)

        looped = (b - a) // slots * slots if all(a - lag >= slots for lag, _ in live) else 0
        if looped >= 2 * slots:
            with eng.Fori(0, looped // slots) as body:
                for n in range(slots):
                    window(body * slots + (a + n), a + n)
            a += looped
        for w in range(a, b):
            window(w, w)


def build(nc, x, ctxT, ctx, mask, rhs, WqT, Wk, Wv, Wo, inv_temp, rwT, rb, ewT, eb, out):
    top = ExitStack()
    with top:
        def scope(recycle=False):
            stack = ExitStack()
            used = []

            def clear():
                nc.clear_and_free_semaphores(used)
                nc.all_engine_barrier()

            if recycle:
                stack.callback(clear)

            def sb(name, shape, dt=fp32):
                return stack.enter_context(nc.sbuf_tensor(name, shape, dt))

            def ps(name, shape, dt=fp32):
                return stack.enter_context(nc.psum_tensor(name, shape, dt))

            def sem(name):
                if not recycle:
                    return stack.enter_context(nc.semaphore(name))
                used.append(nc.alloc_semaphore(name))
                return used[-1]
            return stack, sb, ps, sem

        keep, sb, ps, sem = scope()
        top.enter_context(keep)
        ident = sb("ident", [P, P])
        identb = sb("identb", [P, P], bf16)
        mhalf = sb("mhalf", [P, G])

        Waited.sem = sem("waited")
        hidden = nc.dram_tensor("hidden", (TOKENS, D), fp32, kind="Internal").ap()
        made = nc.dram_tensor("made", (SLOTS * P, D), fp32, kind="Internal").ap()
        residual = nc.dram_tensor("residual", (TOKENS, D), fp32, kind="Internal").ap()
        attention, asb, _, _ = scope()
        with attention:
            X = asb("X", [P, TILES, D])
            maskrow = asb("maskrow", [1, BATCH, HEADS // 2, KV], bf16)
            onesrow = asb("onesrow", [1, P], bf16)
            KT = asb("KT", [P, PAIRS, BATCH * KV])
            VT = asb("VT", [P, PAIRS, BATCH * KV])
            wq = asb("wq", [P, DC, D], bf16)
            wscale = asb("wscale", [P, D])
            phase_a(nc, scope, X, x, ctxT, ctx, ident, identb, mhalf, onesrow, maskrow, mask, KT, VT, Wk, Wv,
                    inv_temp, rhs, wq, wscale)
            products, psb, pps, psem = scope()
            with products:
                heads = HeadProducts(psb, pps, psem, KT, VT, WqT, Wo)
                phase_b(nc, scope, X, wq, wscale, identb, mhalf, heads)
                phase_c(nc, scope, X, heads, ident, mhalf, maskrow, onesrow, hidden, residual)
        routing, rsb, _, _ = scope()
        with routing:
            R = Routing(rsb)
            weights, wsb, _, _ = scope()
            with weights:
                W_high = wsb("W_high", [P, EXPERTS, DC, D], fp32r)
                W_low = wsb("W_low", [P, EXPERTS, DC, D], fp32r)
                for layer in range(LAYERS):
                    route(nc, scope, R, layer, W_high, W_low, ident, rwT, rb, ewT, hidden, made)
                    experts(nc, scope, R, layer, W_high, W_low, ident, eb, hidden, made)
            combine(nc, scope, R, residual, made, out)


def rstd_steps(pool, rstd, nmr, mv, mhalf, chain, base, done):
    pool.tensor_scalar(rstd, mv[:, :, 1], LN_EPS, None, ALU.add).then_inc(chain, 1)
    pool.tensor_scalar(nmr, mv[:, :, 0], -1.0, None, ALU.mult).then_inc(chain, 1)
    wait_for(pool, chain, base + 2)
    pool.tensor_tensor(rstd, rstd, mhalf, ALU.pow).then_inc(chain, 1)
    wait_for(pool, chain, base + 3)
    pool.tensor_tensor(nmr, nmr, rstd, ALU.mult).then_inc(done, 1)


def phase_a(nc, scope, X, x, ctxT, ctx, ident, identb, mhalf, onesrow, maskrow, mask, KT, VT, Wk, Wv, inv_temp,
            rhs, wq, wscale):
    stack, sb, ps, sem = scope()
    with stack:
        DEEP = 4
        m8 = sb("a_m8", [1, BATCH, KV], u8)
        cT = sb("a_cT", [P, DC, BATCH * KV])
        cn = sb("a_cn", [KV, BATCH, D])
        bn = sb("a_bn", [P, DEEP, G, 6])
        mv = sb("a_mv", [P, DEEP, G, 2])
        rstd = sb("a_rstd", [P, DEEP, G])
        nmr = sb("a_nmr", [P, DEEP, G])
        y = sb("a_y", [P, 2, G, D])
        yT = sb("a_yT", [P, 2, G, DC, P])
        nmax = sb("a_nmax", [P, DEEP, G])
        probs = sb("a_probs", [P, DEEP, G, KV])
        Z = sb("a_Z", [P, DEEP, G])
        rZ = sb("a_rZ", [P, DEEP, G])
        pT = sb("a_pT", [KV, DEEP, G, P])
        wk = sb("a_wk", [P, DC, HEADS * DH])
        wv = sb("a_wv", [P, DC, HEADS * DH])
        it = sb("a_it", [P, PAIRS])
        it8 = sb("a_it8", [P, PAIRS])
        w = sb("a_w", [P, DC, D])
        wabs = sb("a_wabs", [P, D])
        wmax = sb("a_wmax", [P, D])
        winv = sb("a_winv", [P, D])
        psK = ps("a_psK", [P, 512])
        psV = ps("a_psV", [P, 512])
        psT = ps("a_psT", [P, G, DC, P])
        psS = ps("a_psS", [P, 512])
        psP = ps("a_psP", [P, 512])
        psO = ps("a_psO", [P, G, D])
        zeroed = sem("a_zeroed")
        constant = sem("a_constant")
        mask_in = sem("a_mask_in")
        c_in = sem("a_c_in")
        x_in = [sem(f"a_x_in{n}") for n in range(DEEP)]
        bn_done = sem("a_bn_done")
        mv_done = sem("a_mv_done")
        chain = sem("a_chain")
        rstd_done = sem("a_rstd_done")
        y_done = sem("a_y_done")
        yT_mm = sem("a_yT_mm")
        yT_done = sem("a_yT_done")
        s_mm = sem("a_s_mm")
        nmax_done = sem("a_nmax_done")
        p_done = sem("a_p_done")
        pT_mm = sem("a_pT_mm")
        pT_done = sem("a_pT_done")
        rZ_done = sem("a_rZ_done")
        o_mm = sem("a_o_mm")
        x_done = sem("a_x_done")
        w_in = sem("a_w_in")
        wk_in = sem("a_wk_in")
        wv_in = sem("a_wv_in")
        it_in = sem("a_it_in")
        it_done = sem("a_it_done")
        k_mm = sem("a_k_mm")
        v_mm = sem("a_v_mm")
        k_out = sem("a_k_out")
        v_out = sem("a_v_out")
        w_chain = sem("a_w_chain")
        wabs_done = sem("a_wabs_done")
        wmax_done = sem("a_wmax_done")
        block = stack.enter_context(nc.Block())
        xv = x.rearrange("(t p) d -> p t d", p=P)
        S = psS[:, 0:G * KV].rearrange("p (g s) -> p g s", g=G)
        PT = psP[0:KV, 0:G * P].rearrange("p (g s) -> p g s", g=G)

        @block.sync
        def _(sp):
            sp.dma_start(X[:, 0:G, :], xv[:, 0:G, :]).then_inc(x_in[0], 16)
            sp.dma_start(cT[:, :, :], ctxT.rearrange("(k p) n -> p k n", p=P)).then_inc(c_in, 16)
            sp.dma_start(X[:, G:2 * G, :], xv[:, G:2 * G, :]).then_inc(x_in[1], 16)
            sp.dma_start(m8[0:1, :, :], mask.rearrange("(o b) s -> o b s", o=1)).then_inc(mask_in, 16)
            sp.dma_start(cn[:, :, :], ctx.rearrange("(b s) d -> s b d", b=BATCH)).then_inc(c_in, 16)

            def load(i, s):
                if isinstance(i, int) and i < 2:
                    return
                if not isinstance(i, int) or i >= DEEP:
                    wait_for(sp, x_in[s], (i // DEEP) * 16)
                sp.dma_start(X[:, bass.ds(i * G, G), :], xv[:, bass.ds(i * G, G), :]).then_inc(x_in[s], 16)

            pipeline(sp, GROUPS, [(0, load)], DEEP)

        AT = 3
        WT = 9

        @block.vector
        def _(dve):
            def stats(i, s):
                wait_for(dve, x_in[s], (i // DEEP + 1) * 16)
                free_slot(dve, rstd_done, i, DEEP)
                for g in range(G):
                    last = dve.bn_stats(bn[:, s, g, :], X[:, i * G + g, :])
                last.then_inc(bn_done, 1)
                wait_for(dve, bn_done, i + 1)
                for g in range(G):
                    last = dve.bn_aggr(mv[:, s, g, :], bn[:, s, g, :])
                last.then_inc(mv_done, 1)

            def row_max(i, s):
                wait_for(dve, s_mm, i + 1)
                free_slot(dve, p_done, i, DEEP)
                dve.tensor_reduce(nmax[:, s, :], S, AX.X, ALU.max, negate=True).then_inc(nmax_done, 1)

            def inverse(i, s):
                wait_for(dve, p_done, i + 1)
                free_slot(dve, x_done, i, DEEP)
                dve.reciprocal(rZ[:, s, :], Z[:, s, :]).then_inc(rZ_done, 1)

            def residual(i, s):
                wait_for(dve, o_mm, i + 1)
                wait_for(dve, rZ_done, i + 1)
                for g in range(G):
                    xt = X[:, i * G + g, :]
                    last = dve.scalar_tensor_tensor(xt, psO[:, g, :], rZ[:, s, g:g + 1], xt, ALU.mult, ALU.add)
                last.then_inc(x_done, 1)

            def copy_V(p, s):
                wait_for(dve, v_mm, p + 1)
                dve.tensor_copy(VT[:, bass.ds(p, 1), :].rearrange("p o n -> p (o n)"),
                                psV[:, 0:BATCH * KV]).then_inc(v_out, 1)

            def quantize_rhs(n, s):
                if n == 0:
                    dve.wait_ge(mask_in, 16)
                    for copy in range(HEADS // 2):
                        dve.tensor_scalar(maskrow[0:1, :, copy, :], m8[0:1, :, :], 1.0, -MASKED, ALU.subtract, ALU.mult)
                    dve.wait_ge(w_in, 16)
                    dve.tensor_reduce(wabs[:, :], w[:, :, :].rearrange("p k n -> p n k"), AX.X, ALU.max,
                                      apply_absolute_value=True).then_inc(wabs_done, 1)
                if n == 1:
                    dve.wait_ge(wmax_done, 1)
                    dve.tensor_scalar(wscale[:, :], wmax[:, :], 1e-12, 1.0 / INT8_MAX, ALU.max,
                                      ALU.mult).then_inc(w_chain, 1)
                    dve.wait_ge(w_chain, 1)
                    dve.reciprocal(winv[:, :], wscale[:, :]).then_inc(w_chain, 1)
                if n == 2:
                    dve.wait_ge(w_chain, 2)
                    for k in range(DC):
                        dve.tensor_tensor(w[:, k, :], w[:, k, :], winv[:, :], ALU.mult).then_inc(w_chain, 1)
                if n == 3:
                    dve.wait_ge(w_chain, 2 + DC)
                    dve.tensor_scalar(w[:, :, :], w[:, :, :], INT8_MAX, -INT8_MAX, ALU.min,
                                      ALU.max).then_inc(w_chain, 1)
                if n == 4:
                    dve.wait_ge(w_chain, 3 + DC)
                    dve.tensor_scalar(w[:, :, :], w[:, :, :], ROUND, None, ALU.add).then_inc(w_chain, 1)
                if n == 5:
                    dve.wait_ge(w_chain, 4 + DC)
                    dve.tensor_scalar(wq[:, :, :], w[:, :, :], -ROUND, None, ALU.add)

            dve.wait_ge(it_in, 16)
            dve.tensor_scalar(it8[:, :], it[:, :], DH ** -0.5, None, ALU.mult).then_inc(it_done, 1)
            pipeline(dve, GROUPS, [(4, row_max), (0, stats), (5, inverse), (6, residual), (AT, copy_V, PAIRS),
                                   (WT, quantize_rhs, 6)], DEEP)

        @block.gpsimd
        def _(pool):
            def rstds(i, s):
                wait_for(pool, mv_done, i + 1)
                free_slot(pool, y_done, i, DEEP)
                rstd_steps(pool, rstd[:, s, :], nmr[:, s, :], mv[:, s, :, :], mhalf[:, 0:G],
                           chain, i * 3, rstd_done)

            pool.memset(mhalf[:, :], -0.5).then_inc(constant, 1)
            pool.memset(ident[:, :], 0.0).then_inc(zeroed, 1)
            pool.memset(identb[:, :], 0.0).then_inc(zeroed, 1)
            pool.memset(onesrow[:, :], 1.0)
            pool.wait_ge(zeroed, 2)
            for m in (ident, identb):
                pool.affine_select(out=m[:, :], in_=m[:, :], compare_op=ALU.not_equal, fill=1.0, base=0,
                                   pattern=[[-1, P]], channel_multiplier=1).then_inc(constant, 1)
            pool.wait_ge(constant, 3)

            def reduce_rhs(n, s):
                pool.wait_ge(wabs_done, 1)
                pool.partition_all_reduce(wmax[:, :], wabs[:, :], P, bass.bass_isa.ReduceOp.max).then_inc(wmax_done, 1)

            pipeline(pool, GROUPS, [(0, rstds), (WT, reduce_rhs, 1)], DEEP)

        @block.scalar
        def _(act):
            def norm(i, s):
                wait_for(act, rstd_done, i + 1)
                free_slot(act, yT_mm, i, 2)
                for g in range(G):
                    last = act.activation(y[:, s % 2, g, :], X[:, i * G + g, :], ACT.Identity,
                                          bias=nmr[:, s, g:g + 1], scale=rstd[:, s, g:g + 1])
                last.then_inc(y_done, 1)

            def copy_yT(i, s):
                wait_for(act, yT_mm, i + 1)
                free_slot(act, s_mm, i, 2)
                act.activation(yT[:, s % 2, :, :, :], psT[:, :, :, :], ACT.Copy).then_inc(yT_done, 1)

            def exps(i, s):
                wait_for(act, nmax_done, i + 1)
                free_slot(act, pT_mm, i, DEEP)
                free_slot(act, rZ_done, i, DEEP)
                for g in range(G):
                    last = act.activation(probs[:, s, g, :], S[:, g, :], ACT.Exp, bias=nmax[:, s, g:g + 1],
                                          accum_out=Z[:, s, g:g + 1])
                last.then_inc(p_done, 1)

            def copy_pT(i, s):
                wait_for(act, pT_mm, i + 1)
                free_slot(act, o_mm, i, DEEP)
                act.activation(pT[:, s, :, :], PT, ACT.Copy).then_inc(pT_done, 1)

            def copy_K(p, s):
                wait_for(act, k_mm, p + 1)
                act.activation(KT[:, bass.ds(p, 1), :].rearrange("p o n -> p (o n)"), psK[:, 0:BATCH * KV],
                               ACT.Copy, scale=it8[:, bass.ds(p, 1)]).then_inc(k_out, 1)

            act.dma_start(it[:, :], inv_temp).then_inc(it_in, 16)
            act.wait_ge(x_in[0], 16)
            act.dma_start(wk[:, :, :], Wk.rearrange("(k p) n -> p k n", p=P)).then_inc(wk_in, 16)
            act.dma_start(wv[:, :, :], Wv.rearrange("(k p) n -> p k n", p=P)).then_inc(wv_in, 16)
            act.dma_start(w[:, :, :], rhs.rearrange("(k p) n -> p k n", p=P)).then_inc(w_in, 16)
            act.wait_ge(it_done, 1)
            pipeline(act, GROUPS, [(1, norm), (2, copy_yT), (4, exps), (5, copy_pT), (AT, copy_K, PAIRS)], DEEP)

        @block.tensor
        def _(pe):
            pe.wait_ge(constant, 3)
            pe.wait_ge(c_in, 32)

            def transpose_y(i, s):
                wait_for(pe, y_done, i + 1)
                free_slot(pe, yT_done, i, 1)
                for g in range(G):
                    for k in range(DC):
                        mm = pe.transpose(psT[:, g, k, :], y[:, s % 2, g, k * P:(k + 1) * P], ident[:, :])
                mm.then_inc(yT_mm, 1)

            def scores(i, s):
                wait_for(pe, yT_done, i + 1)
                free_slot(pe, p_done, i, 1)
                for g in range(G):
                    for k in range(DC):
                        mm = pe.matmul(S[:, g, :], yT[:, s % 2, g, k, :],
                                       cT[:, k, bass.ds((i // GPB) * KV, KV)], start=(k == 0), stop=(k == DC - 1))
                mm.then_inc(s_mm, 1)

            def transpose_p(i, s):
                wait_for(pe, p_done, i + 1)
                free_slot(pe, pT_done, i, 1)
                for g in range(G):
                    mm = pe.transpose(PT[:, g, :], probs[:, s, g, :], ident[:, :])
                mm.then_inc(pT_mm, 1)

            def values(i, s):
                wait_for(pe, pT_done, i + 1)
                free_slot(pe, x_done, i, 1)
                for g in range(G):
                    mm = pe.matmul(psO[:, g, :], pT[:, s, g, :], cn[:, i // GPB, :], start=True, stop=True)
                mm.then_inc(o_mm, 1)

            def keys_values(p, s):
                for weights, acc, loaded, done, released in ((wk, psK, wk_in, k_mm, k_out),
                                                             (wv, psV, wv_in, v_mm, v_out)):
                    if isinstance(p, int) and p == 0:
                        pe.wait_ge(loaded, 16)
                    free_slot(pe, released, p, 1)
                    for k in range(DC):
                        mm = pe.matmul(acc[:, 0:BATCH * KV], weights[:, k, p * P:(p + 1) * P], cT[:, k, :],
                                       start=(k == 0), stop=(k == DC - 1))
                    mm.then_inc(done, 1)

            pipeline(pe, GROUPS, [(2, transpose_y), (5, transpose_p), (6, values), (3, scores),
                                  (AT, keys_values, PAIRS)], DEEP)


class HeadProducts:

    STEPS = BATCH * PAIRS

    def __init__(self, sb, ps, sem, KT, VT, WqT, Wo):
        self.KT, self.VT, self.WqT, self.Wo = KT, VT, WqT, Wo
        self.M = sb("h_M", [P, 2, DC, HEADS * KV])
        self.U = sb("h_U", [P, 2, PAIRS, D])
        self.wq = sb("h_wq", [P, 2, D])
        self.wo = sb("h_wo", [P, 2, D])
        self.KB = sb("h_KB", [P, 2, P])
        self.VB = sb("h_VB", [P, 2, P])
        self.psM = ps("h_psM", [P, DC, P])
        self.psU = ps("h_psU", [P, D])
        self.wq_in = [sem(f"h_wq_in{n}") for n in range(2)]
        self.wo_in = [sem(f"h_wo_in{n}") for n in range(2)]
        self.blocks_zero = sem("h_blocks_zero")
        self.kb_done = sem("h_kb_done")
        self.vb_done = sem("h_vb_done")
        self.m_mm = sem("h_m_mm")
        self.m_done = sem("h_m_done")
        self.u_mm = sem("h_u_mm")
        self.u_done = sem("h_u_done")

    def clear_blocks(self, pool):
        pool.memset(self.KB[:, :, :], 0.0).then_inc(self.blocks_zero, 1)
        pool.memset(self.VB[:, :, :], 0.0).then_inc(self.blocks_zero, 1)

    def load_wq(self, sp, u, s):
        free_slot(sp, self.m_mm, u, 2)
        sp.dma_start(self.wq[:, s % 2, :], self.WqT[bass.ds((u % PAIRS) * P, P), :]).then_inc(self.wq_in[s % 2], 16)

    def load_wo(self, sp, u, s):
        free_slot(sp, self.u_mm, u, 2)
        sp.dma_start(self.wo[:, s % 2, :], self.Wo[bass.ds((u % PAIRS) * P, P), :]).then_inc(self.wo_in[s % 2], 16)

    def spread_K(self, act, u, s):
        self.spread(act, u, s % 2, self.KT, self.KB, self.m_mm, self.kb_done)

    def spread_V(self, act, u, s):
        self.spread(act, u, s % 2, self.VT, self.VB, self.u_mm, self.vb_done)

    def spread(self, act, u, s, T, B, used, done):
        free_slot(act, used, u, 2)
        for h in range(2):
            at = slice(h * DH, (h + 1) * DH)
            last = act.activation(B[at, s, at], T[at, u % PAIRS, bass.ds((u // PAIRS) * KV, KV)], ACT.Copy)
        last.then_inc(done, 1)

    def make_M(self, pe, u, s):
        wait_for(pe, self.wq_in[s % 2], (u // 2 + 1) * 16)
        free_slot(pe, self.m_done, u, 1)
        wait_for(pe, self.kb_done, u + 1)
        for k in range(DC):
            mm = pe.matmul(self.psM[:, k, :], self.wq[:, s % 2, k * P:(k + 1) * P], self.KB[:, s % 2, :],
                           start=True, stop=True)
        mm.then_inc(self.m_mm, 1)

    def make_U(self, pe, u, s):
        wait_for(pe, self.wo_in[s % 2], (u // 2 + 1) * 16)
        free_slot(pe, self.u_done, u, 1)
        wait_for(pe, self.vb_done, u + 1)
        pe.matmul(self.psU[:, :], self.VB[:, s % 2, :], self.wo[:, s % 2, :],
                  start=True, stop=True).then_inc(self.u_mm, 1)

    def copy_M(self, act, u, s):
        wait_for(act, self.m_mm, u + 1)
        act.activation(self.M[:, (u // PAIRS) % 2, :, bass.ds((u % PAIRS) * P, P)], self.psM[:, :, :],
                       ACT.Copy).then_inc(self.m_done, 1)

    def copy_U(self, act, u, s):
        wait_for(act, self.u_mm, u + 1)
        act.activation(self.U[:, (u // PAIRS) % 2, u % PAIRS, :], self.psU[:, :], ACT.Copy).then_inc(self.u_done, 1)


def phase_b(nc, scope, X, wq, wscale, identb, mhalf, heads):
    stack, sb, ps, sem = scope()
    with stack:
        DEEP = 4
        bn = sb("b_bn", [P, DEEP, G, 6])
        mv = sb("b_mv", [P, DEEP, G, 2])
        rstd = sb("b_rstd", [P, DEEP, G])
        nmr = sb("b_nmr", [P, DEEP, G])
        y = sb("b_y", [P, 2, G, D])
        amax = sb("b_amax", [P, DEEP, G])
        scale = sb("b_scale", [P, 2 * DEEP, G])
        inv = sb("b_inv", [P, DEEP, G])
        q = sb("b_q", [P, 2, G, D], bf16)
        qT = sb("b_qT", [P, 2, G, DC, P], bf16)
        delta = sb("b_delta", [P, 2, G, D])
        minus_round = sb("b_minus_round", [P, 1])
        psT = ps("b_psT", [P, 2, G, DC, P], bf16)
        psO = ps("b_psO", [P, 2, G, D])
        constant = sem("b_constant")
        bn_done = sem("b_bn_done")
        mv_done = sem("b_mv_done")
        chain = sem("b_chain")
        rstd_done = sem("b_rstd_done")
        y_done = sem("b_y_done")
        sc_chain = sem("b_sc_chain")
        v_done = sem("b_v_done")
        q_done = sem("b_q_done")
        qT_mm = sem("b_qT_mm")
        qT_done = sem("b_qT_done")
        o_mm = sem("b_o_mm")
        d_done = sem("b_d_done")
        x_done = sem("b_x_done")
        block = stack.enter_context(nc.Block())

        def first(make, eng):
            return lambda u, s: make(eng, u, s)

        @block.sync
        def _(sp):
            pipeline(sp, PAIRS, [(0, first(heads.load_wq, sp)), (0, first(heads.load_wo, sp))])

        @block.vector
        def _(dve):
            dve.memset(minus_round[:, :], -ROUND).then_inc(constant, 1)

            def stats(i, s):
                free_slot(dve, rstd_done, i, DEEP)
                for g in range(G):
                    last = dve.bn_stats(bn[:, s, g, :], X[:, i * G + g, :])
                last.then_inc(bn_done, 1)
                wait_for(dve, bn_done, i + 1)
                for g in range(G):
                    last = dve.bn_aggr(mv[:, s, g, :], bn[:, s, g, :])
                last.then_inc(mv_done, 1)

            def quantize(i, s):
                wait_for(dve, y_done, i + 1)
                dve.tensor_reduce(amax[:, s, :], y[:, s % 2, :, :], AX.X, ALU.max,
                                  apply_absolute_value=True).then_inc(sc_chain, 1)
                wait_for(dve, sc_chain, i * 4 + 1)
                dve.tensor_scalar(scale[:, i % (2 * DEEP), :], amax[:, s, :], 1e-12, 1.0 / INT8_MAX, ALU.max,
                                  ALU.mult).then_inc(sc_chain, 1)
                wait_for(dve, sc_chain, i * 4 + 2)
                dve.reciprocal(inv[:, s, :], scale[:, i % (2 * DEEP), :]).then_inc(sc_chain, 1)
                wait_for(dve, sc_chain, i * 4 + 3)
                for g in range(G):
                    yt = y[:, s % 2, g, :]
                    last = dve.tensor_scalar(yt, yt, inv[:, s, g:g + 1], INT8_MAX, ALU.mult, ALU.min)
                last.then_inc(sc_chain, 1)
                wait_for(dve, sc_chain, i * 4 + 4)
                dve.tensor_scalar(y[:, s % 2, :, :], y[:, s % 2, :, :], -INT8_MAX, ROUND, ALU.max,
                                  ALU.add).then_inc(v_done, 1)

            def rescale(i, s):
                wait_for(dve, o_mm, i + 1)
                free_slot(dve, x_done, i, 2)
                for g in range(G):
                    last = dve.scalar_tensor_tensor(delta[:, s % 2, g, :], psO[:, s % 2, g, :],
                                                    scale[:, i % (2 * DEEP), g:g + 1], wscale[:, :], ALU.mult, ALU.mult)
                last.then_inc(d_done, 1)

            pipeline(dve, GROUPS, [(0, stats), (5, rescale), (2, quantize)], DEEP)

        @block.gpsimd
        def _(pool):
            def rstds(i, s):
                wait_for(pool, mv_done, i + 1)
                free_slot(pool, y_done, i, DEEP)
                rstd_steps(pool, rstd[:, s, :], nmr[:, s, :], mv[:, s, :, :], mhalf[:, 0:G],
                           chain, i * 3, rstd_done)

            def residual(i, s):
                wait_for(pool, d_done, i + 1)
                xt = X[:, bass.ds(i * G, G), :]
                pool.tensor_tensor(xt, delta[:, s % 2, :, :], xt, ALU.add).then_inc(x_done, 1)

            heads.clear_blocks(pool)
            pipeline(pool, GROUPS, [(6, residual), (0, rstds)], DEEP)

        @block.scalar
        def _(act):
            def norm(i, s):
                wait_for(act, rstd_done, i + 1)
                free_slot(act, q_done, i, 2)
                for g in range(G):
                    last = act.activation(y[:, s % 2, g, :], X[:, i * G + g, :], ACT.Identity,
                                          bias=nmr[:, s, g:g + 1], scale=rstd[:, s, g:g + 1])
                last.then_inc(y_done, 1)

            def unround(i, s):
                wait_for(act, v_done, i + 1)
                free_slot(act, qT_mm, i, 2)
                act.activation(q[:, s % 2, :, :], y[:, s % 2, :, :], ACT.Identity,
                               bias=minus_round[:, :]).then_inc(q_done, 1)

            def copy_qT(i, s):
                wait_for(act, qT_mm, i + 1)
                free_slot(act, o_mm, i, 2)
                act.activation(qT[:, s % 2, :, :, :], psT[:, s % 2, :, :, :], ACT.Copy).then_inc(qT_done, 1)

            act.wait_ge(constant, 1)
            act.wait_ge(heads.blocks_zero, 2)
            pipeline(act, GROUPS, [(3, unround), (1, norm), (4, copy_qT), (5, first(heads.spread_K, act), PAIRS),
                                   (5, first(heads.spread_V, act), PAIRS), (6, first(heads.copy_M, act), PAIRS),
                                   (6, first(heads.copy_U, act), PAIRS)], DEEP)

        @block.tensor
        def _(pe):
            def transpose_q(i, s):
                wait_for(pe, q_done, i + 1)
                free_slot(pe, qT_done, i, 2)
                for g in range(G):
                    for k in range(DC):
                        mm = pe.transpose(psT[:, s % 2, g, k, :], q[:, s % 2, g, k * P:(k + 1) * P], identb[:, :])
                mm.then_inc(qT_mm, 1)

            def product(i, s):
                wait_for(pe, qT_done, i + 1)
                free_slot(pe, d_done, i, 2)
                for g in range(G):
                    for k in range(DC):
                        mm = pe.matmul(psO[:, s % 2, g, :], qT[:, s % 2, g, k, :], wq[:, k, :],
                                       start=(k == 0), stop=(k == DC - 1))
                mm.then_inc(o_mm, 1)

            pipeline(pe, GROUPS, [(4, transpose_q), (4, product), (5, first(heads.make_M, pe), PAIRS),
                                  (5, first(heads.make_U, pe), PAIRS)], DEEP)


def phase_c(nc, scope, X, heads, ident, mhalf, maskrow, onesrow, hidden, residual):
    stack, sb, ps, sem = scope()
    with stack:
        HK = KV // 2
        bn = sb("c_bn", [P, 2, 1, 6])
        mv = sb("c_mv", [P, 2, 1, 2])
        rstd = sb("c_rstd", [P, 2, 1])
        nmr = sb("c_nmr", [P, 2, 1])
        bn2 = sb("c_bn2", [P, 2, 1, 6])
        mv2 = sb("c_mv2", [P, 2, 1, 2])
        rstd2 = sb("c_rstd2", [P, 2, 1])
        nmr2 = sb("c_nmr2", [P, 2, 1])
        h = sb("c_h", [P, 2, D])
        y = sb("c_y", [P, D])
        yT = sb("c_yT", [P, 2, DC, P])
        S = sb("c_S", [P, 2, HEADS, KV])
        nmax = sb("c_nmax", [P, HEADS])
        SN = sb("c_SN", [P, HEADS, HK])
        W = sb("c_W", [P, 2, HEADS, HK])
        top = sb("c_top", [P, 2, HEADS, HK // 2 + 1])
        cut = sb("c_cut", [P, HEADS, HK // 2 + 1])
        least = sb("c_least", [P, HEADS])
        E = sb("c_E", [P, 2, HEADS, KV])
        Z = sb("c_Z", [P, 2, HEADS])
        kept = sb("c_kept", [P, HEADS])
        den = sb("c_den", [P, HEADS])
        rden = sb("c_rden", [P, HEADS])
        aT = sb("c_aT", [P, PAIRS, P])
        psY = ps("c_psY", [P, DC, P])
        psS = ps("c_psS", [P, HEADS, KV])
        psA = ps("c_psA", [P, PAIRS, P])
        psO = ps("c_psO", [P, D])
        bn_done = sem("c_bn_done")
        mv_done = sem("c_mv_done")
        chain = sem("c_chain")
        rstd_done = sem("c_rstd_done")
        y_done = sem("c_y_done")
        yT_mm = sem("c_yT_mm")
        yT_done = sem("c_yT_done")
        s_mm = sem("c_s_mm")
        s_done = sem("c_s_done")
        pads_done = sem("c_pads_done")
        topk = sem("c_topk")
        e_done = sem("c_e_done")
        marked = sem("c_marked")
        dropped = sem("c_dropped")
        kept_done = sem("c_kept_done")
        den_chain = sem("c_den_chain")
        den_done = sem("c_den_done")
        rden_done = sem("c_rden_done")
        a_done = sem("c_a_done")
        aT_mm = sem("c_aT_mm")
        aT_done = sem("c_aT_done")
        o_mm = sem("c_o_mm")
        x_done = sem("c_x_done")
        bn2_done = sem("c_bn2_done")
        mv2_done = sem("c_mv2_done")
        chain2 = sem("c_chain2")
        rstd2_done = sem("c_rstd2_done")
        h_done = sem("c_h_done")
        x_out = sem("c_x_out")
        h_out = [sem(f"c_h_out{n}") for n in range(2)]
        block = stack.enter_context(nc.Block())
        xv = residual.rearrange("(t p) d -> p t d", p=P)
        hv = hidden.rearrange("(t p) d -> p t d", p=P)
        HALF = HEADS // 2
        STEPS = 11
        M, U, REST = heads.M, heads.U, heads.STEPS - PAIRS

        def rest(make, eng):
            return lambda u, s: make(eng, u + PAIRS, s)

        @block.sync
        def _(sp):
            def store_x(t, s):
                wait_for(sp, x_done, t + 1)
                sp.dma_start(xv[:, bass.ds(t, 1), :], X[:, bass.ds(t, 1), :]).then_inc(x_out, 16)

            def store_h(t, s):
                wait_for(sp, h_done, t + 1)
                sp.dma_start(hv[:, bass.ds(t, 1), :], h[:, s:s + 1, :]).then_inc(h_out[s], 16)

            pipeline(sp, TILES, [(0, rest(heads.load_wq, sp), REST), (3, rest(heads.load_wo, sp), REST), (7, store_x),
                                 (8, store_h)])
            sp.wait_ge(x_out, TILES * 16)
            for n in range(2):
                sp.wait_ge(h_out[n], TILES // 2 * 16)

        @block.vector
        def _(dve):
            def stats(t, s):
                free_slot(dve, rstd_done, t, 2)
                dve.bn_stats(bn[:, s, 0, :], X[:, t, :]).then_inc(bn_done, 1)
                wait_for(dve, bn_done, t + 1)
                dve.bn_aggr(mv[:, s, 0, :], bn[:, s, 0, :]).then_inc(mv_done, 1)

            def residual(t, s):
                wait_for(dve, o_mm, t + 1)
                dve.tensor_tensor(X[:, t, :], psO[:, :], X[:, t, :], ALU.add).then_inc(x_done, 1)

            def stats_of_result(t, s):
                free_slot(dve, rstd2_done, t, 2)
                wait_for(dve, x_done, t + 1)
                dve.bn_stats(bn2[:, s, 0, :], X[:, t, :]).then_inc(bn2_done, 1)
                wait_for(dve, bn2_done, t + 1)
                dve.bn_aggr(mv2[:, s, 0, :], bn2[:, s, 0, :]).then_inc(mv2_done, 1)

            def eights(first, step):
                for n in range(2):
                    wait_for(dve, topk, first + 2 * step + n + 2)
                    for h in range(HEADS):
                        at = n + 8 * (step // 2)
                        eight = top[:, n, h, at:at + 8]
                        if step == 1:
                            last = dve.match_replace(W[:, n, h, :], eight, W[:, n, h, :], TAKEN)
                        else:
                            last = dve.max(eight, W[:, n, h, :])
                    last.then_inc(topk, 1)

            def pair(t, s):
                first = t * STEPS
                wait_for(dve, s_done, t + 1)
                free_slot(dve, e_done, t, 1)
                low, neg_high = S[:, s, :, 0:HK], SN[:, :, :]
                dve.scalar_tensor_tensor(W[:, 0, :, :], low, -1.0, neg_high, ALU.mult, ALU.min).then_inc(topk, 1)
                dve.scalar_tensor_tensor(W[:, 1, :, :], neg_high, -1.0, low, ALU.mult, ALU.min).then_inc(topk, 1)
                wait_for(dve, topk, first + 1)
                dve.tensor_reduce(nmax[:, :], W[:, 0, :, :], AX.X, ALU.min).then_inc(topk, 1)
                eights(first, 0)

            def select(t, s):
                first = t * STEPS
                eights(first, 1)
                eights(first, 2)
                wait_for(dve, topk, first + 9)
                dve.scalar_tensor_tensor(cut[:, :, :], top[:, 0, :, :], -1.0, top[:, 1, :, :], ALU.mult,
                                         ALU.min).then_inc(topk, 1)
                wait_for(dve, topk, first + 10)
                dve.tensor_reduce(least[:, :], cut[:, :, :], AX.X, ALU.max).then_inc(topk, 1)

            def mark(t, s):
                wait_for(dve, topk, (t + 1) * STEPS)
                wait_for(dve, e_done, t + 1)
                scores = S[:, s, :, :]
                dve.tensor_tensor(scores, scores, least[:, :].unsqueeze(2).to_broadcast([P, HEADS, KV]),
                                  ALU.is_ge).then_inc(marked, 1)

            def inverse(t, s):
                wait_for(dve, den_done, t + 1)
                free_slot(dve, a_done, t, 1)
                dve.reciprocal(rden[:, :], den[:, :]).then_inc(rden_done, 1)

            dve.memset(top[:, 0, :, HK // 2:], TAKEN).then_inc(pads_done, 1)
            dve.memset(top[:, 1, :, 0:1], -TAKEN).then_inc(pads_done, 1)
            dve.wait_ge(pads_done, 2)
            pipeline(dve, TILES, [(0, stats), (7, stats_of_result), (3, pair), (6, residual), (3, select), (4, inverse),
                                  (3, mark)])

        @block.gpsimd
        def _(pool):
            def rstds(t, s):
                wait_for(pool, mv_done, t + 1)
                free_slot(pool, y_done, t, 2)
                rstd_steps(pool, rstd[:, s, :], nmr[:, s, :], mv[:, s, :, :], mhalf[:, 0:1],
                           chain, t * 3, rstd_done)

            def denominator(t, s):
                wait_for(pool, kept_done, t + 1)
                free_slot(pool, rden_done, t, 1)
                pool.tensor_scalar(den[:, :], Z[:, s, :], NORM_EPS, None, ALU.mult).then_inc(den_chain, 1)
                wait_for(pool, den_chain, t + 1)
                pool.tensor_tensor(den[:, :], den[:, :], kept[:, :], ALU.add).then_inc(den_done, 1)

            def rstds_of_result(t, s):
                wait_for(pool, mv2_done, t + 1)
                free_slot(pool, h_done, t, 2)
                rstd_steps(pool, rstd2[:, s, :], nmr2[:, s, :], mv2[:, s, :, :], mhalf[:, 0:1],
                           chain2, t * 3, rstd2_done)

            def drop(t, s):
                wait_for(pool, marked, t + 1)
                e = E[:, s, :, :]
                pool.tensor_tensor(e, e, S[:, s, :, :], ALU.mult).then_inc(dropped, 1)

            def normalize(t, s):
                wait_for(pool, rden_done, t + 1)
                e = E[:, s, :, :]
                pool.tensor_tensor(e, e, rden[:, :].unsqueeze(2).to_broadcast([P, HEADS, KV]),
                                   ALU.mult).then_inc(a_done, 1)

            pipeline(pool, TILES, [(0, rstds), (7, rstds_of_result), (4, denominator), (4, normalize), (3, drop)])

        @block.scalar
        def _(act):
            def norm(t, s):
                wait_for(act, rstd_done, t + 1)
                free_slot(act, yT_mm, t, 1)
                act.activation(y[:, :], X[:, t, :], ACT.Identity, bias=nmr[:, s, :],
                               scale=rstd[:, s, :]).then_inc(y_done, 1)

            def norm_result(t, s):
                wait_for(act, rstd2_done, t + 1)
                if not isinstance(t, int) or t >= 2:
                    wait_for(act, h_out[s], (t // 2) * 16)
                act.activation(h[:, s, :], X[:, t, :], ACT.Identity, bias=nmr2[:, s, :],
                               scale=rstd2[:, s, :]).then_inc(h_done, 1)

            def copy_yT(t, s):
                wait_for(act, yT_mm, t + 1)
                free_slot(act, s_mm, t, 2)
                act.activation(yT[:, s, :, :], psY[:, :, :], ACT.Copy).then_inc(yT_done, 1)

            def exps(t, s):
                wait_for(act, topk, t * STEPS + 3)
                free_slot(act, den_done, t, 2)
                free_slot(act, aT_mm, t, 2)
                for h in range(HEADS):
                    last = act.activation(E[:, s, h, :], S[:, s, h, :], ACT.Exp, bias=nmax[:, h:h + 1],
                                          accum_out=Z[:, s, h:h + 1])
                last.then_inc(e_done, 1)

            def sums(t, s):
                wait_for(act, dropped, t + 1)
                free_slot(act, den_done, t, 1)
                for h in range(HEADS):
                    e = E[:, s, h, :]
                    last = act.activation(e, e, ACT.Copy, accum_out=kept[:, h:h + 1])
                last.then_inc(kept_done, 1)

            def copy_aT(t, s):
                wait_for(act, aT_mm, t + 1)
                free_slot(act, o_mm, t, 1)
                act.activation(aT[:, :, :], psA[:, :, :], ACT.Copy).then_inc(aT_done, 1)

            def copy_S(t, s):
                wait_for(act, s_mm, t + 1)
                free_slot(act, dropped, t, 2)
                if not isinstance(t, int) or t >= 1:
                    wait_for(act, topk, t * STEPS - 9)
                act.activation(SN[:, :, :], psS[:, :, HK:], ACT.Copy, scale=-1.0)
                act.activation(S[:, s, :, :], psS[:, :, :], ACT.Copy).then_inc(s_done, 1)

            pipeline(act, TILES, [(5, copy_aT), (0, rest(heads.spread_K, act), REST), (3, rest(heads.spread_V, act), REST),
                                  (1, norm), (4, sums), (3, exps), (8, norm_result), (2, copy_S), (1, copy_yT),
                                  (1, rest(heads.copy_M, act), REST), (4, rest(heads.copy_U, act), REST)])

        @block.tensor
        def _(pe):
            def scores(t, s):
                wait_for(pe, yT_done, t + 1)
                wait_for(pe, heads.m_done, (t // TPB) * PAIRS + PAIRS)
                free_slot(pe, s_done, t, 1)
                for n in range(2):
                    half = psS[:, n * HALF:(n + 1) * HALF, :]
                    pe.matmul(half, onesrow[:, :], maskrow[:, t // TPB, :, :], start=True, stop=False)
                    for k in range(DC):
                        mm = pe.matmul(half, yT[:, s, k, :], M[:, (t // TPB) % 2, k, n * 512:(n + 1) * 512],
                                       start=False, stop=(k == DC - 1))
                mm.then_inc(s_mm, 1)

            def transpose_y(t, s):
                wait_for(pe, y_done, t + 1)
                free_slot(pe, yT_done, t, 1)
                for k in range(DC):
                    mm = pe.transpose(psY[:, k, :], y[:, k * P:(k + 1) * P], ident[:, :])
                mm.then_inc(yT_mm, 1)

            def transpose_a(t, s):
                wait_for(pe, a_done, t + 1)
                free_slot(pe, aT_done, t, 1)
                a = E[:, s, :, :].rearrange("p h s -> p (h s)")
                for n in range(PAIRS):
                    mm = pe.transpose(psA[:, n, :], a[:, n * P:(n + 1) * P], ident[:, :])
                mm.then_inc(aT_mm, 1)

            def values(t, s):
                wait_for(pe, aT_done, t + 1)
                wait_for(pe, heads.u_done, (t // TPB) * PAIRS + PAIRS)
                free_slot(pe, x_done, t, 1)
                for n in range(PAIRS):
                    mm = pe.matmul(psO[:, :], aT[:, n, :], U[:, (t // TPB) % 2, n, :],
                                   start=(n == 0), stop=(n == PAIRS - 1))
                mm.then_inc(o_mm, 1)

            pipeline(pe, TILES, [(5, transpose_a), (2, scores), (5, values), (1, transpose_y),
                                 (1, rest(heads.make_M, pe), REST), (4, rest(heads.make_U, pe), REST)])


class Routing:

    def __init__(self, sb):
        self.tri = sb("r_tri", [P, P], bf16)
        self.ones = sb("r_ones", [P, P], bf16)
        self.eid = sb("r_eid", [P, EXPERTS])
        self.follows = sb("r_follows", [P, EXPERTS, TILES])
        self.token = sb("r_token", [P, TILES])
        self.lane = sb("r_lane", [P, P], fp16)
        self.first = sb("r_first", [P, SLOTS], fp16)
        self.pos = sb("r_pos", [P, TILES, CHOICES], u32)
        self.tokens = sb("r_tokens", [P, SLOTS], u32)
        self.expert_of = sb("r_expert_of", [1, SLOTS], i32)


def gather_rows(pool, done, R, t, s, idx, picked, rows, made, count):
    pool.tensor_copy(idx[:, s, :, :], R.pos[:, bass.ds(t * count, count), :]).then_inc(picked, 1)
    wait_for(pool, picked, t + 1)
    for g in range(count):
        for c in range(CHOICES):
            pool.indirect_dma_start(rows[:, s, g, c, :], None, made,
                                    bass.IndirectOffsetOnAxis(ap=idx[:, s, g, c:c + 1], axis=0)).then_inc(done[s], 16)


def route(nc, scope, R, layer, W_high, W_low, ident, rwT, rb, ewT, hidden, made):
    stack, sb, ps, sem = scope(recycle=True)
    with stack:
        L = f"r{layer}_"
        DEEP = 8
        PER_EXPERT = TILES // EXPERTS
        TWO = 2 * PER_EXPERT
        PICKS = TILES * CHOICES
        CHUNK = 8
        CHUNKS = PICKS // CHUNK
        raw = sb(L + "raw", [P, 2, DC * D])
        rw = sb(L + "rw", [P, DC, EXPERTS])
        rbc = sb(L + "rbc", [EXPERTS, 1])
        logT = sb(L + "logT", [EXPERTS, 2, P])
        rows = sb(L + "rows", [P, DEEP, 1, CHOICES, D])
        h = rows[:, :, 0, 0, :]
        hT = sb(L + "hT", [P, 2, DC, P])
        logits = sb(L + "logits", [P, TILES, EXPERTS])
        best = sb(L + "best", [P, TILES, 8])
        which = sb(L + "which", [P, TILES, 8], u32)
        whichf = sb(L + "whichf", [P, TILES, CHOICES])
        hot = sb(L + "hot", [P, TILES, CHOICES, EXPERTS])
        chosen = sb(L + "chosen", [P, TILES, EXPERTS], bf16)
        perm = sb(L + "perm", [P, EXPERTS, TILES])
        upto = sb(L + "upto", [P, EXPERTS, TILES])
        row = sb(L + "row", [P, TILES, EXPERTS])
        n_pad = sb(L + "n_pad", [P, EXPERTS], i32)
        n_cut = sb(L + "n_cut", [P, EXPERTS], i32)
        filled = sb(L + "filled", [P, EXPERTS])
        one = sb(L + "one", [P, EXPERTS])
        ends = sb(L + "ends", [P, EXPERTS])
        starts = sb(L + "starts", [P, EXPERTS])
        past = sb(L + "past", [1, SLOTS, EXPERTS])
        npast = sb(L + "npast", [1, SLOTS])
        rowf = sb(L + "rowf", [P, PICKS])
        lane_i = sb(L + "lane_i", [P, PICKS], u32)
        lane_f = sb(L + "lane_f", [P, PICKS])
        tile_f = sb(L + "tile_f", [P, PICKS])
        lane_hot = sb(L + "lane_hot", [P, 2, CHUNK, P], fp16)
        slot_hot = sb(L + "slot_hot", [P, 2, CHUNK, SLOTS], fp16)
        slot_tok = sb(L + "slot_tok", [P, 2, CHUNK, SLOTS], fp16)
        psT = ps(L + "psT", [P, 2, DC, P])
        psL = ps(L + "psL", [P, 512])
        psE = ps(L + "psE", [P, 512])
        psR = ps(L + "psR", [P, 2, TILES * EXPERTS])
        psI = ps(L + "psI", [P, 512])
        made_const = sem(L + "const")
        w_in = sem(L + "w_in")
        W_in = [sem(L + f"W_in{n}") for n in range(2)]
        high_done = sem(L + "high_done")
        low_done = [sem(L + f"low_done{n}") for n in range(2)]
        h_done = sem(L + "h_done")
        hT_mm = sem(L + "hT_mm")
        hT_done = sem(L + "hT_done")
        l_mm = sem(L + "l_mm")
        l_done = sem(L + "l_done")
        turned = sem(L + "turned")
        top = sem(L + "top")
        chosen_done = sem(L + "chosen_done")
        n_mm = sem(L + "n_mm")
        c = sem(L + "chain")
        slot_found = sem(L + "slot_found")
        lane_done = sem(L + "lane_done")
        slot_done = sem(L + "slot_done")
        i_mm = sem(L + "i_mm")
        LG = psL[:, 0:TILES * EXPERTS].rearrange("p (t e) -> p t e", t=TILES)
        LT = psE[0:EXPERTS, 0:P]
        RW = psR[:, 0, :].rearrange("p (t e) -> p t e", t=TILES)
        NT = psR[:, 1, :].rearrange("p (t e) -> p t e", t=TILES)
        rows_in = [sem(L + f"rows_in{n}") for n in range(DEEP)]
        if layer > 0:
            idx = sb(L + "idx", [P, DEEP, 1, CHOICES], u32)
            picked = sem(L + "picked")
            h_out = [sem(L + f"h_out{n}") for n in range(DEEP)]
        block = stack.enter_context(nc.Block())
        hv = hidden.rearrange("(t p) d -> p t d", p=P)

        @block.sync
        def _(sp):
            sp.dma_start(rw[:, :, :], rwT[layer].rearrange("(k p) e -> p k e", p=P)).then_inc(w_in, 16)
            sp.dma_start(rbc[:, :], rb[layer:layer + 1, :].rearrange("o e -> e o")).then_inc(w_in, 16)

            def load_h(i, place):
                s = place % DEEP
                free_slot(sp, hT_mm, i, DEEP)
                sp.dma_start(h[:, s, :], hv[:, bass.ds(i, 1), :].rearrange("p o d -> p (o d)")).then_inc(rows_in[s], 16)

            def store_h(i, place):
                s = place % DEEP
                wait_for(sp, h_done, i + 1)
                sp.dma_start(hv[:, bass.ds(i, 1), :].rearrange("p o d -> p (o d)"), h[:, s, :]).then_inc(h_out[s], 16)

            def load_W(i, place):
                if place % PER_EXPERT == 0:
                    e = i // PER_EXPERT
                    n = place // PER_EXPERT
                    if not isinstance(i, int) or i >= TWO:
                        wait_for(sp, low_done[n], i // TWO)
                    expert = ewT[layer][bass.ds(e, 1), :, :]
                    sp.dma_start(raw[:, n, :].rearrange("p (k n) -> p k n", k=DC),
                                 expert.rearrange("e (k p) n -> p (e k) n", p=P)).then_inc(W_in[n], 16)

            pipeline(sp, TILES, [(0, load_h), (DEEP - 1, load_W)] if layer == 0 else [(0, store_h), (0, load_W)], TWO)
            if layer > 0:
                for n in range(DEEP):
                    sp.wait_ge(h_out[n], TILES // DEEP * 16)

        @block.vector
        def _(dve):
            def add_outputs(i, place):
                s = place % DEEP
                wait_for(dve, rows_in[s], (i // DEEP + 1) * (CHOICES * 16))
                dve.tensor_tensor(h[:, s, :], h[:, s, :], rows[:, s, 0, 1, :], ALU.add).then_inc(h_done, 1)

            def split_low(i, place):
                if place % PER_EXPERT == PER_EXPERT - 1:
                    e, n = i // PER_EXPERT, place // PER_EXPERT
                    wait_for(dve, high_done, e + 1)
                    low, high = (W[:, bass.ds(e, 1), :, :].rearrange("p e k d -> p (e k d)") for W in (W_low, W_high))
                    dve.tensor_tensor(low, raw[:, n, :], high.bitcast(fp32), ALU.subtract).then_inc(low_done[n], 1)

            def spread(values, shape, axis):
                return values.unsqueeze(axis).to_broadcast(shape)

            dve.memset(one[:, :], 1.0).then_inc(c, 1)
            pipeline(dve, TILES, ([] if layer == 0 else [(0, add_outputs)]) + [(3, split_low)], TWO)

            dve.wait_ge(turned, TILES)
            dve.tensor_copy(logits[:, :, :], LG).then_inc(top, 1)
            dve.wait_ge(top, 1)
            for t in range(TILES):
                last = dve.max(best[:, t, :], logits[:, t, :])
            last.then_inc(top, 1)
            dve.wait_ge(top, 2)
            for t in range(TILES):
                last = dve.max_index(which[:, t, :], best[:, t, :], logits[:, t, :])
            last.then_inc(top, 1)
            dve.wait_ge(top, 3)
            dve.tensor_copy(whichf[:, :, :], which[:, :, 0:CHOICES]).then_inc(top, 1)
            dve.wait_ge(top, 4)
            shape = [P, PICKS, EXPERTS]
            dve.tensor_tensor(hot[:, :, :, :].rearrange("p t c e -> p (t c) e"), spread(R.eid[:, :], shape, 1),
                              spread(whichf[:, :, :].rearrange("p t c -> p (t c)"), shape, 2),
                              ALU.is_equal).then_inc(top, 1)
            dve.wait_ge(top, 5)
            dve.tensor_tensor(chosen[:, :, :], hot[:, :, 0, :], hot[:, :, 1, :], ALU.add).then_inc(chosen_done, 1)

            dve.wait_ge(n_mm, 1)
            dve.tensor_copy(perm[:, :, :], NT.rearrange("p t e -> p e t")).then_inc(c, 1)
            dve.wait_ge(c, 2)
            dve.tensor_tensor_scan(upto[:, :, :].rearrange("p e t -> p (e t)"),
                                   R.follows[:, :, :].rearrange("p e t -> p (e t)"),
                                   perm[:, :, :].rearrange("p e t -> p (e t)"), 0.0, ALU.mult, ALU.add).then_inc(c, 1)
            dve.wait_ge(c, 3)
            dve.tensor_scalar(n_pad[:, :], upto[:, :, TILES - 1], float(P - 1), None, ALU.add).then_inc(c, 1)
            dve.tensor_tensor(perm[:, :, :], upto[:, :, :], perm[:, :, :], ALU.subtract).then_inc(c, 1)
            dve.wait_ge(c, 4)
            dve.tensor_scalar(n_cut[:, :], n_pad[:, :], -P, None, ALU.bitwise_and).then_inc(c, 1)
            dve.wait_ge(c, 6)
            dve.tensor_copy(filled[:, :], n_cut[:, :]).then_inc(c, 1)
            dve.wait_ge(c, 7)
            dve.tensor_tensor_scan(ends[:, :], one[:, :], filled[:, :], 0.0, ALU.mult, ALU.add).then_inc(c, 1)
            dve.wait_ge(c, 8)
            dve.tensor_tensor(starts[:, :], ends[:, :], filled[:, :], ALU.subtract).then_inc(c, 1)
            shape = [1, SLOTS, EXPERTS]
            dve.tensor_tensor(past[:, :, :], spread(ends[0:1, :], shape, 1), spread(R.first[0:1, :], shape, 2),
                              ALU.is_le).then_inc(c, 1)
            dve.wait_ge(c, 9)
            dve.tensor_tensor(perm[:, :, :], perm[:, :, :], spread(starts[:, :], [P, EXPERTS, TILES], 2),
                              ALU.add).then_inc(c, 1)
            dve.wait_ge(c, 11)
            dve.tensor_tensor(row[:, :, :], RW, perm[:, :, :].rearrange("p e t -> p t e"), ALU.add).then_inc(c, 1)
            dve.wait_ge(c, 12)
            for n in range(CHOICES):
                dve.tensor_tensor(hot[:, :, n, :], hot[:, :, n, :], row[:, :, :], ALU.mult).then_inc(c, 1)
            dve.wait_ge(c, 12 + CHOICES)
            dve.tensor_reduce(rowf[:, :], hot[:, :, :, :].rearrange("p t c e -> p (t c) e"), AX.X, ALU.add).then_inc(c, 1)
            dve.wait_ge(c, 13 + CHOICES)
            dve.tensor_copy(R.pos[:, :, :].rearrange("p t c -> p (t c)"), rowf[:, :]).then_inc(c, 1)
            dve.wait_ge(c, 14 + CHOICES)
            dve.tensor_scalar(lane_i[:, :], R.pos[:, :, :].rearrange("p t c -> p (t c)"), P - 1, None,
                              ALU.bitwise_and).then_inc(c, 1)
            dve.wait_ge(c, 15 + CHOICES)
            dve.tensor_copy(lane_f[:, :], lane_i[:, :]).then_inc(c, 1)
            dve.wait_ge(c, 16 + CHOICES)
            dve.tensor_tensor(tile_f[:, :], rowf[:, :], lane_f[:, :], ALU.subtract).then_inc(c, 1)
            dve.wait_ge(c, 17 + CHOICES)
            for n in range(CHUNKS):
                free_slot(dve, i_mm, n, 2)
                part = slice(n * CHUNK, (n + 1) * CHUNK)
                shape = [P, CHUNK, SLOTS]
                dve.tensor_tensor(slot_hot[:, n % 2, :, :], spread(R.first[:, :], shape, 1),
                                  spread(tile_f[:, part], shape, 2), ALU.is_equal).then_inc(slot_found, 1)
                last = dve.tensor_tensor(lane_hot[:, n % 2, :, :], spread(R.lane[:, :], [P, CHUNK, P], 1),
                                  spread(lane_f[:, part], [P, CHUNK, P], 2), ALU.is_equal)
                last.then_inc(lane_done, 1)
            dve.tensor_reduce(npast[:, :], past[:, :, :], AX.X, ALU.add).then_inc(c, 1)
            dve.wait_ge(c, 18 + CHOICES)
            dve.tensor_scalar(R.expert_of[:, :], npast[:, :], float(EXPERTS - 1), None, ALU.min)
            dve.wait_ge(i_mm, CHUNKS)
            dve.tensor_scalar(R.tokens[:, :], psI[:, 0:SLOTS], float(TOKEN_ZERO), None, ALU.add)

        @block.gpsimd
        def _(pool):
            if layer == 0:
                pool.memset(R.ones[:, :], 1.0).then_inc(made_const, 1)
                pool.memset(R.follows[:, :, :], 1.0).then_inc(made_const, 1)
                for out, step, size, base, lane in ((R.eid, 1, EXPERTS, 0, 0), (R.token, P, TILES, -TOKEN_ZERO, 1),
                                                    (R.lane, 1, P, 0, 0), (R.first, P, SLOTS, 0, 0)):
                    pool.iota(out[:, :], [[step, size]], base=base, channel_multiplier=lane,
                              allow_small_or_imprecise_dtypes=True).then_inc(made_const, 1)
                pool.wait_ge(made_const, 6)
                pool.affine_select(out=R.tri[:, :], in_=R.ones[:, :], compare_op=ALU.is_gt, fill=0.0, base=0,
                                   pattern=[[1, P]], channel_multiplier=-1).then_inc(made_const, 1)
                pool.memset(R.follows[:, :, 0:1], 0.0).then_inc(made_const, 1)

            def fetch(i, s):
                free_slot(pool, hT_mm, i, DEEP)
                if not isinstance(i, int) or i >= DEEP:
                    wait_for(pool, h_out[s], (i // DEEP) * 16)
                gather_rows(pool, rows_in, R, i, s, idx, picked, rows, made, 1)

            if layer > 0:
                pipeline(pool, TILES, [(0, fetch)], DEEP)
            for n in range(CHUNKS):
                pool.wait_ge(slot_found, n + 1)
                free_slot(pool, i_mm, n, 2)
                each = [P, CHUNK // CHOICES, CHOICES, SLOTS]
                numbers = R.token[:, n * CHUNK // CHOICES:(n + 1) * CHUNK // CHOICES]
                pool.tensor_tensor(slot_tok[:, n % 2, :, :].rearrange("p (t c) s -> p t c s", c=CHOICES),
                                   slot_hot[:, n % 2, :, :].rearrange("p (t c) s -> p t c s", c=CHOICES),
                                   numbers.unsqueeze(2).unsqueeze(3).to_broadcast(each), ALU.mult).then_inc(slot_done, 1)

        @block.scalar
        def _(act):
            def copy_hT(i, s):
                wait_for(act, hT_mm, i + 1)
                free_slot(act, l_mm, i, 2)
                act.activation(hT[:, s % 2, :, :], psT[:, s % 2, :, :], ACT.Copy).then_inc(hT_done, 1)

            def copy_logits(i, s):
                wait_for(act, l_mm, i + 1)
                free_slot(act, turned, i, 2)
                act.activation(logT[:, s % 2, :], LT, ACT.Identity, bias=rbc[:, :]).then_inc(l_done, 1)

            def split_high(i, place):
                if place % PER_EXPERT == PER_EXPERT - 1:
                    e, n = i // PER_EXPERT, place // PER_EXPERT
                    wait_for(act, W_in[n], (i // TWO + 1) * 16)
                    act.activation(W_high[:, bass.ds(e, 1), :, :].rearrange("p e k d -> p (e k d)"),
                                   raw[:, n, :], ACT.Copy).then_inc(high_done, 1)

            act.wait_ge(w_in, 32)
            pipeline(act, TILES, [(0, copy_hT), (1, copy_logits), (2, split_high)], TWO)

        @block.tensor
        def _(pe):
            pe.wait_ge(w_in, 32)
            if layer == 0:
                pe.wait_ge(made_const, 8)

            def transpose_h(i, s):
                if layer == 0:
                    wait_for(pe, rows_in[s], (i // DEEP + 1) * 16)
                else:
                    wait_for(pe, h_done, i + 1)
                free_slot(pe, hT_done, i, 2)
                for k in range(DC):
                    mm = pe.transpose(psT[:, s % 2, k, :], h[:, s, k * P:(k + 1) * P], ident[:, :])
                mm.then_inc(hT_mm, 1)

            def logit(i, s):
                wait_for(pe, hT_done, i + 1)
                free_slot(pe, l_done, i, 1)
                for k in range(DC):
                    mm = pe.matmul(LT, rw[:, k, :], hT[:, s % 2, k, :], start=(k == 0), stop=(k == DC - 1))
                mm.then_inc(l_mm, 1)

            def turn(i, s):
                wait_for(pe, l_done, i + 1)
                pe.matmul(psL[:, bass.ds(i * EXPERTS, EXPERTS)], logT[:, s % 2, :], ident[0:EXPERTS, 0:EXPERTS],
                          start=True, stop=True).then_inc(turned, 1)

            pipeline(pe, TILES, [(0, transpose_h), (1, logit), (2, turn)], DEEP)
            pe.wait_ge(chosen_done, 1)
            marks = chosen[:, :, :].rearrange("p t e -> p (t e)")
            pe.matmul(psR[:, 0, :], R.tri[:, :], marks, start=True, stop=True)
            pe.matmul(psR[:, 1, :], R.ones[:, :], marks, start=True, stop=True).then_inc(n_mm, 1)
            for n in range(CHUNKS):
                pe.wait_ge(slot_done, n + 1)
                pe.wait_ge(lane_done, n + 1)
                for i in range(CHUNK):
                    mm = pe.matmul(psI[:, 0:SLOTS], lane_hot[:, n % 2, i, :], slot_tok[:, n % 2, i, :],
                                   start=(n == 0 and i == 0), stop=(n == CHUNKS - 1 and i == CHUNK - 1))
                mm.then_inc(i_mm, 1)


def experts(nc, scope, R, layer, W_high, W_low, ident, eb, hidden, made):
    stack, sb, ps, sem = scope(recycle=True)
    with stack:
        L = f"e{layer}_"
        DEEP = 6
        bias = sb(L + "bias", [P, EXPERTS, D])
        idx = sb(L + "idx", [P, DEEP], u32)
        rows = sb(L + "rows", [P, DEEP, D])
        rT_high = sb(L + "rT_high", [P, 2, DC, P], fp32r)
        rT_low = sb(L + "rT_low", [P, 2, DC, P], fp32r)
        y = sb(L + "y", [P, DEEP, D])
        psT = ps(L + "psT", [P, 2, DC, P])
        psO = ps(L + "psO", [P, 2, D])
        bias_in = sem(L + "bias_in")
        picked = sem(L + "picked")
        rows_in = [sem(L + f"rows_in{n}") for n in range(DEEP)]
        rT_mm = sem(L + "rT_mm")
        high_done = sem(L + "high_done")
        rT_done = sem(L + "rT_done")
        o_mm = sem(L + "o_mm")
        y_done = sem(L + "y_done")
        y_out = [sem(L + f"y_out{n}") for n in range(DEEP)]
        block = stack.enter_context(nc.Block())

        @block.sync
        def _(sp):
            sp.wait_ge(rows_in[1], 16)
            sp.dma_start(bias[:, :, :], eb[layer:layer + 1, :, :].to_broadcast([P, EXPERTS, D])).then_inc(bias_in, 16)
            slot = made.rearrange("(t p) d -> t p d", p=P)

            def store(t, s):
                wait_for(sp, y_done, t + 1)
                sp.dma_start(slot[bass.ds(t, 1), :, :].rearrange("o p d -> (o p) d"), y[:, s, :]).then_inc(y_out[s], 16)

            pipeline(sp, SLOTS, [(0, store)], DEEP)
            for n in range(DEEP):
                sp.wait_ge(y_out[n], (SLOTS - n + DEEP - 1) // DEEP * 16)

        @block.vector
        def _(dve):
            def add_bias(t, s):
                e = dve.value_load(R.expert_of[0:1, bass.ds(t, 1)], min_val=0, max_val=EXPERTS - 1)
                if isinstance(t, int) and t == 0:
                    dve.wait_ge(bias_in, 16)
                wait_for(dve, o_mm, t + 1)
                if not isinstance(t, int) or t >= DEEP:
                    wait_for(dve, y_out[s], (t // DEEP) * 16)
                dve.tensor_tensor(y[:, s, :], psO[:, s % 2, :], bias[:, bass.ds(e, 1), :].rearrange("p o d -> p (o d)"),
                                  ALU.add).then_inc(y_done, 1)

            def split_rT(t, s):
                wait_for(dve, high_done, t + 1)
                free_slot(dve, o_mm, t, 2)
                dve.tensor_tensor(rT_low[:, s % 2, :, :], psT[:, s % 2, :, :], rT_high[:, s % 2, :, :].bitcast(fp32),
                                  ALU.subtract).then_inc(rT_done, 1)

            pipeline(dve, SLOTS, [(2, add_bias), (0, split_rT)], DEEP)

        @block.gpsimd
        def _(pool):
            def fetch(t, s):
                free_slot(pool, rT_mm, t, DEEP)
                pool.tensor_copy(idx[:, s:s + 1], R.tokens[:, bass.ds(t, 1)]).then_inc(picked, 1)
                wait_for(pool, picked, t + 1)
                pool.indirect_dma_start(rows[:, s, :], None, hidden,
                                        bass.IndirectOffsetOnAxis(ap=idx[:, s:s + 1], axis=0)).then_inc(rows_in[s], 16)

            pipeline(pool, SLOTS, [(0, fetch)], DEEP)

        @block.scalar
        def _(act):
            def copy_rT(t, s):
                wait_for(act, rT_mm, t + 1)
                free_slot(act, o_mm, t, 2)
                act.activation(rT_high[:, s % 2, :, :], psT[:, s % 2, :, :], ACT.Copy).then_inc(high_done, 1)

            pipeline(act, SLOTS, [(0, copy_rT)], DEEP)

        @block.tensor
        def _(pe):
            def transpose_rows(t, s):
                wait_for(pe, rows_in[s], (t // DEEP + 1) * 16)
                free_slot(pe, rT_done, t, 2)
                for k in range(DC):
                    mm = pe.transpose(psT[:, s % 2, k, :], rows[:, s, k * P:(k + 1) * P], ident[:, :])
                mm.then_inc(rT_mm, 1)

            def product(t, s):
                e = pe.value_load(R.expert_of[0:1, bass.ds(t, 1)], min_val=0, max_val=EXPERTS - 1)
                wait_for(pe, rT_done, t + 1)
                free_slot(pe, y_done, t, 2)
                for k in range(DC):
                    high, low = rT_high[:, s % 2, k, :], rT_low[:, s % 2, k, :]
                    for n, (row_part, W_part) in enumerate(((high, W_high), (low, W_high), (high, W_low))):
                        mm = pe.matmul(psO[:, s % 2, :], row_part,
                                       W_part[:, bass.ds(e, 1), k, :].rearrange("p o d -> p (o d)"),
                                       start=(k == 0 and n == 0), stop=(k == DC - 1 and n == 2))
                mm.then_inc(o_mm, 1)

            pipeline(pe, SLOTS, [(0, transpose_rows), (1, product)], DEEP)


def combine(nc, scope, R, residual, made, out):
    stack, sb, ps, sem = scope()
    with stack:
        DEEP = 8
        idx = sb("o_idx", [P, DEEP, G, CHOICES], u32)
        rows = sb("o_rows", [P, DEEP, G, CHOICES, D])
        xt = sb("o_x", [P, DEEP, G, D])
        picked = sem("o_picked")
        rows_in = [sem(f"o_rows_in{n}") for n in range(DEEP)]
        x_in = [sem(f"o_x_in{n}") for n in range(DEEP)]
        sum_done = sem("o_sum_done")
        y_done = sem("o_y_done")
        y_out = [sem(f"o_y_out{n}") for n in range(DEEP)]
        block = stack.enter_context(nc.Block())
        ov = out.rearrange("(t p) d -> p t d", p=P)
        xv = residual.rearrange("(t p) d -> p t d", p=P)

        @block.gpsimd
        def _(pool):
            def fetch(i, s):
                if not isinstance(i, int) or i >= DEEP:
                    wait_for(pool, y_out[s], (i // DEEP) * 16)
                gather_rows(pool, rows_in, R, i, s, idx, picked, rows, made, G)

            pipeline(pool, GROUPS, [(0, fetch)], DEEP)

        @block.vector
        def _(dve):
            def add(i, s):
                wait_for(dve, rows_in[s], (i // DEEP + 1) * (G * CHOICES * 16))
                y = rows[:, s, :, 0, :]
                dve.tensor_tensor(y, y, rows[:, s, :, 1, :], ALU.add).then_inc(sum_done, 1)
                wait_for(dve, sum_done, i + 1)
                wait_for(dve, x_in[s], (i // DEEP + 1) * 16)
                dve.tensor_tensor(y, y, xt[:, s, :, :], ALU.add).then_inc(y_done, 1)

            pipeline(dve, GROUPS, [(0, add)], DEEP)

        @block.sync
        def _(sp):
            def store(i, s):
                wait_for(sp, y_done, i + 1)
                sp.dma_start(ov[:, bass.ds(i * G, G), :], rows[:, s, :, 0, :]).then_inc(y_out[s], 16)

            def load_x(i, s):
                free_slot(sp, y_done, i, DEEP)
                sp.dma_start(xt[:, s, :, :], xv[:, bass.ds(i * G, G), :]).then_inc(x_in[s], 16)

            pipeline(sp, GROUPS, [(0, load_x), (2, store)], DEEP)
            for n in range(DEEP):
                sp.wait_ge(y_out[n], GROUPS // DEEP * 16)


def kernel(x, ctx_1024, mask_BxS2_bf1, L0_ffn_rhs, L1_xattn_Wq, L1_xattn_Wk, L1_xattn_Wv, L1_xattn_Wo,
           L1_xattn_inv_temp, L1_ffn_router_w, L1_ffn_router_b, L1_ffn_expert_w, L1_ffn_expert_b):
    import numpy as np
    import concourse.bacc as bacc
    from concourse.bass_utils import run_bass_kernel_spmd

    ctx = np.asarray(ctx_1024).reshape(BATCH * KV, D)
    laid = {
        "x": np.asarray(x).reshape(TOKENS, D),
        "ctxT": ctx.T,
        "ctx": ctx,
        "mask": np.asarray(mask_BxS2_bf1).view(np.uint8),
        "rhs": np.asarray(L0_ffn_rhs),
        "WqT": np.asarray(L1_xattn_Wq).T,
        "Wk": np.asarray(L1_xattn_Wk),
        "Wv": np.asarray(L1_xattn_Wv),
        "Wo": np.asarray(L1_xattn_Wo),
        "inv_temp": np.repeat(np.asarray(L1_xattn_inv_temp), DH).reshape(PAIRS, P).T,
        "rwT": np.asarray(L1_ffn_router_w).transpose(0, 2, 1),
        "rb": np.asarray(L1_ffn_router_b),
        "ewT": np.asarray(L1_ffn_expert_w).transpose(0, 1, 3, 2),
        "eb": np.asarray(L1_ffn_expert_b),
    }
    nc = bacc.Bacc("TRN2", target_bir_lowering=False, num_devices=1)
    arrays, args = {}, []
    for name, a in laid.items():
        a = np.ascontiguousarray(a)
        arrays["in_" + name] = a
        args.append(nc.dram_tensor("in_" + name, a.shape, mybir.dt.from_np(a.dtype), kind="ExternalInput").ap())
    out = nc.dram_tensor("out_x", (TOKENS, D), fp32, kind="ExternalOutput").ap()
    build(nc, *args, out)
    r = run_bass_kernel_spmd(nc, [arrays], core_ids=[0])
    return r.results[0]["out_x"].reshape(BATCH, SEQ, D)
```
